# Optimizing a Trainium2 kernel written in Bass

```python
import numpy as np
import jax
import jax.numpy as jnp

def _softmax(x, axis=-1):
    return jax.nn.softmax(x, axis=axis)

def _gelu(x):
    return jax.nn.gelu(x, approximate=True)

def _silu(x):
    return jax.nn.silu(x)

def _sigmoid(x):
    return jax.nn.sigmoid(x)

def _layernorm(x, axis=-1, eps=1e-05):
    m = jnp.mean(x, axis=axis, keepdims=True)
    v = jnp.var(x, axis=axis, keepdims=True)
    return (x - m) / jnp.sqrt(v + eps)

def _scatter_add(tgt, idx, src, axis=0):
    return tgt.at[idx].add(src)

def _segment_sum(src, seg, n):
    return jax.ops.segment_sum(src, seg, n)
kernel_name = 'mk_recurrent_d2_jaxref_r4_321654'

def setup_inputs(seed: int=0):
    np.random.seed(seed)
    _w = jnp.asarray

    def _L0_attn_setup():
        import math
        import jax, jax.numpy as jnp
        import numpy as np
        HIDDEN = 256
        NUM_HEADS = 16
        NUM_QUERIES = 2
        NUM_Q_HEADS = NUM_HEADS * NUM_QUERIES
        HEAD_DIM = 64
        Q_DIM = NUM_Q_HEADS * HEAD_DIM
        KV_DIM = NUM_HEADS * HEAD_DIM
        BATCH, SEQ = (4, 256)

        def _alibi_slopes(num_heads: int) -> np.ndarray:
            closest_pow2 = 2 ** int(math.floor(math.log2(num_heads)))
            base = 2.0 ** (-2.0 ** (-(math.log2(closest_pow2) - 3)))
            powers = np.arange(1, closest_pow2 + 1, dtype=np.float32)
            slopes = base ** powers
            if closest_pow2 != num_heads:
                extra_base = 2.0 ** (-2.0 ** (-(math.log2(2 * closest_pow2) - 3)))
                extra_powers = np.arange(1, 2 * (num_heads - closest_pow2) + 1, 2, dtype=np.float32)
                slopes = np.concatenate([slopes, extra_base ** extra_powers])
            return slopes[:num_heads].astype(np.float32)
        ALIBI_SLOPES = jnp.asarray(_alibi_slopes(NUM_Q_HEADS))
        key = jax.random.key(seed)
        k1, k2, k3 = jax.random.split(key, 3)
        inputs = jax.random.normal(k1, (BATCH, SEQ, HIDDEN), dtype=jnp.float32)
        W_qkv = jax.random.normal(k2, (HIDDEN, Q_DIM + 2 * KV_DIM), dtype=jnp.float32) * (1.0 / math.sqrt(HIDDEN))
        W_out = jax.random.normal(k3, (Q_DIM, HIDDEN), dtype=jnp.float32) * (1.0 / math.sqrt(Q_DIM))
        return {'inputs': inputs, 'W_qkv': W_qkv, 'W_out': W_out}
    _L0_attn_in = _L0_attn_setup()

    def _L0_ffn_setup():
        import jax, jax.numpy as jnp
        import numpy as np
        from jax import lax
        B, N, D, H, E, K = (16, 256, 256, 1024, 8, 2)
        key = jax.random.key(seed)
        ks = jax.random.split(key, 12)
        s = 0.02
        return {'x': jax.random.normal(ks[0], (B, N, D), jnp.float32), 'alpha': jnp.asarray(0.9, jnp.float32), 'w_gate': jax.random.normal(ks[1], (D, E), jnp.float32) * s, 'b_gate': jnp.zeros((E,), jnp.float32), 'W1m': jax.random.normal(ks[2], (D, H), jnp.float32) * s, 'b1m': jnp.zeros((H,), jnp.float32), 'W2m': jax.random.normal(ks[3], (H, D), jnp.float32) * s, 'b2m': jnp.zeros((D,), jnp.float32), 'W1e': jax.random.normal(ks[4], (E, D, H), jnp.float32) * s, 'b1e': jnp.zeros((E, H), jnp.float32), 'W2e': jax.random.normal(ks[5], (E, H, D), jnp.float32) * s, 'b2e': jnp.zeros((E, D), jnp.float32)}
    _L0_ffn_in = _L0_ffn_setup()

    def _L1_attn_setup():
        import jax, jax.numpy as jnp
        import numpy as np
        B, T, D = (4, 1024, 256)
        HD = 64
        H = D // HD
        C = 64
        key = jax.random.key(seed)
        k1, k2, k3 = jax.random.split(key, 3)
        out = jax.random.normal(k1, (B, T, D), jnp.float32)
        W_write = jax.random.normal(k2, (D, D), jnp.float32) * 0.03
        W_read = jax.random.normal(k3, (D, D), jnp.float32) * 0.03
        decay = jnp.full((H,), 4.6, jnp.float32)
        log_alpha = jnp.log(jnp.full((H,), 0.03, jnp.float32))
        return {'out': out, 'W_write': W_write, 'W_read': W_read, 'decay': decay, 'log_alpha': log_alpha}
    _L1_attn_in = _L1_attn_setup()

    def _L1_ffn_setup():
        import jax, jax.numpy as jnp
        import numpy as np
        DIM = 256
        N_HEADS = 16
        N_KV_HEADS = 4
        HEAD_DIM = DIM // N_HEADS
        N_REP = N_HEADS // N_KV_HEADS
        N_EXPERTS = 4
        TOP_K = 2
        HIDDEN = 3 * DIM
        EPS = 1.1920928955078125e-07

        def _rmsnorm(x, g):
            var = jnp.mean(jnp.square(x), axis=-1, keepdims=True)
            return x * jax.lax.rsqrt(var + EPS) * g

        def _rotate_half(x):
            x1, x2 = jnp.split(x, 2, axis=-1)
            return jnp.concatenate([-x2, x1], axis=-1)

        def _rope_tables(S):
            inv_freq = 1.0 / 10000.0 ** (jnp.arange(0, HEAD_DIM, 2, dtype=jnp.float32) / HEAD_DIM)
            freqs = jnp.arange(S, dtype=jnp.float32)[:, None] * inv_freq[None, :]
            emb = jnp.concatenate([freqs, freqs], axis=-1)
            return (jnp.cos(emb), jnp.sin(emb))

        def _attention(x, wq, wk, wv, wo):
            B, S, D = x.shape
            q = (x @ wq).reshape(B, S, N_HEADS, HEAD_DIM).transpose(0, 2, 1, 3)
            k = (x @ wk).reshape(B, S, N_KV_HEADS, HEAD_DIM).transpose(0, 2, 1, 3)
            v = (x @ wv).reshape(B, S, N_KV_HEADS, HEAD_DIM).transpose(0, 2, 1, 3)
            cos, sin = _rope_tables(S)
            q = q * cos + _rotate_half(q) * sin
            k = k * cos + _rotate_half(k) * sin
            k = jnp.repeat(k, N_REP, axis=1)
            v = jnp.repeat(v, N_REP, axis=1)
            scores = jnp.einsum('bhqd,bhkd->bhqk', q, k) / jnp.sqrt(jnp.float32(HEAD_DIM))
            causal = jnp.tril(jnp.ones((S, S), dtype=bool))
            scores = jnp.where(causal, scores, -jnp.inf)
            attn = jax.nn.softmax(scores, axis=-1)
            out = jnp.einsum('bhqk,bhkd->bhqd', attn, v)
            return out.transpose(0, 2, 1, 3).reshape(B, S, D) @ wo

        def _moe(x, gate, w1, w2, w3):
            B, S, D = x.shape
            xf = x.reshape(-1, D)
            probs = jax.nn.softmax(xf @ gate, axis=-1)
            w, idx = jax.lax.top_k(probs, TOP_K)
            w = w / jnp.sum(w, axis=-1, keepdims=True)
            oh = jax.nn.one_hot(idx, N_EXPERTS, dtype=xf.dtype)
            comb = jnp.einsum('nk,nke->ne', w, oh)
            out = jnp.zeros_like(xf)
            for e in range(N_EXPERTS):
                h = jax.nn.silu(xf @ w1[e]) * (xf @ w3[e])
                out = out + comb[:, e:e + 1] * (h @ w2[e])
            return out.reshape(B, S, D)
        key = jax.random.key(seed)
        ks = jax.random.split(key, 12)
        s = 0.02
        B, S = (2, 512)
        return {'x': jax.random.normal(ks[0], (B, S, DIM), jnp.float32), 'g1': jnp.ones((DIM,), jnp.float32), 'g2': jnp.ones((DIM,), jnp.float32), 'wq': jax.random.normal(ks[1], (DIM, N_HEADS * HEAD_DIM), jnp.float32) * s, 'wk': jax.random.normal(ks[2], (DIM, N_KV_HEADS * HEAD_DIM), jnp.float32) * s, 'wv': jax.random.normal(ks[3], (DIM, N_KV_HEADS * HEAD_DIM), jnp.float32) * s, 'wo': jax.random.normal(ks[4], (N_HEADS * HEAD_DIM, DIM), jnp.float32) * s, 'gate': jax.random.normal(ks[5], (DIM, N_EXPERTS), jnp.float32) * s, 'w1': jax.random.normal(ks[6], (N_EXPERTS, DIM, HIDDEN), jnp.float32) * s, 'w2': jax.random.normal(ks[7], (N_EXPERTS, HIDDEN, DIM), jnp.float32) * s, 'w3': jax.random.normal(ks[8], (N_EXPERTS, DIM, HIDDEN), jnp.float32) * s}
    _L1_ffn_in = _L1_ffn_setup()
    _d = {'L0_attn_inputs': _L0_attn_in['inputs'], 'L0_attn_W_qkv': _L0_attn_in['W_qkv'], 'L0_attn_W_out': _L0_attn_in['W_out'], 'L0_ffn_alpha': _L0_ffn_in['alpha'], 'L0_ffn_w_gate': _L0_ffn_in['w_gate'], 'L0_ffn_b_gate': _L0_ffn_in['b_gate'], 'L0_ffn_W1m': _L0_ffn_in['W1m'], 'L0_ffn_b1m': _L0_ffn_in['b1m'], 'L0_ffn_W2m': _L0_ffn_in['W2m'], 'L0_ffn_b2m': _L0_ffn_in['b2m'], 'L0_ffn_W1e': _L0_ffn_in['W1e'], 'L0_ffn_b1e': _L0_ffn_in['b1e'], 'L0_ffn_W2e': _L0_ffn_in['W2e'], 'L0_ffn_b2e': _L0_ffn_in['b2e'], 'L1_attn_W_write': _L1_attn_in['W_write'], 'L1_attn_W_read': _L1_attn_in['W_read'], 'L1_attn_decay': _L1_attn_in['decay'], 'L1_attn_log_alpha': _L1_attn_in['log_alpha'], 'L1_ffn_g1': _L1_ffn_in['g1'], 'L1_ffn_g2': _L1_ffn_in['g2'], 'L1_ffn_wq': _L1_ffn_in['wq'], 'L1_ffn_wk': _L1_ffn_in['wk'], 'L1_ffn_wv': _L1_ffn_in['wv'], 'L1_ffn_wo': _L1_ffn_in['wo'], 'L1_ffn_gate': _L1_ffn_in['gate'], 'L1_ffn_w1': _L1_ffn_in['w1'], 'L1_ffn_w2': _L1_ffn_in['w2'], 'L1_ffn_w3': _L1_ffn_in['w3']}
    _x0 = _d['L0_attn_inputs']
    _d['L0_attn_inputs'] = jax.random.normal(jax.random.fold_in(jax.random.key(seed), 1), (8, 512, 256), dtype=_x0.dtype)
    del _x0
    return _d

def reference(L0_attn_inputs, L0_attn_W_qkv, L0_attn_W_out, L0_ffn_alpha, L0_ffn_w_gate, L0_ffn_b_gate, L0_ffn_W1m, L0_ffn_b1m, L0_ffn_W2m, L0_ffn_b2m, L0_ffn_W1e, L0_ffn_b1e, L0_ffn_W2e, L0_ffn_b2e, L1_attn_W_write, L1_attn_W_read, L1_attn_decay, L1_attn_log_alpha, L1_ffn_g1, L1_ffn_g2, L1_ffn_wq, L1_ffn_wk, L1_ffn_wv, L1_ffn_wo, L1_ffn_gate, L1_ffn_w1, L1_ffn_w2, L1_ffn_w3):

    def _L0_attn_ref(inputs, W_qkv, W_out):
        import math
        import jax, jax.numpy as jnp
        import numpy as np
        HIDDEN = 256
        NUM_HEADS = 16
        NUM_QUERIES = 2
        NUM_Q_HEADS = NUM_HEADS * NUM_QUERIES
        HEAD_DIM = 64
        Q_DIM = NUM_Q_HEADS * HEAD_DIM
        KV_DIM = NUM_HEADS * HEAD_DIM
        BATCH, SEQ = (4, 256)

        def _alibi_slopes(num_heads: int) -> np.ndarray:
            closest_pow2 = 2 ** int(math.floor(math.log2(num_heads)))
            base = 2.0 ** (-2.0 ** (-(math.log2(closest_pow2) - 3)))
            powers = np.arange(1, closest_pow2 + 1, dtype=np.float32)
            slopes = base ** powers
            if closest_pow2 != num_heads:
                extra_base = 2.0 ** (-2.0 ** (-(math.log2(2 * closest_pow2) - 3)))
                extra_powers = np.arange(1, 2 * (num_heads - closest_pow2) + 1, 2, dtype=np.float32)
                slopes = np.concatenate([slopes, extra_base ** extra_powers])
            return slopes[:num_heads].astype(np.float32)
        ALIBI_SLOPES = jnp.asarray(_alibi_slopes(NUM_Q_HEADS))
        B, S, _ = inputs.shape
        qkv = inputs @ W_qkv
        q = qkv[..., :Q_DIM].reshape(B, S, NUM_Q_HEADS, HEAD_DIM).transpose(0, 2, 1, 3)
        k = qkv[..., Q_DIM:Q_DIM + KV_DIM].reshape(B, S, NUM_HEADS, HEAD_DIM).transpose(0, 2, 1, 3)
        v = qkv[..., Q_DIM + KV_DIM:].reshape(B, S, NUM_HEADS, HEAD_DIM).transpose(0, 2, 1, 3)
        k = jnp.repeat(k, NUM_QUERIES, axis=1)
        v = jnp.repeat(v, NUM_QUERIES, axis=1)
        pos = jnp.arange(S)
        rel = (pos[None, :] - pos[:, None]).astype(jnp.float32)
        bias = ALIBI_SLOPES[:, None, None] * rel[None, :, :]
        scores = jnp.einsum('bhqd,bhkd->bhqk', q, k) / math.sqrt(HEAD_DIM)
        scores = scores + bias[None]
        causal = pos[:, None] >= pos[None, :]
        scores = jnp.where(causal[None, None], scores, -jnp.inf)
        attn = jax.nn.softmax(scores, axis=-1)
        out = jnp.einsum('bhqk,bhkd->bhqd', attn, v)
        out = out.transpose(0, 2, 1, 3).reshape(B, S, Q_DIM)
        return out @ W_out

    def _L0_ffn_ref(x, alpha, w_gate, b_gate, W1m, b1m, W2m, b2m, W1e, b1e, W2e, b2e):
        import jax, jax.numpy as jnp
        import numpy as np
        from jax import lax
        B, N, D, H, E, K = (16, 256, 256, 1024, 8, 2)
        main = jax.nn.gelu(x @ W1m + b1m) @ W2m + b2m
        logits = jnp.mean(x, axis=1) @ w_gate + b_gate
        probs = jax.nn.softmax(logits, axis=-1)
        top_vals, top_idx = lax.top_k(probs, K)
        gate_w = top_vals / jnp.sum(top_vals, axis=-1, keepdims=True)
        W1g = W1e[top_idx]
        b1g = b1e[top_idx]
        W2g = W2e[top_idx]
        b2g = b2e[top_idx]
        h = jax.nn.gelu(jnp.einsum('bnd,bkdh->bknh', x, W1g) + b1g[:, :, None, :])
        eo = jnp.einsum('bknh,bkhd->bknd', h, W2g) + b2g[:, :, None, :]
        expert_out = jnp.einsum('bk,bknd->bnd', gate_w, eo)
        a = jnp.clip(alpha, 0.1, 1.0)
        return a * main + (1.0 - a) * expert_out

    def _L1_attn_ref(out, W_write, W_read, decay, log_alpha):
        import jax, jax.numpy as jnp
        import numpy as np
        B, T, D = (4, 1024, 256)
        HD = 64
        H = D // HD
        C = 64
        Bb, Tt, Dd = out.shape
        d, Hh, Cc = (HD, D // HD, C)
        out32 = out.astype(jnp.float32)
        gamma = jax.nn.sigmoid(decay)
        log_gamma = jnp.log(gamma)
        v = (out32 @ W_write.T).reshape(Bb, Tt, Hh, d).transpose(0, 2, 1, 3)
        rk = out32.reshape(Bb, Tt, Hh, d).transpose(0, 2, 1, 3)
        wk = jnp.pad(rk[:, :, :-1], ((0, 0), (0, 0), (1, 0), (0, 0)))
        BH = Bb * Hh
        gamma_bh = jnp.tile(gamma, Bb)
        log_gamma_bh = jnp.tile(log_gamma, Bb)
        nC = Tt // Cc
        v_ch = v.reshape(BH, nC, Cc, d).transpose(1, 0, 2, 3)
        rk_ch = rk.reshape(BH, nC, Cc, d).transpose(1, 0, 2, 3)
        wk_ch = wk.reshape(BH, nC, Cc, d).transpose(1, 0, 2, 3)
        p = jnp.arange(Cc)
        diffs = jnp.clip(p[:, None] - 1 - p[None, :], 0)
        causal = p[:, None] > p[None, :]
        M = jnp.exp(diffs[None].astype(jnp.float32) * log_gamma_bh[:, None, None]) * causal[None]
        g_p = gamma_bh[:, None] ** p[None, :].astype(jnp.float32)
        g_w = gamma_bh[:, None] ** (Cc - 1 - p)[None, :].astype(jnp.float32)
        g_C = gamma_bh ** Cc

        def scan_fn(W, chunk):
            rk_c, wk_c, v_c = chunk
            inter = jnp.einsum('bij,bcj->bci', W, rk_c) * g_p[:, :, None]
            S = jnp.einsum('bcd,bkd->bck', rk_c, wk_c)
            intra = jnp.einsum('bck,bkd->bcd', S * M, v_c)
            W_new = g_C[:, None, None] * W + jnp.einsum('bci,bcj->bij', v_c * g_w[:, :, None], wk_c)
            return (W_new, inter + intra)
        W0 = jnp.zeros((BH, d, d), jnp.float32)
        _, reads = jax.lax.scan(scan_fn, W0, (rk_ch, wk_ch, v_ch))
        reads = reads.transpose(1, 0, 2, 3).reshape(Bb, Hh, Tt, d)
        alpha = jnp.exp(log_alpha)[None, :, None, None]
        reads = (alpha * reads).transpose(0, 2, 1, 3).reshape(Bb, Tt, Dd)
        return out + (reads @ W_read.T).astype(out.dtype)

    def _L1_ffn_ref(x, g1, g2, wq, wk, wv, wo, gate, w1, w2, w3):
        import jax, jax.numpy as jnp
        import numpy as np
        DIM = 256
        N_HEADS = 16
        N_KV_HEADS = 4
        HEAD_DIM = DIM // N_HEADS
        N_REP = N_HEADS // N_KV_HEADS
        N_EXPERTS = 4
        TOP_K = 2
        HIDDEN = 3 * DIM
        EPS = 1.1920928955078125e-07

        def _rmsnorm(x, g):
            var = jnp.mean(jnp.square(x), axis=-1, keepdims=True)
            return x * jax.lax.rsqrt(var + EPS) * g

        def _rotate_half(x):
            x1, x2 = jnp.split(x, 2, axis=-1)
            return jnp.concatenate([-x2, x1], axis=-1)

        def _rope_tables(S):
            inv_freq = 1.0 / 10000.0 ** (jnp.arange(0, HEAD_DIM, 2, dtype=jnp.float32) / HEAD_DIM)
            freqs = jnp.arange(S, dtype=jnp.float32)[:, None] * inv_freq[None, :]
            emb = jnp.concatenate([freqs, freqs], axis=-1)
            return (jnp.cos(emb), jnp.sin(emb))

        def _attention(x, wq, wk, wv, wo):
            B, S, D = x.shape
            q = (x @ wq).reshape(B, S, N_HEADS, HEAD_DIM).transpose(0, 2, 1, 3)
            k = (x @ wk).reshape(B, S, N_KV_HEADS, HEAD_DIM).transpose(0, 2, 1, 3)
            v = (x @ wv).reshape(B, S, N_KV_HEADS, HEAD_DIM).transpose(0, 2, 1, 3)
            cos, sin = _rope_tables(S)
            q = q * cos + _rotate_half(q) * sin
            k = k * cos + _rotate_half(k) * sin
            k = jnp.repeat(k, N_REP, axis=1)
            v = jnp.repeat(v, N_REP, axis=1)
            scores = jnp.einsum('bhqd,bhkd->bhqk', q, k) / jnp.sqrt(jnp.float32(HEAD_DIM))
            causal = jnp.tril(jnp.ones((S, S), dtype=bool))
            scores = jnp.where(causal, scores, -jnp.inf)
            attn = jax.nn.softmax(scores, axis=-1)
            out = jnp.einsum('bhqk,bhkd->bhqd', attn, v)
            return out.transpose(0, 2, 1, 3).reshape(B, S, D) @ wo

        def _moe(x, gate, w1, w2, w3):
            B, S, D = x.shape
            xf = x.reshape(-1, D)
            probs = jax.nn.softmax(xf @ gate, axis=-1)
            w, idx = jax.lax.top_k(probs, TOP_K)
            w = w / jnp.sum(w, axis=-1, keepdims=True)
            oh = jax.nn.one_hot(idx, N_EXPERTS, dtype=xf.dtype)
            comb = jnp.einsum('nk,nke->ne', w, oh)
            out = jnp.zeros_like(xf)
            for e in range(N_EXPERTS):
                h = jax.nn.silu(xf @ w1[e]) * (xf @ w3[e])
                out = out + comb[:, e:e + 1] * (h @ w2[e])
            return out.reshape(B, S, D)
        x = x + _attention(_rmsnorm(x, g1), wq, wk, wv, wo)
        x = x + _moe(_rmsnorm(x, g2), gate, w1, w2, w3)
        return x
    x = L0_attn_inputs
    xn = _layernorm(x, axis=-1)
    s = _L0_attn_ref(xn, L0_attn_W_qkv, L0_attn_W_out)
    g = _silu(_L0_ffn_ref(xn, L0_ffn_alpha, L0_ffn_w_gate, L0_ffn_b_gate, L0_ffn_W1m, L0_ffn_b1m, L0_ffn_W2m, L0_ffn_b2m, L0_ffn_W1e, L0_ffn_b1e, L0_ffn_W2e, L0_ffn_b2e))
    x = x + s * g
    xn = _layernorm(x, axis=-1)
    s = _L1_attn_ref(xn, L1_attn_W_write, L1_attn_W_read, L1_attn_decay, L1_attn_log_alpha)
    g = _silu(_L1_ffn_ref(xn, L1_ffn_g1, L1_ffn_g2, L1_ffn_wq, L1_ffn_wk, L1_ffn_wv, L1_ffn_wo, L1_ffn_gate, L1_ffn_w1, L1_ffn_w2, L1_ffn_w3))
    x = x + s * g
    return x

_drawn_inputs = setup_inputs


def setup_inputs(seed=0):
    import zlib

    import numpy as np

    out = dict(_drawn_inputs(seed))
    spreads = {'L0_ffn_b_gate': (0.0, 0.8),
     'L0_ffn_b1m': (0.0, 0.8),
     'L0_ffn_b2m': (0.0, 0.423),
     'L0_ffn_b1e': (0.0, 0.8),
     'L0_ffn_b2e': (0.0, 0.8),
     'L1_attn_decay': (4.599999904632568, 0.2),
     'L1_attn_log_alpha': (-3.5065579414367676, 0.2),
     'L1_ffn_g1': (1.0, 0.6),
     'L1_ffn_g2': (1.0, 0.6)}
    factors = {'L0_ffn_w_gate': 8.0,
     'L0_ffn_W1m': 2.84,
     'L0_ffn_W1e': 8.0,
     'L0_ffn_W2e': 8.0,
     'L1_ffn_wq': 8.0,
     'L1_ffn_wk': 8.0,
     'L1_ffn_wv': 8.0,
     'L1_ffn_wo': 8.0,
     'L1_ffn_gate': 8.0,
     'L1_ffn_w1': 5.884,
     'L1_ffn_w2': 5.818,
     'L1_ffn_w3': 5.795}
    for name, (base, spread) in spreads.items():
        noise = np.random.default_rng([zlib.crc32(name.encode()), seed]).standard_normal(out[name].shape)
        drawn = base * np.exp(spread * noise) if base else spread * noise
        out[name] = jnp.asarray(drawn.astype(out[name].dtype))
    for name, factor in factors.items():
        out[name] = (out[name] * factor).astype(out[name].dtype)
    return out
```

```python
from contextlib import ExitStack

import concourse.bass as bass
import numpy as np
from concourse import mybir

F32 = mybir.dt.float32
F32R = mybir.dt.float32r
U32 = mybir.dt.uint32
ALU = mybir.AluOpType
ACT = mybir.ActivationFunctionType
AX = mybir.AxisListType
ds = bass.ds

P = 128
B, S, D = 8, 512, 256
KT = D // P
TT = S // P
T = B * S
EPS_LN = 1e-5
BIG = 1e30

KVH = 16
HD = 64


def hold(ctx, nc):
    def sb(name, shape, dt=F32):
        return ctx.enter_context(nc.sbuf_tensor(name, shape, dt))

    def ps(name, shape=(P, 512)):
        return ctx.enter_context(nc.psum_tensor(name, list(shape), F32))

    def sem(name):
        return ctx.enter_context(nc.semaphore(name))

    return sb, ps, sem


def wait_alone(engine, semaphore, value, ticks):
    engine.wait_ge(semaphore, value)
    engine.sem_inc(ticks, 1)


def layernorm_phase(nc, x_dram, ident, xh, xl, xsum, xh_dram, xl_dram):
    with ExitStack() as ctx:
        sb, ps, sem = hold(ctx, nc)
        x_in = [sb(f"ln_x{i}", [P, TT, D]) for i in range(2)]
        stats = sb("ln_stats", [P, TT, 6])
        mv = sb("ln_mv", [P, TT, 2])
        std = sb("ln_std", [P, TT])
        rstd = sb("ln_rstd", [P, TT])
        eps = sb("ln_eps", [P, 1])
        carry = sb("ln_carry", [P, 1])
        xT_ps = [[ps(f"ln_ps{i}{k}") for k in range(KT)] for i in range(2)]
        x_loaded = [sem("ln_x_loaded0"), sem("ln_x_loaded1")]
        id_done = sem("ln_id_done")
        eps_done = sem("ln_eps_done")
        stats_done = sem("ln_stats_done")
        var_done = sem("ln_var_done")
        std_done = sem("ln_std_done")
        rstd_done = sem("ln_rstd_done")
        normed = sem("ln_normed")
        turned = sem("ln_turned")
        high = sem("ln_high")
        low = sem("ln_low")
        spilled = sem("ln_spilled")
        x_view = x_dram.rearrange("b (i p) d -> b p i d", p=P)
        block = ctx.enter_context(nc.Block())

        @block.sync
        def _(sp):
            for par in range(2):
                sp.dma_start(x_in[par][:], x_view[par]).then_inc(x_loaded[par], 16)
            with sp.Fori(0, B // 2) as pair:
                for par in range(2):
                    sp.wait_ge(low, (pair * 2 + par) + 1)
                    sp.wait_ge(high, (pair * 2 + par) * KT + KT)
                    at = (pair * 2 + par) * S
                    sp.dma_start(xh_dram[:, :, ds(at, S)], xh[:, :, ds(at, S)].bitcast(F32)).then_inc(spilled, 16)
                    sp.dma_start(xl_dram[:, :, ds(at, S)], xl[:, :, ds(at, S)].bitcast(F32)).then_inc(spilled, 16)
                    sp.wait_ge(turned, (pair * 2 + par) + 1)
                    sp.dma_start(x_in[par][:], x_view[ds((pair * 2 + (par + 2)) % B, 1)]
                                 .rearrange("b p i d -> p (b i) d")).then_inc(x_loaded[par], 16)
            for par in range(2):
                sp.wait_ge(x_loaded[par], 16 * (B // 2 + 1))
            sp.wait_ge(spilled, 32 * B)

        @block.gpsimd
        def _(pool):
            pool.memset(ident[:], 0.0).then_inc(id_done, 1)
            pool.wait_ge(id_done, 1)
            pool.affine_select(out=ident[:], in_=ident[:], compare_op=ALU.not_equal, fill=1.0, base=0,
                               pattern=[[-1, P]], channel_multiplier=1).then_inc(id_done, 1)

        @block.vector
        def _(dve):
            dve.memset(eps[:], EPS_LN).then_inc(eps_done, 1)
            with dve.Fori(0, B // 2) as pair:
                for par in range(2):
                    n = pair * 2 + par
                    dve.wait_ge(x_loaded[par], pair * 16 + 16)
                    for i in range(TT):
                        dve.bn_stats(stats[:, i, :], x_in[par][:, i, :]).then_inc(stats_done, 1)
                    dve.wait_ge(stats_done, n * TT + TT)
                    dve.memset(carry[:], 0.0)
                    for i in range(TT):
                        dve.bn_aggr(mv[:, i, :], stats[:, i, :]).then_inc(var_done, 1)
                    dve.wait_ge(std_done, n + 1)
                    dve.reciprocal(rstd[:], std[:]).then_inc(rstd_done, 1)
                    dve.wait_ge(rstd_done, n + 1)
                    for i in range(TT):
                        dve.tensor_scalar(x_in[par][:, i, :], x_in[par][:, i, :], mv[:, i, 0:1], rstd[:, i:i + 1],
                                          ALU.subtract, ALU.mult).then_inc(normed, 1)
                    dve.wait_ge(high, n * KT + KT)
                    at = n * S
                    for k in range(KT):
                        ins = dve.tensor_tensor(xl[:, k, ds(at, S)], xT_ps[par][k][:], xh[:, k, ds(at, S)].bitcast(F32),
                                                ALU.subtract)
                    ins.then_inc(low, 1)

        @block.scalar
        def _(act):
            act.wait_ge(eps_done, 1)
            with act.Fori(0, B // 2) as pair:
                for par in range(2):
                    n = pair * 2 + par
                    act.wait_ge(var_done, n * TT + TT)
                    act.activation(std[:], mv[:, :, 1], ACT.Sqrt, bias=eps[:, 0:1]).then_inc(std_done, 1)
                    act.wait_ge(turned, n + 1)
                    for k in range(KT):
                        act.activation(xh[:, k, ds(n * S, S)], xT_ps[par][k][:], ACT.Copy,
                                       accum_out=xsum[:, k, ds(n, 1)]).then_inc(high, 1)

        @block.tensor
        def _(pe):
            pe.wait_ge(id_done, 2)
            with pe.Fori(0, B // 2) as pair:
                for par in range(2):
                    n = pair * 2 + par
                    pe.wait_ge(normed, n * TT + TT)
                    for k in range(KT):
                        for i in range(TT):
                            ins = pe.transpose(xT_ps[par][k][:, P * i:P * i + P], x_in[par][:, i, P * k:P * k + P], ident[:])
                    ins.then_inc(turned, 1)


E0 = 8
TOP = 2
HID = 1024
MT = HID // P
SLOTS = 3
NF = 1 + TOP


def gate_phase(nc, xsum, w_gate, b_gate, alpha, rows_dram, coef_dram, rows, coef):
    with ExitStack() as ctx:
        sb, ps, sem = hold(ctx, nc)
        wg = sb("gt_wg", [P, KT, E0])
        bg = sb("gt_bg", [B, E0])
        al = sb("gt_alpha", [B, 1])
        logits = sb("gt_logits", [B, E0])
        top = sb("gt_top", [B, 8])
        at = sb("gt_at", [B, 8], U32)
        tiny = sb("gt_tiny", [B, 8])
        row_sb = sb("gt_row", [B, NF], U32)
        row_f = sb("gt_row_f", [B, NF])
        coef_sb = sb("gt_coef", [B, NF])
        l_ps = ps("gt_ps")
        loaded = sem("gt_loaded")
        chain = sem("gt_chain")
        exped = sem("gt_exped")
        ready = sem("gt_ready")
        spilled = sem("gt_spilled")
        back = sem("gt_back")
        block = ctx.enter_context(nc.Block())

        @block.sync
        def _(sp):
            sp.dma_start(wg[:], w_gate.rearrange("(k p) e -> p k e", p=P)).then_inc(loaded, 16)
            sp.dma_start(bg[:], b_gate.rearrange("(a e) -> a e", a=1).broadcast_to([B, E0])).then_inc(loaded, 16)
            sp.dma_start(al[:], alpha.broadcast_to([B, 1])).then_inc(loaded, 16)
            sp.wait_ge(chain, 12)
            sp.dma_start(rows_dram, row_sb[:]).then_inc(spilled, 16)
            sp.dma_start(coef_dram, coef_sb[:]).then_inc(spilled, 16)
            sp.wait_ge(spilled, 32)
            sp.dma_start(rows[:], rows_dram.rearrange("(a b) f -> a (b f)", a=1)).then_inc(back, 16)
            sp.dma_start(coef[:], coef_dram.rearrange("(a b) f -> a (b f)", a=1).broadcast_to([P, B * NF]))\
                .then_inc(back, 16)
            sp.wait_ge(back, 32)

        @block.tensor
        def _(pe):
            pe.wait_ge(loaded, 48)
            for k in range(KT):
                ins = pe.matmul(l_ps[0:B, 0:E0], xsum[:, k, :], wg[:, k, :], start=(k == 0), stop=(k == KT - 1))
            ins.then_inc(ready, 1)

        @block.scalar
        def _(act):
            act.wait_ge(chain, 2)
            act.activation(logits[:], logits[:], ACT.Exp, bias=tiny[:, 0:1], accum_out=tiny[:, 1:2])\
                .then_inc(exped, 1)

        @block.vector
        def _(dve):
            count = [0]

            def link(ins):
                count[0] += 1
                ins.then_inc(chain, 1)
                dve.wait_ge(chain, count[0])

            dve.wait_ge(ready, 1)
            link(dve.scalar_tensor_tensor(out=logits[:], in0=l_ps[0:B, 0:E0], scalar=1.0 / S, in1=bg[:],
                                          op0=ALU.mult, op1=ALU.add))
            link(dve.tensor_reduce(tiny[:, 0:1], logits[:], AX.X, ALU.max, negate=True))
            dve.wait_ge(exped, 1)
            link(dve.reciprocal(tiny[:, 2:3], tiny[:, 1:2]))
            link(dve.tensor_scalar(logits[:], logits[:], tiny[:, 2:3], None, ALU.mult))
            link(dve.max(top[:], logits[:]))
            link(dve.max_index(at[:], top[:], logits[:]))
            link(dve.tensor_tensor(tiny[:, 3:4], top[:, 0:1], top[:, 1:2], ALU.add))
            link(dve.reciprocal(tiny[:, 4:5], tiny[:, 3:4]))
            link(dve.tensor_scalar(coef_sb[:, 0:1], al[:], 0.1, 1.0, ALU.max, ALU.min))
            link(dve.tensor_scalar(tiny[:, 5:6], coef_sb[:, 0:1], -1.0, 1.0, ALU.mult, ALU.add))
            link(dve.tensor_scalar(coef_sb[:, 1:NF], top[:, 0:TOP], tiny[:, 4:5], tiny[:, 5:6], ALU.mult, ALU.mult))
            dve.memset(row_sb[:, 0:1], 0)
            link(dve.tensor_scalar(row_sb[:, 1:NF], at[:, 0:TOP], 1.0, None, ALU.add))


def network_phase(nc, x_dram, w1_all, w2_all, b1_all, b2_all, ident, rows, coef, xh_dram, xl_dram, acc, x1_dram):
    R = B * NF
    with ExitStack() as ctx:
        sb, ps, sem = hold(ctx, nc)
        w1_raw = [sb(f"nw_w1_raw{i}", [P, KT, HID]) for i in range(2)]
        w2_raw = [sb(f"nw_w2_raw{i}", [P, MT, D]) for i in range(2)]
        b1 = [sb(f"nw_b1_{i}", [P, MT]) for i in range(2)]
        b2 = [sb(f"nw_b2_{i}", [P, KT]) for i in range(2)]
        w1h, w1l = ([sb(f"nw_w1{x}{i}", [P, KT, HID], F32R) for i in range(2)] for x in "hl")
        w2h, w2l = ([sb(f"nw_w2{x}{i}", [P, MT, D], F32R) for i in range(2)] for x in "hl")
        xh, xl = ([sb(f"nw_x{x}{i}", [P, KT, S], F32R) for i in range(2)] for x in "hl")
        x_raw = sb("nw_x_raw", [P, 2, KT, S])
        hidden = sb("nw_h", [P, SLOTS, S])
        hh, hl = (sb(f"nw_h{x}", [P, SLOTS, S], F32R) for x in "hl")
        coef_now = sb("nw_coef_now", [P, 2])
        bsum = sb("nw_bsum", [P, 2, KT])
        zT = sb("nw_zT", [P, KT, S])
        x_nat = sb("nw_x", [P, TT, D])
        h_ps = [ps(f"nw_h_ps{i}") for i in range(SLOTS)]
        o_ps = [[ps(f"nw_o_ps{i}{k}") for k in range(KT)] for i in range(2)]
        z_ps = ps("nw_z_ps")

        raw_loaded = [sem("nw_raw_loaded0"), sem("nw_raw_loaded1")]
        x_loaded = sem("nw_x_loaded")
        x_placed = sem("nw_x_placed")
        nat_loaded = sem("nw_nat_loaded")
        stored = sem("nw_stored")
        hid_ready = sem("nw_hid_ready")
        unit_done = sem("nw_unit_done")
        z_turned = sem("nw_z_turned")
        gelued = sem("nw_gelued")
        gated = sem("nw_gated")
        h_high = sem("nw_h_high")
        w_high = sem("nw_w_high")
        h_low = sem("nw_h_low")
        w_low = sem("nw_w_low")
        b_sum = sem("nw_b_sum")
        mixed = sem("nw_mixed")
        added = sem("nw_added")
        coef_set = sem("nw_coef_set")
        pool_ticks, sp_ticks = sem("nw_pool_ticks"), sem("nw_sp_ticks")
        x_view = x_dram.rearrange("b (i p) d -> b p i d", p=P)
        x1_view = x1_dram.rearrange("b (i p) d -> b p i d", p=P)
        block = ctx.enter_context(nc.Block())

        @block.sync
        def _(sp):
            def load_round(r, par):
                row = sp.value_load(rows[0:1, ds(r, 1)], min_val=0, max_val=E0)
                sp.dma_start(w1_raw[par][:], w1_all[ds(row, 1)].rearrange("e (k p) h -> p (e k) h", p=P))\
                    .then_inc(raw_loaded[par], 16)
                sp.dma_start(w2_raw[par][:], w2_all[ds(row, 1)].rearrange("e (m p) d -> p (e m) d", p=P))\
                    .then_inc(raw_loaded[par], 16)
                sp.dma_start(b1[par][:], b1_all[ds(row, 1)].rearrange("e p m -> p (e m)")).then_inc(raw_loaded[par], 16)
                sp.dma_start(b2[par][:], b2_all[ds(row, 1)].rearrange("e p k -> p (e k)")).then_inc(raw_loaded[par], 16)

            def load_x(b, par):
                at = b * S
                for c, src in enumerate((xh_dram, xl_dram)):
                    sp.dma_start(x_raw[:, c], src[:, :, ds(at, S)]).then_inc(x_loaded, 16)

            def load_nat(b):
                sp.dma_start(x_nat[:], x_view[ds(b, 1)].rearrange("b p i d -> p (b i) d")).then_inc(nat_loaded, 16)

            load_x(0, 0)
            load_round(0, 0)
            load_round(1, 1)
            sp.wait_ge(x_placed, 1)
            load_x(1, 1)
            load_nat(B - 1)
            with sp.Fori(0, B // 2) as pair:
                for bp in range(2):
                    b = pair * 2 + bp
                    for f in range(NF):
                        r = pair * (2 * NF) + (bp * NF + f)
                        wait_alone(sp, w_low, r * MT + MT, sp_ticks)
                        wait_alone(sp, gelued, r * MT + MT, sp_ticks)
                        wait_alone(sp, b_sum, r + 1, sp_ticks)
                        load_round((r + 2) % R, (NF * bp + f) % 2)
                        if f == 0:
                            wait_alone(sp, added, b * 2 + 2, sp_ticks)
                            sp.dma_start(x1_view[ds((b + (B - 1)) % B, 1)].rearrange("b p i d -> p (b i) d"), x_nat[:])\
                                .then_inc(stored, 16)
                        if f == 1:
                            wait_alone(sp, stored, b * 16 + 16, sp_ticks)
                            load_nat(b)
                    wait_alone(sp, x_placed, b + 2, sp_ticks)
                    load_x((b + 2) % B, bp)
            sp.wait_ge(added, B * 2 + 2)
            sp.dma_start(x1_view[B - 1], x_nat[:]).then_inc(stored, 16)
            sp.wait_ge(stored, (B + 1) * 16)
            sp.wait_ge(x_loaded, 32 * (B + 2))
            for i in range(2):
                sp.wait_ge(raw_loaded[i], 64 * (R // 2 + 1))

        def pieces(par, m):
            c = slice(m * P, m * P + P)
            return ((w1_raw[par][:, :, c], w1h[par][:, :, c], w1l[par][:, :, c]),
                    (w2_raw[par][:, m, :], w2h[par][:, m, :], w2l[par][:, m, :]))

        @block.gpsimd
        def _(pool):
            def split_high(count, par, m):
                for raw, high, _ in pieces(par, m):
                    ins = pool.tensor_scalar(high, raw, 1.0, 1.0, ALU.mult, ALU.mult)
                ins.then_inc(w_high, 1)

            def place_x(n, par):
                wait_alone(pool, x_loaded, n * 32 + 32, pool_ticks)
                for c, part in enumerate((xh[par], xl[par])):
                    ins = pool.tensor_scalar(part[:], x_raw[:, c], 1.0, 1.0, ALU.mult, ALU.mult)
                ins.then_inc(x_placed, 1)

            place_x(0, 0)
            pool.wait_ge(raw_loaded[0], 64)
            for m in range(MT):
                split_high(m + 1, 0, m)
            with pool.Fori(0, B // 2) as pair:
                for bp in range(2):
                    b = pair * 2 + bp
                    for f in range(NF):
                        r = pair * (2 * NF) + (bp * NF + f)
                        par = (bp * NF + f) % 2
                        for m in range(MT):
                            U = r * MT + m
                            slot = (f * MT + m) % SLOTS
                            if m == 0:
                                pool.wait_ge(coef_set, r + 1)
                            pool.wait_ge(gelued, U + 1)
                            wait_alone(pool, unit_done, U + 1, pool_ticks)
                            pool.tensor_scalar(hh[:, slot, :], hidden[:, slot, :], coef_now[:, par:par + 1], 1.0,
                                               ALU.mult, ALU.mult).then_inc(h_high, 1)
                            if m == 0:
                                pool.wait_ge(raw_loaded[1 - par], (pair * NF + (bp * NF + f + 1) // 2) * 64 + 64)
                                wait_alone(pool, unit_done, r * MT + SLOTS, pool_ticks)
                            split_high(U + (MT + 1), 1 - par, m)
                            if f == 1 and m == 4:
                                place_x(b + 1, 1 - bp)

        @block.scalar
        def _(act):
            def gate(b, bp):
                act.wait_ge(unit_done, b * (NF * MT) + SLOTS)
                for k in range(KT):
                    ins = act.activation(zT[:, k, :], o_ps[1 - bp][k][:], ACT.Silu, bias=bsum[:, 1 - bp, k:k + 1])
                ins.then_inc(gated, 1)

            with act.Fori(0, B // 2) as pair:
                for bp in range(2):
                    b = pair * 2 + bp
                    for f in range(NF):
                        par = (bp * NF + f) % 2
                        for m in range(MT):
                            U = pair * (2 * NF * MT) + ((bp * NF + f) * MT + m)
                            slot = (f * MT + m) % SLOTS
                            act.wait_ge(hid_ready, U + 1)
                            act.wait_ge(h_low, U + 1)
                            act.activation(hidden[:, slot, :], h_ps[slot][:], ACT.Gelu_apprx_tanh,
                                           bias=b1[par][:, m:m + 1]).then_inc(gelued, 1)
                            if f == 0 and m == 2:
                                gate(b, bp)
            gate(B, 0)

        @block.vector
        def _(dve):
            dve.memset(bsum[:], 0.0)
            for k in range(KT):
                dve.memset(o_ps[1][k][:], 0.0)
            dve.drain()
            dve.sem_inc(h_low, SLOTS)

            def split_low(count, par, m):
                dve.wait_ge(w_high, count)
                for raw, high, low in pieces(par, m):
                    ins = dve.tensor_tensor(low, raw, high.bitcast(F32), ALU.subtract)
                ins.then_inc(w_low, 1)

            def mix(b, b_before):
                dve.wait_ge(gated, b + 1)
                for k in range(KT):
                    ins = dve.tensor_tensor(zT[:, k, :], zT[:, k, :], acc[:, k, ds(b_before * S, S)], ALU.mult)
                ins.then_inc(mixed, 1)

            def add(b, half):
                dve.wait_ge(z_turned, b * 2 + (half + 1))
                if half == 0:
                    dve.wait_ge(nat_loaded, b * 16 + 16)
                at = x_nat[:, 2 * half:2 * half + 2, :]
                dve.tensor_tensor(at, z_ps[:].rearrange("p (i d) -> p i d", d=D), at, ALU.add).then_inc(added, 1)

            dve.tensor_copy(coef_now[:, 0:1], coef[:, 0:1]).then_inc(coef_set, 1)
            for m in range(MT):
                split_low(m + 1, 0, m)
            with dve.Fori(0, B // 2) as pair:
                for bp in range(2):
                    b = pair * 2 + bp
                    for f in range(NF):
                        r = pair * (2 * NF) + (bp * NF + f)
                        par = (bp * NF + f) % 2
                        if f == 0:
                            dve.tensor_scalar(bsum[:, bp, :], b2[par][:], coef[:, ds(r, 1)], None, ALU.mult)\
                                .then_inc(b_sum, 1)
                        else:
                            dve.wait_ge(b_sum, r)
                            dve.scalar_tensor_tensor(out=bsum[:, bp, :], in0=b2[par][:], scalar=coef[:, ds(r, 1)],
                                                     in1=bsum[:, bp, :], op0=ALU.mult, op1=ALU.add).then_inc(b_sum, 1)
                        for m in range(MT):
                            U = pair * (2 * NF * MT) + ((bp * NF + f) * MT + m)
                            slot = (f * MT + m) % SLOTS
                            dve.wait_ge(h_high, U + 1)
                            if m == 0:
                                dve.wait_ge(coef_set, r + 1)
                            if m == 2:
                                dve.wait_ge(h_low, U + SLOTS)
                                dve.tensor_copy(coef_now[:, 1 - par:2 - par], coef[:, ds((r + 1) % R, 1)])\
                                    .then_inc(coef_set, 1)
                            dve.scalar_tensor_tensor(out=hl[:, slot, :], in0=hidden[:, slot, :],
                                                     scalar=coef_now[:, par:par + 1], in1=hh[:, slot, :].bitcast(F32),
                                                     op0=ALU.mult, op1=ALU.subtract).then_inc(h_low, 1)
                            split_low(U + (MT + 1), 1 - par, m)
                            if f == 0 and m == 3:
                                mix(b, (b + (B - 1)) % B)
                            if f == 0 and m in (5, 7):
                                add(b, (m - 5) // 2)
            mix(B, B - 1)
            add(B, 0)
            add(B, 1)

        @block.tensor
        def _(pe):
            pe.sem_inc(unit_done, SLOTS)

            def hidden_sums(U, pair, c):
                c_round, m = c // MT % (2 * NF), c % MT
                par, bp = c_round % 2, c_round // NF
                if c % (NF * MT) == 0:
                    pe.wait_ge(x_placed, pair * 2 + (c // (NF * MT) + 1))
                pe.wait_ge(w_low, U + 1)
                w = slice(m * P, m * P + P)
                for i, (weight, x) in enumerate([(w1h, xh), (w1l, xh), (w1h, xl)]):
                    for k in range(KT):
                        ins = pe.matmul(h_ps[c % SLOTS][:], weight[par][:, k, w], x[bp][:, k, :],
                                        start=(i == 0 and k == 0), stop=(i == 2 and k == KT - 1))
                ins.then_inc(hid_ready, 1)

            def output_sums(U, c):
                c_round, m = c // MT, c % MT
                par, bp, f = c_round % 2, c_round // NF, c_round % NF
                pe.wait_ge(h_low, U + (SLOTS + 1))
                for k in range(KT):
                    w = slice(k * P, k * P + P)
                    for i, (weight, h) in enumerate([(w2h, hh), (w2l, hh), (w2h, hl)]):
                        ins = pe.matmul(o_ps[bp][k][:], weight[par][:, m, w], h[:, c % SLOTS, :],
                                        start=(f == 0 and m == 0 and i == 0),
                                        stop=(f == NF - 1 and m == MT - 1 and i == 2))
                ins.then_inc(unit_done, 1)

            def turn(b, half):
                if half == 0:
                    pe.wait_ge(mixed, b + 1)
                else:
                    pe.wait_ge(added, b * 2 + 1)
                for i in range(2):
                    for k in range(KT):
                        at = (2 * half + i) * P
                        ins = pe.transpose(z_ps[:, i * D + k * P:i * D + k * P + P], zT[:, k, at:at + P], ident[:])
                ins.then_inc(z_turned, 1)

            hidden_sums(0, 0, 0)
            hidden_sums(1, 0, 1)
            with pe.Fori(0, B // 2) as pair:
                for c in range(2 * NF * MT):
                    U = pair * (2 * NF * MT) + c
                    hidden_sums(pair * (2 * NF * MT) + (c + 2), pair, c + 2)
                    output_sums(U, c)
                    if c % (NF * MT) in (4, 6):
                        turn(pair * 2 + c // (NF * MT), (c % (NF * MT) - 4) // 2)
            turn(B, 0)
            turn(B, 1)


def head_attention_phase(nc, w_heads, wo_heads, slopes, ident, xh, xl, acc):
    with ExitStack() as ctx:
        sb, ps, sem = hold(ctx, nc)
        rel = sb("at_rel", [P, S])
        slope_sb = sb("at_slope", [P, 2 * KVH])
        bias = sb("at_bias", [P, 2, S])
        w_raw = [sb(f"at_w_raw{i}", [P, KT, 256]) for i in range(2)]
        wo_raw = [sb(f"at_wo_raw{i}", [P, D]) for i in range(2)]
        wh, wl = (sb(f"at_w{x}", [P, KT, 256], F32R) for x in "hl")
        woh, wol = (sb(f"at_wo{x}", [P, D], F32R) for x in "hl")
        qst = [sb(f"at_q{i}", [P, 2, S], F32R) for i in range(2)]
        kh = [sb(f"at_kh{i}", [P, S], F32R) for i in range(2)]
        kl = [sb(f"at_kl{i}", [P, S], F32R) for i in range(2)]
        k_parts = sb("at_k_parts", [P, 2, S], F32R)
        k_twice = [sb(f"at_k_twice{i}", [P, 2, S]) for i in range(2)]
        vT = sb("at_vT", [P, S])
        v = [sb(f"at_v{i}", [P, TT, HD]) for i in range(2)]
        s_sb = sb("at_s", [P, 4, S])
        p_sb = sb("at_p", [P, 4, S])
        pT = sb("at_pT", [P, 4, S])
        nmax = sb("at_nmax", [P, 2, 8])
        total = sb("at_total", [P, 2, 8])
        recip = sb("at_recip", [P, 2, 8])
        oh = [sb(f"at_oh{i}", [P, S], F32R) for i in range(2)]
        ol = [sb(f"at_ol{i}", [P, S], F32R) for i in range(2)]

        s_ps = [ps(f"at_s_ps{i}") for i in range(2)]
        t_ps = [ps(f"at_t_ps{i}") for i in range(2)]
        o_ps = [ps(f"at_o_ps{i}") for i in range(2)]
        m_ps = [ps(f"at_m_ps{i}") for i in range(2)]

        w_loaded = [sem("at_w_loaded0"), sem("at_w_loaded1")]
        slope_loaded = sem("at_slope_loaded")
        k_copied = [sem("at_k_copied0"), sem("at_k_copied1")]
        consts = sem("at_consts")
        w_split = sem("at_w_split")
        wo_split = sem("at_wo_split")
        w_chain = sem("at_w_chain")
        k_placed = sem("at_k_placed")
        scaled = sem("at_scaled")
        proj = sem("at_proj")
        scored = sem("at_scored")
        turned = sem("at_turned")
        summed = sem("at_summed")
        q_high = sem("at_q_high")
        vT_out = sem("at_vT_out")
        exped = sem("at_exped")
        o_high = sem("at_o_high")
        odd_out = sem("at_odd_out")
        even_out = sem("at_even_out")
        biased = sem("at_biased")
        masked = sem("at_masked")
        recips = sem("at_recips")
        proj_out = sem("at_proj_out")
        o_low = sem("at_o_low")
        zeroed = sem("at_zeroed")
        pool_ticks, dve_ticks, pe_ticks = sem("at_pool_ticks"), sem("at_dve_ticks"), sem("at_pe_ticks")
        block = ctx.enter_context(nc.Block())

        def q_count(n):
            return n * 5 + (-1)

        def kv_count(n):
            return n * 5

        def v_count(n):
            return n * 5 + 1

        def out_count(n, m):
            return n * 5 + (12 + m)

        def after(half, par):
            return (half, 1) if par == 0 else (half + 1, 0)

        PAIRS = B // 2

        @block.sync
        def _(sp):
            sp.dma_start(slope_sb[:], slopes).then_inc(slope_loaded, 16)
            for i in range(2):
                sp.dma_start(w_raw[i][:], w_heads[i]).then_inc(w_loaded[i], 16)
                sp.dma_start(wo_raw[i][:], wo_heads[i]).then_inc(w_loaded[i], 16)

            def copy_k(count, par):
                sp.wait_ge(proj_out, count)
                for half in range(2):
                    sp.dma_start(k_twice[par][HD * half:HD * half + HD, :, :], k_parts[0:HD, :, :].bitcast(F32))\
                        .then_inc(k_copied[par], 16)

            copy_k(2, 0)
            with sp.Fori(0, KVH // 2) as jj:
                for jp in range(2):
                    j = jj * 2 + jp
                    with sp.Fori(0, PAIRS) as pair:
                        for par in range(2):
                            copy_k(kv_count(j * B + pair * 2 + (par + 1)), 1 - par)
                    sp.wait_ge(w_split, j + 1)
                    sp.wait_ge(wo_split, j + 1)
                    sp.dma_start(w_raw[jp][:], w_heads[ds((j + 2) % KVH, 1)].rearrange("a p k n -> p (a k) n"))\
                        .then_inc(w_loaded[jp], 16)
                    sp.dma_start(wo_raw[jp][:], wo_heads[ds((j + 2) % KVH, 1)].rearrange("a p n -> p (a n)"))\
                        .then_inc(w_loaded[jp], 16)
            for i in range(2):
                sp.wait_ge(w_loaded[i], 32 * (KVH // 2 + 1))
                sp.wait_ge(k_copied[i], 32 * (KVH * B // 2 + 1 - i))
            sp.wait_ge(k_placed, KVH * B + 1)

        @block.gpsimd
        def _(pool):
            pool.iota(rel[:], [[-1, S]], base=S - P, channel_multiplier=1,
                      allow_small_or_imprecise_dtypes=True).then_inc(consts, 1)
            pool.wait_ge(consts, 1)
            pool.affine_select(out=rel[:], in_=rel[:], compare_op=ALU.is_ge, fill=BIG, base=S - P,
                               pattern=[[-1, S]], channel_multiplier=1).then_inc(consts, 1)

            def split(hi, lo, raw, n):
                pool.tensor_scalar(hi, raw, 1.0, 1.0, ALU.mult, ALU.mult).then_inc(w_chain, 1)
                pool.wait_ge(w_chain, n + 1)
                return pool.tensor_tensor(lo, raw, hi.bitcast(F32), ALU.subtract)

            pool.wait_ge(w_loaded[0], 32)
            split(wh[:], wl[:], w_raw[0][:], 0).then_inc(w_split, 1)

            def place_k(n, half, par):
                wait_alone(pool, k_copied[par], half * 32 + 32, pool_ticks)
                for c, part in enumerate((kh[par], kl[par])):
                    ins = pool.tensor_scalar(part[:], k_twice[par][:, c, :], 1.0, 1.0, ALU.mult, ALU.mult)
                ins.then_inc(k_placed, 1)

            def step(t, half, par):
                for qt in range(TT):
                    if qt == 3:
                        place_k(t + 1, after(half, par)[0], 1 - par)
                    wait_alone(pool, recips, t * TT + (qt + 1), pool_ticks)
                    for h in range(2):
                        u = 2 * qt + h
                        p = p_sb[:, u % 4, 0:(qt + 1) * P]
                        pool.tensor_scalar(p, p, recip[:, par, u:u + 1], 1.0, ALU.mult, ALU.mult).then_inc(scaled, 1)

            place_k(0, 0, 0)
            with pool.Fori(0, KVH // 2) as jj:
                for jp in range(2):
                    j = jj * 2 + jp
                    step(j * B, j * PAIRS, 0)
                    pool.wait_ge(proj, j * (5 * B) + out_count(-1, 1))
                    wait_alone(pool, w_loaded[jp], jj * 32 + 32, pool_ticks)
                    split(woh[:], wol[:], wo_raw[jp][:], j * 2 + 1).then_inc(wo_split, 1)
                    step(j * B + 1, j * PAIRS, 1)
                    with pool.Fori(1, PAIRS - 1) as pair:
                        for par in range(2):
                            step(j * B + pair * 2 + par, j * PAIRS + pair, par)
                    step(j * B + (B - 2), j * PAIRS + (PAIRS - 1), 0)
                    pool.wait_ge(proj, j * (5 * B) + kv_count(B - 1))
                    wait_alone(pool, w_loaded[1 - jp], (jj + jp) * 32 + 32, pool_ticks)
                    split(wh[:], wl[:], w_raw[1 - jp][:], j * 2 + 2).then_inc(w_split, 1)
                    step(j * B + (B - 1), j * PAIRS + (PAIRS - 1), 1)

        @block.scalar
        def _(act):
            def take_q(count, par):
                act.wait_ge(proj, count)
                act.activation(qst[par][0:HD, 0, :], m_ps[par][0:HD, :], ACT.Copy, scale=-HD ** -0.5)
                act.activation(qst[par][HD:P, 1, :], m_ps[par][HD:P, :], ACT.Copy, scale=-HD ** -0.5)\
                    .then_inc(q_high, 1)

            def take_kv(count, par, n=None):
                act.wait_ge(proj, count)
                if n is not None:
                    act.wait_ge(k_placed, n)
                act.activation(k_parts[0:HD, 0, :], m_ps[1 - par][0:HD, :], ACT.Copy)
                act.activation(vT[HD:P, :], m_ps[1 - par][HD:P, :], ACT.Copy).then_inc(vT_out, 1)

            def exps(n, par, u):
                N = (u // 2 + 1) * P
                act.wait_ge(masked, n * 8 + (u + 1))
                act.activation(p_sb[:, u % 4, 0:N], s_sb[:, u % 4, 0:N], ACT.Exp, bias=nmax[:, par, u:u + 1],
                               scale=-1.0, accum_out=total[:, par, u:u + 1]).then_inc(exped, 1)

            def turn_out(n, u):
                N = (u // 2 + 1) * P
                act.wait_ge(turned, n * 8 + (u + 1))
                if u >= 4:
                    act.wait_ge(summed, n * 4 + (u // 2 - 1))
                act.activation(pT[:, u % 4, 0:N], t_ps[u % 2][:, 0:N], ACT.Copy).then_inc(odd_out, 1)

            def step(t, par):
                nxt = 1 - par
                exps(t, par, 2)
                exps(t, par, 3)
                take_q(q_count(t + 1), nxt)
                turn_out(t, 1)
                take_kv(kv_count(t + 1), nxt, t + 1)
                exps(t, par, 4)
                turn_out(t, 3)
                exps(t, par, 5)
                exps(t, par, 6)
                turn_out(t, 5)
                exps(t, par, 7)
                exps(t + 1, nxt, 0)
                exps(t + 1, nxt, 1)
                turn_out(t, 7)
                act.wait_ge(summed, t * 4 + 4)
                act.activation(oh[par][:], o_ps[par][:], ACT.Copy).then_inc(o_high, 1)

            take_q(1, 0)
            take_kv(2, 0)
            exps(0, 0, 0)
            exps(0, 0, 1)
            with act.Fori(0, KVH * B // 2) as pair:
                for par in range(2):
                    step(pair * 2 + par, par)

        @block.vector
        def _(dve):
            dve.memset(acc[:], 0.0).then_inc(zeroed, 1)
            dve.wait_ge(zeroed, 1)
            for tile in (woh, wol, oh[1], ol[1]):
                ins = dve.tensor_copy(tile[:], acc[:, 0, 0:tile.shape[1]])
            ins.then_inc(o_low, 1)
            dve.wait_ge(slope_loaded, 16)
            dve.wait_ge(consts, 2)

            def set_bias(j, first, count):
                for h in range(2):
                    at = h if first else ds((j * 2 + h) % (2 * KVH), 1)
                    slope = slope_sb[:, h:h + 1] if first else slope_sb[:, at]
                    dve.tensor_scalar(bias[:, h, :], rel[:], slope, None, ALU.mult).then_inc(biased, 1)
                dve.wait_ge(biased, count)

            def q_rest(n, par):
                dve.wait_ge(q_high, n + 1)
                dve.scalar_tensor_tensor(out=qst[par][HD:P, 0, :], in0=m_ps[par][0:HD, :], scalar=-HD ** -0.5,
                                         in1=qst[par][0:HD, 0, :].bitcast(F32), op0=ALU.mult, op1=ALU.subtract)
                dve.scalar_tensor_tensor(out=qst[par][0:HD, 1, :], in0=m_ps[par][HD:P, :], scalar=-HD ** -0.5,
                                         in1=qst[par][HD:P, 1, :].bitcast(F32), op0=ALU.mult, op1=ALU.subtract)\
                    .then_inc(proj_out, 1)

            def k_rest(n, par):
                dve.wait_ge(vT_out, n + 1)
                dve.tensor_tensor(k_parts[0:HD, 1, :], m_ps[1 - par][0:HD, :], k_parts[0:HD, 0, :].bitcast(F32),
                                  ALU.subtract).then_inc(proj_out, 1)

            def values(count, par):
                dve.wait_ge(proj, count)
                dve.tensor_copy(v[par][:].rearrange("p i d -> p (i d)"), m_ps[par][:, 0:TT * HD])\
                    .then_inc(proj_out, 1)

            def mask(n, par, u):
                N = (u // 2 + 1) * P
                wait_alone(dve, scored, n * 8 + (u + 1), dve_ticks)
                dve.tensor_tensor_reduce(out=s_sb[:, u % 4, 0:N], in0=s_ps[u % 2][:, 0:N],
                                         in1=bias[:, u % 2, S - N:S], scale=1.0, scalar=BIG, op0=ALU.add,
                                         op1=ALU.min, accum_out=nmax[:, par, u:u + 1]).then_inc(masked, 1)

            def invert(n, par, qt):
                dve.wait_ge(exped, n * 8 + (2 * qt + 2))
                dve.reciprocal(recip[:, par, 2 * qt:2 * qt + 2], total[:, par, 2 * qt:2 * qt + 2]).then_inc(recips, 1)

            def turn_out(n, u):
                N = (u // 2 + 1) * P
                dve.wait_ge(turned, n * 8 + (u + 1))
                if u >= 4:
                    dve.wait_ge(summed, n * 4 + (u // 2 - 1))
                dve.tensor_copy(pT[:, u % 4, 0:N], t_ps[u % 2][:, 0:N]).then_inc(even_out, 1)

            def add_out(n, par, b, skipped=0):
                for m in range(KT):
                    dve.wait_ge(proj, out_count(n, m) + (-skipped))
                    at = acc[:, m, ds(b * S, S)]
                    dve.tensor_tensor(at, m_ps[(par + 1 + m + skipped) % 2][:], at, ALU.add).then_inc(proj_out, 1)

            def step(t, par, b_before, new_head=None):
                nxt = 1 - par
                mask(t, par, 2)
                mask(t, par, 3)
                invert(t, par, 0)
                q_rest(t + 1, nxt)
                mask(t, par, 4)
                turn_out(t, 0)
                k_rest(t + 1, nxt)
                invert(t, par, 1)
                turn_out(t, 2)
                mask(t, par, 5)
                values(v_count(t + 1), nxt)
                mask(t, par, 6)
                invert(t, par, 2)
                turn_out(t, 4)
                mask(t, par, 7)
                add_out(t + (-1), nxt, b_before)
                if new_head is not None:
                    dve.wait_ge(masked, t * 8 + 8)
                    set_bias(new_head, False, new_head * 2 + 2)
                invert(t, par, 3)
                mask(t + 1, nxt, 0)
                mask(t + 1, nxt, 1)
                turn_out(t, 6)
                dve.wait_ge(o_high, t + 1)
                dve.tensor_tensor(ol[par][:], o_ps[par][:], oh[par][:].bitcast(F32), ALU.subtract).then_inc(o_low, 1)

            set_bias(0, True, 2)
            q_rest(0, 0)
            k_rest(0, 0)
            values(3, 0)
            mask(0, 0, 0)
            mask(0, 0, 1)
            with dve.Fori(0, KVH) as j:
                with dve.Fori(0, PAIRS - 1) as pair:
                    for par in range(2):
                        step(j * B + pair * 2 + par, par, (pair * 2 + (par + B - 1)) % B)
                step(j * B + (B - 2), 0, B - 3)
                step(j * B + (B - 1), 1, B - 2, new_head=j + 1)
            add_out(KVH * B - 1, 1, B - 1, skipped=3)

        @block.tensor
        def _(pe):
            def project(bank, w, b):
                terms = [(wh, xh), (wl, xh), (wh, xl)]
                for i, (weight, x) in enumerate(terms):
                    for k in range(KT):
                        ins = pe.matmul(bank[:], weight[:, k, w:w + P], x[:, k, ds(b * S, S)],
                                        start=(i == 0 and k == 0), stop=(i == 2 and k == KT - 1))
                ins.then_inc(proj, 1)

            def project_q(n, par, b):
                pe.wait_ge(proj_out, q_count(n) + (-2))
                project(m_ps[par], 0, b)

            def project_kv(n, par, b):
                pe.wait_ge(proj_out, kv_count(n) + (-2))
                project(m_ps[1 - par], P, b)

            def turn_v(n, par, out):
                pe.wait_ge(vT_out, n + 1)
                wait_alone(pe, proj_out, out, pe_ticks)
                for i in range(TT):
                    ins = pe.transpose(m_ps[par][:, HD * i:HD * i + HD], vT[HD:P, P * i:P * i + P], ident[HD:P, HD:P])
                ins.then_inc(proj, 1)

            def project_out(n, par, skipped=0):
                pe.wait_ge(o_low, n + 2)
                for m in range(KT):
                    bank = m_ps[(par + 1 + m + skipped) % 2]
                    pe.wait_ge(proj_out, out_count(n, m) + (-2 - skipped))
                    for i, (w, o) in enumerate([(woh, oh), (wol, oh), (woh, ol)]):
                        ins = pe.matmul(bank[:], w[:, m * P:m * P + P], o[par][:], start=(i == 0), stop=(i == 2))
                    ins.then_inc(proj, 1)

            def score(n, half, par, u, first=False):
                N = (u // 2 + 1) * P
                if u == 0:
                    pe.wait_ge(proj_out, 2 if first else kv_count(n))
                    wait_alone(pe, k_placed, n + 1, pe_ticks)
                if not first:
                    pe.wait_ge(masked, n * 8 + (u - 1))
                q = qst[par][:, u % 2, u // 2 * P:(u // 2 + 1) * P]
                pe.matmul(s_ps[u % 2][:, 0:N], q, kh[par][:, 0:N], start=True, stop=False)
                pe.matmul(s_ps[u % 2][:, 0:N], q, kl[par][:, 0:N], start=False, stop=True).then_inc(scored, 1)

            def turn(n, u):
                pe.wait_ge(scaled, n * 8 + (u + 1))
                for k in range(u // 2 + 1):
                    ins = pe.transpose(t_ps[u % 2][:, k * P:k * P + P], p_sb[:, u % 4, k * P:k * P + P], ident[:])
                ins.then_inc(turned, 1)

            def weigh(n, par, qt):
                pe.wait_ge(even_out, n * 4 + (qt + 1))
                pe.wait_ge(odd_out, n * 4 + (qt + 1))
                for k in range(qt + 1):
                    for h in range(2):
                        ins = pe.matmul(o_ps[par][HD * h:HD * h + HD, qt * P:qt * P + P], v[par][:, k, :],
                                        pT[:, (2 * qt + h) % 4, k * P:k * P + P], start=(k == 0), stop=(k == qt))
                ins.then_inc(summed, 1)

            def step(t, half, par, b_next, new_head=None, new_out=None):
                nxt, (nxt_half, _) = 1 - par, after(half, par)
                score(t, half, par, 2)
                score(t, half, par, 3)
                if new_head is not None:
                    pe.wait_ge(w_split, new_head + 1)
                project_q(t + 1, nxt, b_next)
                turn(t, 0)
                turn(t, 1)
                score(t, half, par, 4)
                project_kv(t + 1, nxt, b_next)
                weigh(t, par, 0)
                turn(t, 2)
                turn(t, 3)
                score(t, half, par, 5)
                turn_v(t + 1, nxt, v_count(t + 1) + (-2))
                weigh(t, par, 1)
                score(t, half, par, 6)
                turn(t, 4)
                turn(t, 5)
                score(t, half, par, 7)
                if new_out is not None:
                    pe.wait_ge(wo_split, new_out + 1)
                project_out(t + (-1), nxt)
                weigh(t, par, 2)
                score(t + 1, nxt_half, nxt, 0)
                score(t + 1, nxt_half, nxt, 1)
                turn(t, 6)
                turn(t, 7)
                weigh(t, par, 3)

            pe.wait_ge(w_split, 1)
            project(m_ps[0], 0, 0)
            project(m_ps[1], P, 0)
            turn_v(0, 0, 1)
            score(0, 0, 0, 0, first=True)
            score(0, 0, 0, 1, first=True)
            with pe.Fori(0, KVH) as j:
                step(j * B, j * PAIRS, 0, 1)
                step(j * B + 1, j * PAIRS, 1, 2, new_out=j)
                with pe.Fori(1, PAIRS - 1) as pair:
                    for par in range(2):
                        step(j * B + pair * 2 + par, j * PAIRS + pair, par, pair * 2 + (par + 1))
                step(j * B + (B - 2), j * PAIRS + (PAIRS - 1), 0, B - 1)
                step(j * B + (B - 1), j * PAIRS + (PAIRS - 1), 1, 0, new_head=j + 1)
            project_out(KVH * B - 1, 1, skipped=3)


RH = D // HD
WIDTHS = [S - P * i for i in range(TT)]
STARTS = [sum(WIDTHS[:i]) for i in range(TT)]
EPS_RMS = 1.1920928955078125e-07


def recurrence_phase(nc, x1_dram, w_write, w_read, decay, log_alpha, ident, y, r1, s_dram):
    with ExitStack() as ctx:
        sb, ps, sem = hold(ctx, nc)
        x_in = [sb(f"rc_x{i}", [P, TT, D]) for i in range(2)]
        stats = sb("rc_stats", [P, TT, 6])
        mv = sb("rc_mv", [P, TT, 2])
        std = sb("rc_std", [P, 2, TT])
        rstd = sb("rc_rstd", [P, TT])
        squares = sb("rc_squares", [P, TT, D])
        sq_sum = sb("rc_sq_sum", [P, TT])
        eps = sb("rc_eps", [P, 2])
        carry = sb("rc_carry", [P, 1])
        ww = sb("rc_ww", [P, KT, D])
        wr = sb("rc_wr", [P, KT, D])
        gam = sb("rc_gam", [P, RH])
        la = sb("rc_la", [P, RH])
        ahead = sb("rc_ahead", [P, S])
        factor = sb("rc_factor", [P, RH, S])
        yT = [sb(f"rc_yT{i}", [P, KT, S + 1]) for i in range(2)]
        v = [sb(f"rc_v{i}", [P, TT, D]) for i in range(2)]
        prod = sb("rc_prod", [P, RH, sum(WIDTHS)])
        readT = sb("rc_readT", [P, KT, S])
        s_sb = [sb(f"rc_s{i}", [P, TT, D]) for i in range(2)]
        xT_ps = [ps(f"rc_xT_ps{k}") for k in range(KT)]
        n_ps = [ps(f"rc_n_ps{k}") for k in range(2)]
        d_ps = [ps(f"rc_d_ps{k}") for k in range(2)]
        r_ps = [ps(f"rc_r_ps{k}") for k in range(2)]

        x_loaded = [sem("rc_x_loaded0"), sem("rc_x_loaded1")]
        w_loaded = sem("rc_w_loaded")
        s_stored = [sem("rc_s_stored0"), sem("rc_s_stored1")]
        s_free = sem("rc_s_free")
        pool_chain = sem("rc_pool_chain")
        act_chain = sem("rc_act_chain")
        dve_chain = sem("rc_dve_chain")
        stats_done = sem("rc_stats_done")
        var_done = sem("rc_var_done")
        std_done = sem("rc_std_done")
        rstd_done = sem("rc_rstd_done")
        normed = sem("rc_normed")
        copied = sem("rc_copied")
        sp_ticks = sem("rc_sp_ticks")
        squared = sem("rc_squared")
        rms_done = sem("rc_rms_done")
        r1_done = sem("rc_r1_done")
        turned = sem("rc_turned")
        turn_out = sem("rc_turn_out")
        valued = sem("rc_valued")
        value_out = sem("rc_value_out")
        dotted = sem("rc_dotted")
        decayed = sem("rc_decayed")
        read = sem("rc_read")
        read_out = sem("rc_read_out")
        mixed = sem("rc_mixed")
        s_done = sem("rc_s_done")
        dve_ticks = sem("rc_dve_ticks")
        x_view = x1_dram.rearrange("b (i p) d -> b p i d", p=P)
        s_view = s_dram.rearrange("b (i p) d -> b p i d", p=P)
        block = ctx.enter_context(nc.Block())

        def row(vector):
            return vector.rearrange("(a h) -> a h", a=1).broadcast_to([P, RH])

        @block.sync
        def _(sp):
            sp.sem_inc(s_free, 2)
            for i in range(2):
                sp.dma_start(x_in[i][:], x_view[i]).then_inc(x_loaded[i], 16)
            sp.dma_start(gam[:], row(decay)).then_inc(w_loaded, 16)
            sp.dma_start(la[:], row(log_alpha)).then_inc(w_loaded, 16)
            sp.dma_start(ww[:], w_write.rearrange("(k p) n -> p k n", p=P)).then_inc(w_loaded, 16)
            sp.dma_start(wr[:], w_read.rearrange("(k p) n -> p k n", p=P)).then_inc(w_loaded, 16)
            with sp.Fori(0, B // 2) as pair:
                for par in range(2):
                    b = pair * 2 + par
                    sp.wait_ge(turned, b + 1)
                    sp.wait_ge(rms_done, b + 1)
                    wait_alone(sp, copied, b + 1, sp_ticks)
                    sp.dma_start(x_in[par][:], x_view[ds((b + 2) % B, 1)].rearrange("b p i d -> p (b i) d"))\
                        .then_inc(x_loaded[par], 16)
                    sp.wait_ge(s_done, b * 2 + 2)
                    sp.dma_start(s_view[ds(b, 1)].rearrange("b p i d -> p (b i) d"), s_sb[par][:])\
                        .then_inc(s_stored[par], 16)
                    sp.wait_ge(s_stored[par], pair * 16 + 16)
                    sp.sem_inc(s_free, 1)
            for i in range(2):
                sp.wait_ge(x_loaded[i], 16 * (B // 2 + 1))
                sp.wait_ge(s_stored[i], 16 * (B // 2))

        @block.gpsimd
        def _(pool):
            pool.iota(ahead[:], [[1, S]], base=-1, channel_multiplier=-1,
                      allow_small_or_imprecise_dtypes=True).then_inc(pool_chain, 1)
            pool.wait_ge(act_chain, 2 + RH)
            for h in range(RH):
                pool.affine_select(out=factor[:, h, :], in_=factor[:, h, :], compare_op=ALU.is_ge, fill=0.0,
                                   base=-1, pattern=[[1, S]], channel_multiplier=-1).then_inc(pool_chain, 1)

        @block.scalar
        def _(act):
            act.wait_ge(w_loaded, 64)
            act.activation(gam[:], gam[:], ACT.Exp, scale=-1.0).then_inc(act_chain, 1)
            act.wait_ge(dve_chain, 2)
            act.activation(gam[:], gam[:], ACT.Ln).then_inc(act_chain, 1)
            act.wait_ge(dve_chain, 3)
            for h in range(RH):
                act.activation(factor[:, h, :], ahead[:], ACT.Exp, scale=gam[:, h:h + 1], bias=la[:, h:h + 1])\
                    .then_inc(act_chain, 1)

            def roots(n, par):
                act.wait_ge(var_done, n * TT + TT)
                act.activation(std[:, 0, :], mv[:, :, 1], ACT.Sqrt, bias=eps[:, 0:1]).then_inc(std_done, 1)

            def rms(n, par):
                act.wait_ge(normed, n * TT + TT)
                for i in range(TT):
                    act.activation(squares[:, i, :], x_in[par][:, i, :], ACT.Square,
                                   accum_out=sq_sum[:, i:i + 1]).then_inc(squared, 1)
                act.wait_ge(squared, n * TT + TT)
                act.activation(std[:, 1, :], sq_sum[:], ACT.Sqrt, scale=1.0 / D, bias=eps[:, 1:2]).then_inc(rms_done, 1)

            def take_turn(n, par):
                act.wait_ge(turned, n + 1)
                for k in range(KT):
                    ins = act.activation(yT[par][:, k, 1:S + 1], xT_ps[k][:], ACT.Copy)
                ins.then_inc(turn_out, 1)

            def take_values(n, par):
                for half in range(2):
                    act.wait_ge(valued, n * 2 + (half + 1))
                    act.activation(v[par][:, 2 * half:2 * half + 2, :].rearrange("p i d -> p (i d)"), n_ps[half][:],
                                   ACT.Copy).then_inc(value_out, 1)

            def take_read(n, g):
                act.wait_ge(read, n * 2 + (g + 1))
                act.activation(readT[:, g, :], r_ps[g][:], ACT.Copy).then_inc(read_out, 1)

            roots(0, 0)
            rms(0, 0)
            take_turn(0, 0)
            take_values(0, 0)
            with act.Fori(0, B // 2) as pair:
                for par in range(2):
                    b, nxt = pair * 2 + par, 1 - par
                    roots(b + 1, nxt)
                    rms(b + 1, nxt)
                    take_turn(b + 1, nxt)
                    take_read(b, 0)
                    take_values(b + 1, nxt)
                    take_read(b, 1)

        @block.vector
        def _(dve):
            dve.sem_inc(decayed, 2)
            dve.memset(eps[:, 0:1], EPS_LN)
            dve.memset(eps[:, 1:2], EPS_RMS)
            for i in range(2):
                dve.memset(yT[i][:, :, 0:1], 0.0)
            dve.wait_ge(pool_chain, 1)
            dve.tensor_scalar(ahead[:], ahead[:], 0.0, None, ALU.max).then_inc(dve_chain, 1)
            dve.wait_ge(act_chain, 1)
            dve.tensor_scalar(gam[:], gam[:], 1.0, None, ALU.add).then_inc(dve_chain, 1)
            dve.wait_ge(act_chain, 2)
            dve.tensor_scalar(gam[:], gam[:], -1.0, None, ALU.mult).then_inc(dve_chain, 1)

            def norm(n, pair_n, par):
                wait_alone(dve, x_loaded[par], pair_n * 16 + 16, dve_ticks)
                for i in range(TT):
                    dve.bn_stats(stats[:, i, :], x_in[par][:, i, :]).then_inc(stats_done, 1)
                wait_alone(dve, stats_done, n * TT + TT, dve_ticks)
                for i in range(TT):
                    dve.bn_aggr(mv[:, i, :], stats[:, i, :]).then_inc(var_done, 1)
                dve.wait_ge(std_done, n + 1)
                dve.reciprocal(rstd[:], std[:, 0, :]).then_inc(rstd_done, 1)
                dve.wait_ge(rstd_done, n + 1)
                for i in range(TT):
                    dve.tensor_scalar(x_in[par][:, i, :], x_in[par][:, i, :], mv[:, i, 0:1], rstd[:, i:i + 1], ALU.subtract, ALU.mult).then_inc(normed, 1)
                wait_alone(dve, normed, n * TT + TT, dve_ticks)
                dve.tensor_copy(y[:, ds((n % B) * TT, TT), :], x_in[par][:]).then_inc(copied, 1)
                dve.wait_ge(rms_done, n + 1)
                dve.reciprocal(r1[:, ds((n % B) * TT, TT)], std[:, 1, :]).then_inc(r1_done, 1)

            def decay_unit(n, h, i):
                dve.wait_ge(dotted, n * (RH * TT) + (h * TT + i + 1))
                dve.tensor_tensor(prod[:, h, STARTS[i]:STARTS[i] + WIDTHS[i]], d_ps[i % 2][:, 0:WIDTHS[i]],
                                  factor[:, h, 0:WIDTHS[i]], ALU.mult).then_inc(decayed, 1)

            def finish(n, par):
                wait_alone(dve, copied, n + 1, dve_ticks)
                dve.wait_ge(s_free, n + 1)
                for half in range(2):
                    dve.wait_ge(mixed, n * 2 + (half + 1))
                    dve.tensor_tensor(s_sb[par][:, 2 * half:2 * half + 2, :].rearrange("p i d -> p (i d)"), n_ps[half][:],
                                      y[:, ds(n * TT + 2 * half, 2), :].rearrange("p i d -> p (i d)"), ALU.add)\
                        .then_inc(s_done, 1)

            norm(0, 0, 0)
            dve.wait_ge(pool_chain, 1 + RH)
            with dve.Fori(0, B // 2) as pair:
                for par in range(2):
                    b, nxt = pair * 2 + par, 1 - par
                    for h in range(RH):
                        for i in range(TT):
                            decay_unit(b, h, i)
                        if h == 0:
                            norm(b + 1, pair + par, nxt)
                    finish(b, par)

        @block.tensor
        def _(pe):
            def turn(n, par):
                pe.wait_ge(normed, n * TT + TT)
                for k in range(KT):
                    for i in range(TT):
                        ins = pe.transpose(xT_ps[k][:, P * i:P * i + P], x_in[par][:, i, P * k:P * k + P], ident[:])
                ins.then_inc(turned, 1)

            def values(n, par):
                pe.wait_ge(turn_out, n + 1)
                for half in range(2):
                    for i in range(2):
                        for k in range(KT):
                            at = 1 + (2 * half + i) * P
                            ins = pe.matmul(n_ps[half][:, i * D:i * D + D], yT[par][:, k, at:at + P], ww[:, k, :],
                                            start=(k == 0), stop=(k == KT - 1))
                    ins.then_inc(valued, 1)

            def dots(n, par, h):
                row = slice(HD * (h % 2), HD * (h % 2) + HD)
                for i in range(TT):
                    pe.wait_ge(decayed, n * (RH * TT) + (h * TT + i + 1))
                    pe.matmul(d_ps[i % 2][:, 0:WIDTHS[i]], yT[par][row, h // 2, P * i:P * i + P],
                              yT[par][row, h // 2, 1 + P * i:1 + S], start=True, stop=True).then_inc(dotted, 1)

            def reads(n, par, g):
                pe.wait_ge(decayed, n * (RH * TT) + ((2 * g + 2) * TT + 2))
                for i in range(TT):
                    for h in range(2):
                        head = 2 * g + h
                        ins = pe.matmul(r_ps[g][HD * h:HD * h + HD, P * i:S], v[par][:, i, HD * head:HD * head + HD],
                                        prod[:, head, STARTS[i]:STARTS[i] + WIDTHS[i]],
                                        start=(i == 0), stop=(i == TT - 1))
                ins.then_inc(read, 1)

            def mix(n):
                pe.wait_ge(read_out, n * 2 + 2)
                for half in range(2):
                    for i in range(2):
                        for g in range(KT):
                            at = (2 * half + i) * P
                            ins = pe.matmul(n_ps[half][:, i * D:i * D + D], readT[:, g, at:at + P], wr[:, g, :],
                                            start=(g == 0), stop=(g == KT - 1))
                    ins.then_inc(mixed, 1)

            pe.wait_ge(w_loaded, 64)
            turn(0, 0)
            values(0, 0)
            with pe.Fori(0, B // 2) as pair:
                for par in range(2):
                    b, nxt = pair * 2 + par, 1 - par
                    dots(b, par, 0)
                    dots(b, par, 1)
                    turn(b + 1, nxt)
                    dots(b, par, 2)
                    pe.wait_ge(value_out, b * 2 + 2)
                    reads(b, par, 0)
                    values(b + 1, nxt)
                    dots(b, par, 3)
                    reads(b, par, 1)
                    pe.wait_ge(value_out, b * 2 + 4)
                    mix(b)


QH = 16
QD = D // QH
KV1 = 4
REP = QH // KV1
VP = 32
RING = 4
QUADS = KV1 * TT
PROJ = {"q0": 0, "s0": 2 * P, "q1": P, "s1": 3 * P, "kk": 4 * P, "v": 5 * P}
PROJ_COLS = 5 * P + KV1 * QD
JOBS = 22


def rope_tables():
    inv = (1.0 / 10000.0 ** (np.arange(0, QD, 2, dtype=np.float32) / np.float32(QD))).astype(np.float32)
    angle = (np.arange(S, dtype=np.float32)[:, None] * inv[None, :]).astype(np.float32)
    angle = np.concatenate([angle, angle], -1).T
    cos, sin = np.cos(angle).astype(np.float32), np.sin(angle).astype(np.float32)
    sin[:QD // 2] *= -1.0
    cos, sin = np.tile(cos, (P // QD, 1)), np.tile(sin, (P // QD, 1))
    k_table = np.concatenate([cos[:P // 2], sin[:P // 2]])
    return np.ascontiguousarray(np.stack([-0.25 * cos, -0.25 * sin, k_table], 1).astype(np.float32))


def spread_tables():
    table = np.zeros((P, 3, 4, P), np.float32)
    for n in range(4):
        for r in range(P):
            e, c, d = r // 64, r % 64 // QD, r % QD
            table[(2 * n + e) * QD + d, c // 2, n, r] = 1.0
            table[(c % 2) * 64 + n * QD + d, 2, n, r] = 1.0
    return table


def attention_phase(nc, w_proj, w_out, g1, ropes, spreads, ident, y, r1):
    with ExitStack() as ctx:
        sb, ps, sem = hold(ctx, nc)
        wp = sb("aa_wp", [P, KT, PROJ_COLS])
        wo = sb("aa_wo", [P, KV1, D])
        g1_sb = sb("aa_g1", [P, KT])
        rope = sb("aa_rope", [P, 3, S])
        spread = sb("aa_spread", [P, 3, 4, P], F32R)
        hidden = sb("aa_hidden", [P, S])
        xr = sb("aa_xr", [P, TT, D])
        xrT = sb("aa_xrT", [P, KT, S])
        turn1 = sb("aa_turn1", [P, 3, S])
        turn2 = sb("aa_turn2", [P, 3, S])
        qh = sb("aa_qh", [P, 2, S], F32R)
        ql = sb("aa_ql", [P, 2, S], F32R)
        kk = sb("aa_kk", [P, S], F32R)
        v = [sb(f"aa_v{i}", [P, TT, KV1, VP]) for i in range(2)]
        q_all = [sb(f"aa_q{i}", [P, QH // 2, S], F32R) for i in range(2)]
        k_all = [sb(f"aa_k{i}", [P, KV1, S], F32R) for i in range(2)]
        p_sb = sb("aa_p", [P, RING * REP, S])
        pT = sb("aa_pT", [P, 2 * REP, S])
        oT = sb("aa_oT", [P, KV1, S])
        nmax = sb("aa_nmax", [P, RING * REP])
        total = sb("aa_total", [P, RING * REP])
        recip = sb("aa_recip", [P, RING * REP])

        s_ps = [ps(f"aa_s_ps{i}") for i in range(2)]
        t_ps = [ps(f"aa_t_ps{i}") for i in range(2)]
        o_ps = [ps(f"aa_o_ps{i}") for i in range(2)]
        m_ps = [ps(f"aa_m_ps{i}") for i in range(2)]

        loaded = sem("aa_loaded")
        consts = sem("aa_consts")
        xr_made = sem("aa_xr_made")
        made = sem("aa_made")
        dve_out = sem("aa_dve_out")
        act_out = sem("aa_act_out")
        roped = sem("aa_roped")
        k_low = sem("aa_k_low")
        scored = sem("aa_scored")
        masked = sem("aa_masked")
        exped = sem("aa_exped")
        recips = sem("aa_recips")
        scaled = sem("aa_scaled")
        turned = sem("aa_turned")
        out_a = sem("aa_out_a")
        out_d = sem("aa_out_d")
        weighed = sem("aa_weighed")
        o_out = sem("aa_o_out")
        zeroed = sem("aa_zeroed")
        dve_ticks, pool_ticks = sem("aa_dve_ticks"), sem("aa_pool_ticks")
        act_ticks, pe_ticks = sem("aa_act_ticks"), sem("aa_pe_ticks")
        block = ctx.enter_context(nc.Block())

        BY_DVE, BY_ACT = 10, JOBS - 10

        def made_count(n, j):
            return n * JOBS + (JOBS - 2 + j + 1)

        def dve_count(n, j):
            return n * BY_DVE + (BY_DVE - 2 + j + 1)

        def act_count(n, j):
            return n * BY_ACT + (BY_ACT + j - BY_DVE + 1)

        @block.sync
        def _(sp):
            for to, src in ((wp, w_proj.rearrange("(k p) n -> p k n", p=P)), (wo, w_out),
                            (rope, ropes), (g1_sb, g1)):
                sp.dma_start(to[:], src).then_inc(loaded, 16)
            sp.dma_start(p_sb[:, 0:3, :], spreads).then_inc(loaded, 16)
            sp.wait_ge(loaded, 80)

        @block.gpsimd
        def _(pool):
            pool.memset(hidden[:], 0.0).then_inc(consts, 1)
            pool.wait_ge(consts, 1)
            pool.affine_select(out=hidden[:], in_=hidden[:], compare_op=ALU.is_ge, fill=BIG, base=S - P,
                               pattern=[[-1, S]], channel_multiplier=1).then_inc(consts, 1)

            def rope_q(n, m):
                wait_alone(pool, dve_out, dve_count(n, 5 + 2 * m), pool_ticks)
                base = (n + 1) * 8 + 3 * m
                pool.tensor_tensor(turn1[:, m, :], turn1[:, m, :], turn2[:, m, :], ALU.add).then_inc(roped, 1)
                wait_alone(pool, roped, base + 1, pool_ticks)
                pool.tensor_scalar(qh[:, m, :], turn1[:, m, :], 1.0, 1.0, ALU.mult, ALU.mult).then_inc(roped, 1)
                wait_alone(pool, roped, base + 2, pool_ticks)
                pool.tensor_tensor(ql[:, m, :], turn1[:, m, :], qh[:, m, :].bitcast(F32), ALU.subtract)\
                    .then_inc(roped, 1)

            def rope_k(n):
                wait_alone(pool, dve_out, dve_count(n, 8), pool_ticks)
                base = (n + 1) * 8 + 6
                low = slice(0, P // 2)
                pool.tensor_tensor(turn1[low, 2, :], turn1[low, 2, :], turn2[low, 2, :], ALU.add).then_inc(roped, 1)
                wait_alone(pool, roped, base + 1, pool_ticks)
                pool.tensor_scalar(kk[low, :], turn1[low, 2, :], 1.0, 1.0, ALU.mult, ALU.mult).then_inc(roped, 1)

            def scale(Q, q):
                wait_alone(pool, recips, Q + 1, pool_ticks)
                N = (q % TT + 1) * P
                for h in range(REP):
                    slot = q % RING * REP + h
                    pool.tensor_scalar(p_sb[:, slot, 0:N], p_sb[:, slot, 0:N], recip[:, slot:slot + 1], 1.0,
                                       ALU.mult, ALU.mult).then_inc(scaled, 1)

            rope_q(-1, 0)
            rope_q(-1, 1)
            rope_k(-1)
            scale(0, 0)
            with pool.Fori(0, B // 2) as pair:
                for par in range(2):
                    b = pair * 2 + par
                    for q in range(QUADS):
                        scale(b * QUADS + (q + 1), q + 1)
                        if q == 3:
                            rope_q(b, 0)
                        if q == 4:
                            rope_q(b, 1)
                        if q == 5:
                            rope_k(b)

        @block.scalar
        def _(act):
            def exps(Q, q):
                N = (q % TT + 1) * P
                for h in range(REP):
                    slot = q % RING * REP + h
                    act.wait_ge(masked, Q * REP + (h + 3))
                    act.activation(p_sb[:, slot, 0:N], p_sb[:, slot, 0:N], ACT.Exp, bias=nmax[:, slot:slot + 1],
                                   scale=-1.0, accum_out=total[:, slot:slot + 1]).then_inc(exped, 1)

            def turn_out(Q, q):
                N = (q % TT + 1) * P
                act.wait_ge(turned, Q * REP + 1)
                act.activation(pT[:, q % 2 * REP, 0:N], t_ps[0][:, 0:N], ACT.Copy).then_inc(out_a, 1)

            def take_spread(n, nxt, j):
                act.wait_ge(made, made_count(n, j))
                to = q_all[nxt][:, j - 10, :] if j < 18 else k_all[nxt][:, j - 18, :]
                act.activation(to, m_ps[j % 2][:], ACT.Copy).then_inc(act_out, 1)

            def take_o(n, g):
                act.wait_ge(weighed, n * QUADS + (g * TT + TT))
                act.activation(oT[:, g, :], o_ps[g % 2][:], ACT.Copy).then_inc(o_out, 1)

            act.sem_inc(o_out, 2)
            for j in range(10, JOBS):
                take_spread(-1, 0, j)
            exps(0, 0)
            exps(1, 1)
            with act.Fori(0, B // 2) as pair:
                for par in range(2):
                    b, nxt = pair * 2 + par, 1 - par
                    for q in range(QUADS):
                        Q = b * QUADS + q
                        turn_out(Q, q)
                        exps(b * QUADS + (q + 2), q + 2)
                        if 7 <= q < 13:
                            take_spread(b, nxt, 2 * q - 4)
                            take_spread(b, nxt, 2 * q - 3)
                        if q % TT == TT - 1:
                            take_o(b, q // TT)

        @block.vector
        def _(dve):
            for i in range(2):
                dve.memset(v[i][:], 0.0)
            dve.memset(oT[:], 0.0).then_inc(zeroed, 1)
            dve.sem_inc(masked, 2)
            dve.wait_ge(consts, 2)
            dve.wait_ge(loaded, 80)
            dve.tensor_copy(spread[:].rearrange("p a b c -> p a (b c)"), p_sb[:, 0:3, :]).then_inc(zeroed, 1)

            def make_xr(n):
                at = (n % B) * TT
                for i in range(TT):
                    dve.tensor_scalar(xr[:, i, :], y[:, ds(at + i, 1), :].rearrange("p a d -> p (a d)"),
                                      r1[:, ds(at + i, 1)], None, ALU.mult).then_inc(xr_made, 1)

            def take_x(n):
                for k in range(KT):
                    dve.wait_ge(made, made_count(n, 2 + k))
                    dve.tensor_scalar(xrT[:, k, :], m_ps[k][:], g1_sb[:, k:k + 1], None, ALU.mult).then_inc(dve_out, 1)

            def take_q(n, m):
                for c, to in enumerate((turn1, turn2)):
                    dve.wait_ge(made, made_count(n, 4 + 2 * m + c))
                    dve.tensor_tensor(to[:, m, :], m_ps[c][:], rope[:, c, :], ALU.mult).then_inc(dve_out, 1)

            def take_k(n):
                dve.wait_ge(made, made_count(n, 8))
                low, high = slice(0, P // 2), slice(P // 2, P)
                dve.tensor_tensor(turn1[low, 2, :], m_ps[0][low, :], rope[low, 2, :], ALU.mult)
                dve.tensor_tensor(turn2[low, 2, :], m_ps[0][high, :], rope[high, 2, :], ALU.mult).then_inc(dve_out, 1)

            def low_k(n):
                dve.wait_ge(roped, (n + 1) * 8 + 8)
                low, high = slice(0, P // 2), slice(P // 2, P)
                dve.tensor_tensor(kk[high, :], turn1[low, 2, :], kk[low, :].bitcast(F32), ALU.subtract)\
                    .then_inc(k_low, 1)

            def take_v(n, nxt):
                dve.wait_ge(made, made_count(n, 9))
                dve.tensor_copy(v[nxt][:, :, :, 0:QD], m_ps[1][:, 0:TT * KV1 * QD]
                                .rearrange("p (i g d) -> p i g d", g=KV1, d=QD)).then_inc(dve_out, 1)

            def take_out(count, bank_at, rows):
                for half in range(2):
                    dve.wait_ge(made, count + half)
                    at = y[:, ds(rows + 2 * half, 2), :].rearrange("p i d -> p (i d)")
                    dve.tensor_tensor(at, m_ps[half][:], at, ALU.add).then_inc(dve_out, 1)

            def mask(Q, q, h):
                N = (q % TT + 1) * P
                slot = q % RING * REP + h
                wait_alone(dve, scored, Q * REP + (h + 1), dve_ticks)
                dve.tensor_tensor_reduce(out=p_sb[:, slot, 0:N], in0=s_ps[h % 2][:, 0:N], in1=hidden[:, S - N:S],
                                         scale=1.0, scalar=BIG, op0=ALU.add, op1=ALU.min,
                                         accum_out=nmax[:, slot:slot + 1]).then_inc(masked, 1)

            def invert(Q, q):
                dve.wait_ge(exped, Q * REP + REP)
                at = slice(q % RING * REP, q % RING * REP + REP)
                dve.reciprocal(recip[:, at], total[:, at]).then_inc(recips, 1)

            def turn_out(Q, q, h):
                N = (q % TT + 1) * P
                dve.wait_ge(turned, Q * REP + (h + 1))
                dve.tensor_copy(pT[:, q % 2 * REP + h, 0:N], t_ps[h % 2][:, 0:N]).then_inc(out_d, 1)

            make_xr(0)
            take_x(-1)
            take_q(-1, 0)
            take_q(-1, 1)
            take_k(-1)
            low_k(-1)
            take_v(-1, 0)
            for q in range(2):
                for h in range(REP):
                    mask(q, q, h)
            invert(0, 0)
            with dve.Fori(0, B // 2) as pair:
                for par in range(2):
                    b, nxt = pair * 2 + par, 1 - par
                    for q in range(QUADS):
                        Q = b * QUADS + q
                        invert(b * QUADS + (q + 1), q + 1)
                        for h in range(REP):
                            mask(b * QUADS + (q + 2), q + 2, h)
                            if h > 0:
                                turn_out(Q, q, h)
                        if q == 0:
                            make_xr(b + 1)
                        if q == 1:
                            take_out(made_count(b, 0), 0, ((b + (B - 1)) % B) * TT)
                        if q == 2:
                            take_x(b)
                        if q == 3:
                            take_q(b, 0)
                        if q == 4:
                            take_q(b, 1)
                        if q == 5:
                            take_k(b)
                            take_v(b, nxt)
                        if q == 6:
                            low_k(b)
            take_out(made_count(B, 0), 0, (B - 1) * TT)

        @block.tensor
        def _(pe):
            def bank_free(n, j):
                last = j - 2 if j >= 2 else JOBS - 2 + j
                before = n if j >= 2 else n + (-1)
                if last < 10:
                    wait_alone(pe, dve_out, dve_count(before, last), pe_ticks)
                else:
                    wait_alone(pe, act_out, act_count(before, last), pe_ticks)

            def turn_x(n, first=False):
                wait_alone(pe, xr_made, (n + 1) * TT + TT, pe_ticks)
                for k in range(KT):
                    if not first:
                        bank_free(n, 2 + k)
                    for i in range(TT):
                        ins = pe.transpose(m_ps[k][:, P * i:P * i + P], xr[:, i, P * k:P * k + P], ident[:])
                    ins.then_inc(made, 1)

            def project(n, j, name):
                bank_free(n, j)
                for k in range(KT):
                    ins = pe.matmul(m_ps[j % 2][:], wp[:, k, PROJ[name]:PROJ[name] + P], xrT[:, k, :],
                                    start=(k == 0), stop=(k == KT - 1))
                ins.then_inc(made, 1)

            def project_q(n, m):
                if m == 0:
                    wait_alone(pe, dve_out, dve_count(n, 3), pe_ticks)
                project(n, 4 + 2 * m, f"q{m}")
                project(n, 5 + 2 * m, f"s{m}")

            def project_kv(n):
                project(n, 8, "kk")
                bank_free(n, 9)
                W = KV1 * QD
                for i in range(TT):
                    for k in range(KT):
                        ins = pe.matmul(m_ps[1][:, i * W:i * W + W], xrT[:, k, i * P:i * P + P],
                                        wp[:, k, PROJ["v"]:PROJ["v"] + W], start=(k == 0), stop=(k == KT - 1))
                ins.then_inc(made, 1)

            def spread_parts(n, j):
                bank_free(n, j)
                bank = m_ps[j % 2]
                if j == 10:
                    wait_alone(pe, roped, (n + 1) * 8 + 6, pe_ticks)
                if j == 18:
                    wait_alone(pe, k_low, n + 2, pe_ticks)
                if j < 18:
                    m, pair_of = divmod(j - 10, 4)
                    pe.matmul(bank[:], spread[:, 0, pair_of, :], qh[:, m, :], start=True, stop=False)
                    pe.matmul(bank[:], spread[:, 1, pair_of, :], ql[:, m, :], start=False, stop=True).then_inc(made, 1)
                else:
                    pe.matmul(bank[:], spread[:, 2, j - 18, :], kk[:], start=True, stop=True).then_inc(made, 1)

            def score(Q, q, par, h):
                g, N = q // TT, (q % TT + 1) * P
                head = g * REP + h
                row = slice(64 * (head % 2), 64 * (head % 2) + 64)
                wait_alone(pe, masked, Q * REP + (h + 1), pe_ticks)
                pe.matmul(s_ps[h % 2][:, 0:N], q_all[par][row, head // 2, N - P:N], k_all[par][row, g, 0:N],
                          start=True, stop=True).then_inc(scored, 1)

            def turn(Q, q, h):
                pe.wait_ge(scaled, Q * REP + (h + 1))
                if h == 2:
                    pe.wait_ge(out_a, Q + 1)
                if h == 3:
                    pe.wait_ge(out_d, Q * (REP - 1) + 1)
                slot = q % RING * REP + h
                for k in range(q % TT + 1):
                    ins = pe.transpose(t_ps[h % 2][:, k * P:k * P + P], p_sb[:, slot, k * P:k * P + P], ident[:])
                ins.then_inc(turned, 1)

            def weigh(Q, q, par):
                g, i = divmod(q, TT)
                wait_alone(pe, out_a, Q + 1, pe_ticks)
                wait_alone(pe, out_d, Q * (REP - 1) + (REP - 1), pe_ticks)
                for k in range(i + 1):
                    for h in range(REP):
                        ins = pe.matmul(o_ps[g % 2][VP * h:VP * h + VP, i * P:i * P + P], v[par][:, k, g, :],
                                        pT[:, q % 2 * REP + h, k * P:k * P + P], start=(k == 0), stop=(k == i))
                ins.then_inc(weighed, 1)

            def project_out(n, last=False):
                for half in range(2):
                    bank_free(n, half)
                    for i in range(2):
                        for g in range(KV1):
                            at = (2 * half + i) * P
                            ins = pe.matmul(m_ps[half][:, i * D:i * D + D], oT[:, g, at:at + P], wo[:, g, :],
                                            start=(g == 0), stop=(g == KV1 - 1))
                    ins.then_inc(made, 1)

            pe.wait_ge(loaded, 80)
            pe.wait_ge(zeroed, 2)
            turn_x(-1, first=True)
            project_q(-1, 0)
            project_q(-1, 1)
            project_kv(-1)
            for j in range(10, JOBS):
                spread_parts(-1, j)
            pe.wait_ge(act_out, BY_ACT)
            for q in range(2):
                for h in range(REP):
                    score(q, q, 0, h)
            with pe.Fori(0, B // 2) as pair:
                for par in range(2):
                    b, nxt = pair * 2 + par, 1 - par
                    for q in range(QUADS):
                        Q = b * QUADS + q
                        ahead = q + 2
                        if ahead == QUADS:
                            wait_alone(pe, act_out, act_count(b, JOBS - 1), pe_ticks)
                        for h in range(REP):
                            score(b * QUADS + ahead, ahead % QUADS, nxt if ahead >= QUADS else par, h)
                            turn(Q, q, h)
                        if q == 1:
                            wait_alone(pe, o_out, b * KV1 + 2, pe_ticks)
                            project_out(b)
                        if q == 2:
                            turn_x(b)
                        if q == 3:
                            project_q(b, 0)
                        if q == 4:
                            project_q(b, 1)
                        if q == 5:
                            project_kv(b)
                        if 7 <= q < 13:
                            spread_parts(b, 2 * q - 4)
                            spread_parts(b, 2 * q - 3)
                        if q % TT == 0:
                            wait_alone(pe, o_out, b * KV1 + (q // TT + 1), pe_ticks)
                        weigh(Q, q, par)
            pe.wait_ge(o_out, B * KV1 + 2)
            project_out(B)


E1 = 4
H1 = 3 * D
M1 = H1 // P
RING1 = 3


def routing_phase(nc, g2, gate, ident, y, yh, yl, comb):
    with ExitStack() as ctx:
        sb, ps, sem = hold(ctx, nc)
        squares = sb("rt_squares", [P, TT, D])
        sq_sum = sb("rt_sq_sum", [P, TT])
        rms = sb("rt_rms", [P, TT])
        r2 = sb("rt_r2", [P, 2, TT])
        eps = sb("rt_eps", [P, 1])
        yr = [sb(f"rt_yr{i}", [P, TT, D]) for i in range(2)]
        yg = [sb(f"rt_yg{i}", [P, KT, S]) for i in range(2)]
        g2_sb = sb("rt_g2", [P, KT])
        gate_sb = sb("rt_gate", [P, KT, E1])
        prob = sb("rt_prob", [P, E1, B * TT])
        rank = sb("rt_rank", [P, E1, B * TT])
        beats = sb("rt_beats", [P, E1 - 1, B * TT])
        top = sb("rt_top", [P, B * TT])
        y_ps = [[ps(f"rt_y_ps{i}{k}") for k in range(KT)] for i in range(2)]
        l_ps = [ps(f"rt_l_ps{i}") for i in range(2)]

        loaded = sem("rt_loaded")
        squared = sem("rt_squared")
        rooted = sem("rt_rooted")
        inverted = sem("rt_inverted")
        normed = sem("rt_normed")
        turned = sem("rt_turned")
        gained = sem("rt_gained")
        high = sem("rt_high")
        low = sem("rt_low")
        voted = sem("rt_voted")
        vote_out = sem("rt_vote_out")
        chain = sem("rt_chain")
        exped = sem("rt_exped")
        dve_ticks = sem("rt_dve_ticks")
        block = ctx.enter_context(nc.Block())

        @block.sync
        def _(sp):
            sp.dma_start(g2_sb[:], g2).then_inc(loaded, 16)
            sp.dma_start(gate_sb[:], gate.rearrange("(k p) e -> p k e", p=P)).then_inc(loaded, 16)
            sp.wait_ge(loaded, 32)

        @block.scalar
        def _(act):
            def root(n):
                for i in range(TT):
                    act.activation(squares[:, i, :], y[:, ds((n % B) * TT + i, 1), :].rearrange("p a d -> p (a d)"),
                                   ACT.Square, accum_out=sq_sum[:, i:i + 1]).then_inc(squared, 1)
                act.wait_ge(squared, n * TT + TT)
                act.activation(rms[:], sq_sum[:], ACT.Sqrt, scale=1.0 / D, bias=eps[:, 0:1]).then_inc(rooted, 1)

            act.wait_ge(chain, 1)
            act.wait_ge(loaded, 32)
            root(0)
            with act.Fori(0, B // 2) as pair:
                for par in range(2):
                    b = pair * 2 + par
                    act.wait_ge(inverted, b + 1)
                    root(b + 1)
                    act.wait_ge(turned, b + 1)
                    for k in range(KT):
                        act.activation(yg[par][:, k, :], y_ps[par][k][:], ACT.Copy, scale=g2_sb[:, k:k + 1])\
                            .then_inc(gained, 1)
                    act.wait_ge(gained, b * KT + KT)
                    act.activation(yh[:, :, ds(b * S, S)], yg[par][:], ACT.Copy).then_inc(high, 1)
            act.wait_ge(chain, 3)
            act.activation(prob[:], prob[:], ACT.Exp).then_inc(exped, 1)

        @block.vector
        def _(dve):
            dve.memset(eps[:], EPS_RMS).then_inc(chain, 1)

            def norm(n, par):
                dve.wait_ge(rooted, n + 1)
                dve.reciprocal(r2[:, par, :], rms[:]).then_inc(inverted, 1)
                wait_alone(dve, inverted, n + 1, dve_ticks)
                for i in range(TT):
                    dve.tensor_scalar(yr[par][:, i, :], y[:, ds((n % B) * TT + i, 1), :].rearrange("p a d -> p (a d)"),
                                      r2[:, par, i:i + 1], None, ALU.mult).then_inc(normed, 1)

            norm(0, 0)
            with dve.Fori(0, B // 2) as pair:
                for par in range(2):
                    b = pair * 2 + par
                    norm(b + 1, 1 - par)
                    dve.wait_ge(high, b + 1)
                    at = ds(b * S, S)
                    dve.tensor_tensor(yl[:, :, at], yg[par][:], yh[:, :, at].bitcast(F32), ALU.subtract).then_inc(low, 1)
                    dve.wait_ge(voted, b + 1)
                    dve.tensor_copy(prob[:, :, ds(b * TT, TT)].rearrange("p e i -> p i e"),
                                    l_ps[par][:, 0:TT * E1].rearrange("p (i e) -> p i e", e=E1)).then_inc(vote_out, 1)

            count = [1]

            def link(ins):
                count[0] += 1
                ins.then_inc(chain, 1)
                dve.wait_ge(chain, count[0])

            def over_experts(tile):
                return tile[:].rearrange("p e t -> p t e")

            def each_expert(tile):
                return tile[:].rearrange("p (a t) -> p a t", a=1).broadcast_to([P, E1, B * TT])

            dve.wait_ge(vote_out, B)
            link(dve.tensor_reduce(top[:], over_experts(prob), AX.X, ALU.max))
            link(dve.tensor_tensor(prob[:], prob[:], each_expert(top), ALU.subtract))
            dve.wait_ge(exped, 1)
            link(dve.tensor_reduce(top[:], over_experts(prob), AX.X, ALU.add))
            link(dve.reciprocal(top[:], top[:]))
            link(dve.tensor_tensor(prob[:], prob[:], each_expert(top), ALU.mult))
            link(dve.memset(rank[:], 0.0))
            for d in range(1, E1):
                n = E1 - d
                link(dve.tensor_tensor(beats[:, 0:n, :], prob[:, 0:n, :], prob[:, d:E1, :], ALU.is_ge))
                link(dve.tensor_tensor(rank[:, d:E1, :], rank[:, d:E1, :], beats[:, 0:n, :], ALU.add))
                link(dve.tensor_scalar(beats[:, 0:n, :], beats[:, 0:n, :], -1.0, 1.0, ALU.mult, ALU.add))
                link(dve.tensor_tensor(rank[:, 0:n, :], rank[:, 0:n, :], beats[:, 0:n, :], ALU.add))
            link(dve.tensor_scalar(rank[:], rank[:], 1.5, None, ALU.is_lt))
            link(dve.tensor_tensor(prob[:], prob[:], rank[:], ALU.mult))
            link(dve.tensor_reduce(top[:], over_experts(prob), AX.X, ALU.add))
            link(dve.reciprocal(top[:], top[:]))
            link(dve.tensor_tensor(comb[:], prob[:], each_expert(top), ALU.mult))

        @block.tensor
        def _(pe):
            def turn(n, par):
                pe.wait_ge(normed, n * TT + TT)
                for k in range(KT):
                    for i in range(TT):
                        ins = pe.transpose(y_ps[par][k][:, P * i:P * i + P], yr[par][:, i, P * k:P * k + P], ident[:])
                ins.then_inc(turned, 1)

            turn(0, 0)
            with pe.Fori(0, B // 2) as pair:
                for par in range(2):
                    b = pair * 2 + par
                    turn(b + 1, 1 - par)
                    pe.wait_ge(gained, b * KT + KT)
                    for i in range(TT):
                        for k in range(KT):
                            ins = pe.matmul(l_ps[par][:, i * E1:i * E1 + E1], yg[par][:, k, i * P:i * P + P],
                                            gate_sb[:, k, :], start=(k == 0), stop=(k == KT - 1))
                    ins.then_inc(voted, 1)


def expert_phase(nc, w1, w3, w2, y, yh, yl, comb, x1_dram, s_dram, out_dram):
    with ExitStack() as ctx:
        sb, ps, sem = hold(ctx, nc)
        w13_raw = sb("ex_w13_raw", [P, KT, 2, H1])
        w2_raw = sb("ex_w2_raw", [P, M1, D])
        w13h, w13l = (sb(f"ex_w13{x}", [P, KT, 2, H1], F32R) for x in "hl")
        w2h, w2l = (sb(f"ex_w2{x}", [P, M1, D], F32R) for x in "hl")
        act1 = sb("ex_act1", [P, 2, S])
        hid = sb("ex_hid", [P, RING1, S])
        hh, hl = (sb(f"ex_h{x}", [P, RING1, S], F32R) for x in "hl")
        s_in = [sb(f"ex_s{i}", [P, TT, D]) for i in range(2)]
        x_in = [sb(f"ex_x{i}", [P, TT, D]) for i in range(2)]
        z = sb("ex_z", [P, TT, D])
        a_ps = [ps(f"ex_a_ps{i}") for i in range(2)]
        b_ps = [ps(f"ex_b_ps{i}") for i in range(2)]
        o_ps = [[ps(f"ex_o_ps{i}{k}") for k in range(2)] for i in range(2)]

        w_loaded = sem("ex_w_loaded")
        f_loaded = [sem("ex_f_loaded0"), sem("ex_f_loaded1")]
        stored = sem("ex_stored")
        ready = sem("ex_ready")
        unit_done = sem("ex_unit_done")
        silued = sem("ex_silued")
        gated = sem("ex_gated")
        h_high = sem("ex_h_high")
        h_low = sem("ex_h_low")
        w_high = sem("ex_w_high")
        w_low = sem("ex_w_low")
        added = sem("ex_added")
        f_silued = sem("ex_f_silued")
        f_mixed = sem("ex_f_mixed")
        f_added = sem("ex_f_added")
        pool_ticks = sem("ex_pool_ticks")
        dve_ticks = sem("ex_dve_ticks")
        x_view = x1_dram.rearrange("b (i p) d -> b p i d", p=P)
        s_view = s_dram.rearrange("b (i p) d -> b p i d", p=P)
        out_view = out_dram.rearrange("b (i p) d -> b p i d", p=P)
        block = ctx.enter_context(nc.Block())
        LAST = E1 - 1

        def pieces(m):
            c = slice(m * P, m * P + P)
            return ((w13_raw[:, :, :, c], w13h[:, :, :, c], w13l[:, :, :, c]),
                    (w2_raw[:, m, :], w2h[:, m, :], w2l[:, m, :]))

        @block.sync
        def _(sp):
            def load_weights(e):
                for c, w in ((0, w1), (1, w3)):
                    for k in range(KT):
                        sp.dma_start(w13_raw[:, k, c, :], w[ds(e, 1), k * P:k * P + P, :]
                                     .rearrange("e p h -> p (e h)")).then_inc(w_loaded, 16)
                sp.dma_start(w2_raw[:], w2[ds(e, 1)].rearrange("e (m p) d -> p (e m) d", p=P)).then_inc(w_loaded, 16)

            def load_final(b, par):
                sp.dma_start(s_in[par][:], s_view[b]).then_inc(f_loaded[par], 16)
                sp.dma_start(x_in[par][:], x_view[b]).then_inc(f_loaded[par], 16)

            load_weights(0)
            with sp.Fori(0, E1) as e:
                sp.wait_ge(w_low, e * M1 + M1)
                load_weights((e + 1) % E1)
            load_final(0, 0)
            load_final(1, 1)
            for b in range(B):
                sp.wait_ge(f_added, b + 1)
                sp.dma_start(out_view[b], x_in[b % 2][:]).then_inc(stored, 16)
                sp.wait_ge(stored, b * 16 + 16)
                if b + 2 < B:
                    load_final(b + 2, b % 2)
            sp.wait_ge(w_loaded, (2 * KT + 1) * 16 * (E1 + 1))
            sp.wait_ge(stored, 16 * B)

        @block.gpsimd
        def _(pool):
            def split_high(m):
                for raw, high, _ in pieces(m):
                    ins = pool.tensor_scalar(high, raw, 1.0, 1.0, ALU.mult, ALU.mult)
                ins.then_inc(w_high, 1)

            def unit(U, m):
                pool.wait_ge(gated, U + 3)
                wait_alone(pool, unit_done, U + 1, pool_ticks)
                pool.tensor_scalar(hh[:, m % RING1, :], hid[:, m % RING1, :], 1.0, 1.0, ALU.mult, ALU.mult)\
                    .then_inc(h_high, 1)

            pool.wait_ge(w_loaded, (2 * KT + 1) * 16)
            for m in range(M1):
                split_high(m)
            with pool.Fori(0, E1) as e:
                with pool.Fori(0, B - 1) as b:
                    for m in range(M1):
                        unit(e * (B * M1) + b * M1 + m, m)
                for m in range(M1):
                    U = e * (B * M1) + ((B - 1) * M1 + m)
                    unit(U, m)
                    if m == 0:
                        wait_alone(pool, w_loaded, e * ((2 * KT + 1) * 16) + (2 * KT + 1) * 32, pool_ticks)
                    wait_alone(pool, unit_done, U + (RING1 + 1), pool_ticks)
                    split_high(m)

        @block.scalar
        def _(act):
            def unit(U, m):
                act.wait_ge(ready, U + 1)
                act.activation(act1[:, m % 2, :], a_ps[m % 2][:], ACT.Silu).then_inc(silued, 1)

            def final(b):
                act.wait_ge(added, (LAST * B + b + 3) * TT)
                if b > 0:
                    act.wait_ge(f_added, b)
                act.activation(z[:], y[:, b * TT:b * TT + TT, :], ACT.Silu).then_inc(f_silued, 1)

            with act.Fori(0, LAST * B) as eb:
                for m in range(M1):
                    unit(eb * M1 + m, m)
            for b in range(B):
                for m in range(M1):
                    unit((LAST * B + b) * M1 + m, m)
                    if m == 3 and b > 0:
                        final(b - 1)
            final(B - 1)

        @block.vector
        def _(dve):
            dve.sem_inc(gated, 2)
            dve.sem_inc(added, 2 * TT)

            def split_low(count, m):
                dve.wait_ge(w_high, count)
                for raw, high, low in pieces(m):
                    ins = dve.tensor_tensor(low, raw, high.bitcast(F32), ALU.subtract)
                ins.then_inc(w_low, 1)

            def product(U, m):
                dve.wait_ge(silued, U + 1)
                dve.tensor_tensor(hid[:, m % RING1, :], act1[:, m % 2, :], b_ps[m % 2][:], ALU.mult).then_inc(gated, 1)

            def rest(U, m):
                dve.wait_ge(h_high, U + 1)
                dve.tensor_tensor(hl[:, m % RING1, :], hid[:, m % RING1, :], hh[:, m % RING1, :].bitcast(F32),
                                  ALU.subtract).then_inc(h_low, 1)

            def take(U_end, e, b, par):
                dve.wait_ge(unit_done, U_end + RING1)
                for i in range(TT):
                    at = y[:, ds(b * TT + i, 1), :].rearrange("p a d -> p (a d)")
                    dve.scalar_tensor_tensor(out=at, in0=o_ps[par][i // 2][:, i % 2 * D:i % 2 * D + D],
                                             scalar=comb[:, ds(e, 1), ds(b * TT + i, 1)].rearrange("p a c -> p (a c)"),
                                             in1=at, op0=ALU.mult, op1=ALU.add).then_inc(added, 1)

            def final(b):
                dve.wait_ge(f_silued, b + 1)
                dve.wait_ge(f_loaded[b % 2], (b // 2 + 1) * 32)
                dve.tensor_tensor(z[:], z[:], s_in[b % 2][:], ALU.mult).then_inc(f_mixed, 1)
                dve.wait_ge(f_mixed, b + 1)
                dve.tensor_tensor(x_in[b % 2][:], x_in[b % 2][:], z[:], ALU.add).then_inc(f_added, 1)

            def batch(e, b, par, split=False, finals=None):
                U = e * (B * M1) + b * M1
                for m in range(M1):
                    product(U + m, m)
                    if m > 0:
                        rest(U + (m - 1), m - 1)
                    if split and m > 1:
                        split_low(e * M1 + (M1 + m - 1), m - 2)
                    if finals is not None and finals > 0 and m == 4:
                        final(finals - 1)
                rest(U + (M1 - 1), M1 - 1)
                take(U + M1, e, b, par)
                if split:
                    for m in (M1 - 2, M1 - 1):
                        split_low(e * M1 + (M1 + m + 1), m)

            for m in range(M1):
                split_low(m + 1, m)
            with dve.Fori(0, LAST) as e:
                with dve.Fori(0, B // 2 - 1) as pair:
                    for par in range(2):
                        batch(e, pair * 2 + par, par)
                batch(e, B - 2, 0)
                batch(e, B - 1, 1, split=True)
            for b in range(B):
                batch(LAST, b, b % 2, finals=b, split=(b == B - 1))
            final(B - 1)

        @block.tensor
        def _(pe):
            pe.sem_inc(unit_done, RING1)

            def hidden_sums(U, e, b, m):
                pe.wait_ge(w_low, e * M1 + (m + 1))
                pe.wait_ge(gated, U + 1)
                for c, bank in ((0, a_ps[m % 2]), (1, b_ps[m % 2])):
                    for i, (w, x) in enumerate([(w13h, yh), (w13l, yh), (w13h, yl)]):
                        for k in range(KT):
                            ins = pe.matmul(bank[:], w[:, k, c, m * P:m * P + P], x[:, k, ds(b * S, S)],
                                            start=(i == 0 and k == 0), stop=(i == 2 and k == KT - 1))
                ins.then_inc(ready, 1)

            def output_sums(U, m, par):
                pe.wait_ge(h_low, U + 1)
                for t in range(TT):
                    bank = o_ps[par][t // 2][:, t % 2 * D:t % 2 * D + D]
                    for i, (h, w) in enumerate([(hh, w2h), (hl, w2h), (hh, w2l)]):
                        ins = pe.matmul(bank, h[:, m % RING1, t * P:t * P + P], w[:, m, :],
                                        start=(m == 0 and i == 0 and t % 2 == 0),
                                        stop=(m == M1 - 1 and i == 2 and t % 2 == 1))
                ins.then_inc(unit_done, 1)

            def batch(e, b, par, e_next, b_next):
                U = e * (B * M1) + b * M1
                for m in range(M1):
                    if m + 2 < M1:
                        hidden_sums(U + (m + 2), e, b, m + 2)
                    else:
                        hidden_sums(U + (m + 2), e_next, b_next, m + 2 - M1)
                    if m == 0:
                        pe.wait_ge(added, e * (B * TT) + (b * TT + TT))
                    output_sums(U + m, m, par)

            hidden_sums(0, 0, 0, 0)
            hidden_sums(1, 0, 0, 1)
            with pe.Fori(0, E1) as e:
                with pe.Fori(0, B // 2 - 1) as pair:
                    for par in range(2):
                        batch(e, pair * 2 + par, par, e, pair * 2 + (par + 1))
                batch(e, B - 2, 0, e, B - 1)
                batch(e, B - 1, 1, e + 1, 0)


def recurrent_kernel(nc, x, w_heads, wo_heads, slopes, w_gate, b_gate, alpha, w1_all, w2_all, b1_all, b2_all, w_write,
                     w_read, decay, log_alpha, w_proj, w_out, g1, ropes, spreads, g2, gate1, w1, w3, w2, out):
    xh_dram = nc.dram_tensor("xh_dram", [P, KT, T], F32).ap()
    xl_dram = nc.dram_tensor("xl_dram", [P, KT, T], F32).ap()
    rows_dram = nc.dram_tensor("rows_dram", [B, NF], U32).ap()
    coef_dram = nc.dram_tensor("coef_dram", [B, NF], F32).ap()
    x1_dram = nc.dram_tensor("x1_dram", [B, S, D], F32).ap()
    s_dram = nc.dram_tensor("s_dram", [B, S, D], F32).ap()
    with ExitStack() as whole:
        sb, _, _ = hold(whole, nc)
        ident = sb("ident", [P, P])
        with ExitStack() as layer0:
            sb, _, _ = hold(layer0, nc)
            xsum = sb("xsum", [P, KT, B])
            rows = sb("rows", [1, B * NF], U32)
            coef = sb("coef", [P, B * NF])
            acc = sb("acc", [P, KT, T])
            with ExitStack() as mixer:
                sb, _, _ = hold(mixer, nc)
                xh = sb("xh", [P, KT, T], F32R)
                xl = sb("xl", [P, KT, T], F32R)
                layernorm_phase(nc, x, ident, xh, xl, xsum, xh_dram, xl_dram)
                gate_phase(nc, xsum, w_gate, b_gate, alpha, rows_dram, coef_dram, rows, coef)
                head_attention_phase(nc, w_heads, wo_heads, slopes, ident, xh, xl, acc)
            network_phase(nc, x, w1_all, w2_all, b1_all, b2_all, ident, rows, coef, xh_dram, xl_dram, acc, x1_dram)
        with ExitStack() as layer1:
            sb, _, _ = hold(layer1, nc)
            y = sb("y", [P, B * TT, D])
            r1 = sb("r1", [P, B * TT])
            comb = sb("comb", [P, E1, B * TT])
            recurrence_phase(nc, x1_dram, w_write, w_read, decay, log_alpha, ident, y, r1, s_dram)
            attention_phase(nc, w_proj, w_out, g1, ropes, spreads, ident, y, r1)
            yh = sb("yh", [P, KT, T], F32R)
            yl = sb("yl", [P, KT, T], F32R)
            routing_phase(nc, g2, gate1, ident, y, yh, yl, comb)
            expert_phase(nc, w1, w3, w2, y, yh, yl, comb, x1_dram, s_dram, out)


def lay_out(inputs):
    a = {name: np.ascontiguousarray(value) for name, value in inputs.items()}

    def join(parts, axis=0):
        return np.ascontiguousarray(np.concatenate(parts, axis))

    def by_partition(vector):
        return np.ascontiguousarray(np.moveaxis(vector.reshape(*vector.shape[:-1], -1, P), -2, -1))

    def halves_exchanged(w):
        return w.reshape(D, -1, 2, QD // 2)[:, :, ::-1].reshape(D, -1)

    w_qkv, n_q, n_kv = a["L0_attn_W_qkv"], 2 * KVH * HD, KVH * HD
    heads = [w_qkv[:, lo:hi].reshape(KT, P, KVH, -1) for lo, hi in
             ((0, n_q), (n_q, n_q + n_kv), (n_q + n_kv, n_q + 2 * n_kv))]
    slopes = (2.0 ** (-2.0 ** (-(np.log2(2 * KVH) - 3)))) ** np.arange(1, 2 * KVH + 1, dtype=np.float32)
    wq, wk, wv = a["L1_ffn_wq"], a["L1_ffn_wk"], a["L1_ffn_wv"]
    wo = np.zeros((REP, VP, KV1, D), np.float32)
    wo[:, :QD] = a["L1_ffn_wo"].reshape(KV1, REP, QD, D).transpose(1, 2, 0, 3)
    return {
        "x": a["L0_attn_inputs"],
        "w_heads": np.ascontiguousarray(join(heads, 3).transpose(2, 1, 0, 3)),
        "wo_heads": a["L0_attn_W_out"].reshape(KVH, P, D),
        "slopes": np.tile(slopes.astype(np.float32), (P, 1)),
        "w_gate": a["L0_ffn_w_gate"],
        "b_gate": a["L0_ffn_b_gate"],
        "alpha": a["L0_ffn_alpha"].reshape(1, 1),
        "w1_all": join([a["L0_ffn_W1m"][None], a["L0_ffn_W1e"]]),
        "w2_all": join([a["L0_ffn_W2m"][None], a["L0_ffn_W2e"]]),
        "b1_all": by_partition(join([a["L0_ffn_b1m"][None], a["L0_ffn_b1e"]])),
        "b2_all": by_partition(join([a["L0_ffn_b2m"][None], a["L0_ffn_b2e"]])),
        "w_write": np.ascontiguousarray(a["L1_attn_W_write"].T),
        "w_read": np.ascontiguousarray(a["L1_attn_W_read"].T),
        "decay": a["L1_attn_decay"],
        "log_alpha": a["L1_attn_log_alpha"],
        "w_proj": join([wq, halves_exchanged(wq), wk, halves_exchanged(wk), wv], 1),
        "w_out": wo.reshape(P, KV1, D),
        "g1": by_partition(a["L1_ffn_g1"]),
        "ropes": rope_tables(),
        "spreads": spread_tables(),
        "g2": by_partition(a["L1_ffn_g2"]),
        "gate1": a["L1_ffn_gate"],
        "w1": a["L1_ffn_w1"],
        "w3": a["L1_ffn_w3"],
        "w2": a["L1_ffn_w2"],
    }


def kernel(**inputs):
    import concourse.bacc as _bacc
    from concourse.bass_utils import run_bass_kernel_spmd as _run

    nc = _bacc.Bacc("TRN2", target_bir_lowering=False, num_devices=1)
    arrays, args = {}, []
    for name, a in lay_out(inputs).items():
        arrays[f"in_{name}_dram"] = a
        args.append(nc.dram_tensor(f"in_{name}_dram", a.shape, mybir.dt.from_np(a.dtype), kind="ExternalInput").ap())
    args.append(nc.dram_tensor("out_0_dram", (B, S, D), F32, kind="ExternalOutput").ap())
    recurrent_kernel(nc, *args)
    r = _run(nc, [arrays], core_ids=[0])
    return r.results[0]["out_0_dram"]
```

```python
from contextlib import ExitStack

import concourse.bass as bass
import numpy as np
from concourse import mybir

F32 = mybir.dt.float32
F32R = mybir.dt.float32r
U32 = mybir.dt.uint32
ALU = mybir.AluOpType
ACT = mybir.ActivationFunctionType
AX = mybir.AxisListType
ds = bass.ds

P = 128
B, S, D = 8, 512, 256
KT = D // P
TT = S // P
T = B * S
EPS_LN = 1e-5
BIG = 1e30

KVH = 16
HD = 64


def hold(ctx, nc):
    def sb(name, shape, dt=F32):
        return ctx.enter_context(nc.sbuf_tensor(name, shape, dt))

    def ps(name, shape=(P, 512)):
        return ctx.enter_context(nc.psum_tensor(name, list(shape), F32))

    def sem(name):
        return ctx.enter_context(nc.semaphore(name))

    return sb, ps, sem


def wait_alone(engine, semaphore, value, ticks):
    engine.wait_ge(semaphore, value)
    engine.sem_inc(ticks, 1)


def layernorm_phase(nc, x_dram, ident, xh, xl, xsum, xh_dram, xl_dram):
    with ExitStack() as ctx:
        sb, ps, sem = hold(ctx, nc)
        x_in = [sb(f"ln_x{i}", [P, TT, D]) for i in range(2)]
        stats = sb("ln_stats", [P, TT, 6])
        mv = sb("ln_mv", [P, TT, 2])
        std = sb("ln_std", [P, TT])
        rstd = sb("ln_rstd", [P, TT])
        eps = sb("ln_eps", [P, 1])
        carry = sb("ln_carry", [P, 1])
        xT_ps = [[ps(f"ln_ps{i}{k}") for k in range(KT)] for i in range(2)]
        x_loaded = [sem("ln_x_loaded0"), sem("ln_x_loaded1")]
        id_done = sem("ln_id_done")
        eps_done = sem("ln_eps_done")
        stats_done = sem("ln_stats_done")
        var_done = sem("ln_var_done")
        std_done = sem("ln_std_done")
        rstd_done = sem("ln_rstd_done")
        normed = sem("ln_normed")
        turned = sem("ln_turned")
        high = sem("ln_high")
        low = sem("ln_low")
        spilled = sem("ln_spilled")
        x_view = x_dram.rearrange("b (i p) d -> b p i d", p=P)
        block = ctx.enter_context(nc.Block())

        @block.sync
        def _(sp):
            for par in range(2):
                sp.dma_start(x_in[par][:], x_view[par]).then_inc(x_loaded[par], 16)
            with sp.Fori(0, B // 2) as pair:
                for par in range(2):
                    sp.wait_ge(turned, (pair * 2 + par) + 1)
                    sp.dma_start(x_in[par][:], x_view[ds((pair * 2 + (par + 2)) % B, 1)]
                                 .rearrange("b p i d -> p (b i) d")).then_inc(x_loaded[par], 16)
                    sp.wait_ge(low, (pair * 2 + par) + 1)
                    sp.wait_ge(high, (pair * 2 + par) * KT + KT)
                    at = (pair * 2 + par) * S
                    sp.dma_start(xh_dram[:, :, ds(at, S)], xh[:, :, ds(at, S)].bitcast(F32)).then_inc(spilled, 16)
                    sp.dma_start(xl_dram[:, :, ds(at, S)], xl[:, :, ds(at, S)].bitcast(F32)).then_inc(spilled, 16)
            for par in range(2):
                sp.wait_ge(x_loaded[par], 16 * (B // 2 + 1))
            sp.wait_ge(spilled, 32 * B)

        @block.gpsimd
        def _(pool):
            pool.memset(ident[:], 0.0).then_inc(id_done, 1)
            pool.wait_ge(id_done, 1)
            pool.affine_select(out=ident[:], in_=ident[:], compare_op=ALU.not_equal, fill=1.0, base=0,
                               pattern=[[-1, P]], channel_multiplier=1).then_inc(id_done, 1)

        @block.vector
        def _(dve):
            dve.memset(eps[:], EPS_LN).then_inc(eps_done, 1)

            def norm(n, pair_n, par):
                dve.wait_ge(x_loaded[par], pair_n * 16 + 16)
                for i in range(TT):
                    dve.bn_stats(stats[:, i, :], x_in[par][:, i, :]).then_inc(stats_done, 1)
                dve.wait_ge(stats_done, n * TT + TT)
                dve.memset(carry[:], 0.0)
                for i in range(TT):
                    dve.bn_aggr(mv[:, i, :], stats[:, i, :]).then_inc(var_done, 1)
                dve.wait_ge(std_done, n + 1)
                dve.reciprocal(rstd[:], std[:]).then_inc(rstd_done, 1)
                dve.wait_ge(rstd_done, n + 1)
                for i in range(TT):
                    dve.tensor_scalar(x_in[par][:, i, :], x_in[par][:, i, :], mv[:, i, 0:1], rstd[:, i:i + 1],
                                      ALU.subtract, ALU.mult).then_inc(normed, 1)

            norm(0, 0, 0)
            with dve.Fori(0, B // 2) as pair:
                for par in range(2):
                    n = pair * 2 + par
                    norm(n + 1, pair + par, 1 - par)
                    dve.wait_ge(high, n * KT + KT)
                    at = n * S
                    for k in range(KT):
                        ins = dve.tensor_tensor(xl[:, k, ds(at, S)], xT_ps[par][k][:], xh[:, k, ds(at, S)].bitcast(F32),
                                                ALU.subtract)
                    ins.then_inc(low, 1)

        @block.scalar
        def _(act):
            act.wait_ge(eps_done, 1)

            def root(n):
                act.wait_ge(var_done, n * TT + TT)
                act.activation(std[:], mv[:, :, 1], ACT.Sqrt, bias=eps[:, 0:1]).then_inc(std_done, 1)

            root(0)
            with act.Fori(0, B // 2) as pair:
                for par in range(2):
                    n = pair * 2 + par
                    root(n + 1)
                    act.wait_ge(turned, n + 1)
                    for k in range(KT):
                        act.activation(xh[:, k, ds(n * S, S)], xT_ps[par][k][:], ACT.Copy,
                                       accum_out=xsum[:, k, ds(n, 1)]).then_inc(high, 1)

        @block.tensor
        def _(pe):
            pe.wait_ge(id_done, 2)
            with pe.Fori(0, B // 2) as pair:
                for par in range(2):
                    n = pair * 2 + par
                    pe.wait_ge(normed, n * TT + TT)
                    for k in range(KT):
                        for i in range(TT):
                            ins = pe.transpose(xT_ps[par][k][:, P * i:P * i + P], x_in[par][:, i, P * k:P * k + P], ident[:])
                    ins.then_inc(turned, 1)


E0 = 8
TOP = 2
HID = 1024
MT = HID // P
SLOTS = 3
NF = 1 + TOP


def gate_phase(nc, xsum, w_gate, b_gate, alpha, rows_dram, coef_dram, rows, coef, acc):
    with ExitStack() as ctx:
        sb, ps, sem = hold(ctx, nc)
        wg = sb("gt_wg", [P, KT, E0])
        bg = sb("gt_bg", [B, E0])
        al = sb("gt_alpha", [B, 1])
        logits = sb("gt_logits", [B, E0])
        top = sb("gt_top", [B, 8])
        at = sb("gt_at", [B, 8], U32)
        tiny = sb("gt_tiny", [B, 8])
        row_sb = sb("gt_row", [B, NF], U32)
        row_f = sb("gt_row_f", [B, NF])
        coef_sb = sb("gt_coef", [B, NF])
        l_ps = ps("gt_ps")
        loaded = sem("gt_loaded")
        chain = sem("gt_chain")
        cleared = sem("gt_cleared")
        exped = sem("gt_exped")
        ready = sem("gt_ready")
        spilled = sem("gt_spilled")
        back = sem("gt_back")
        block = ctx.enter_context(nc.Block())

        @block.sync
        def _(sp):
            sp.dma_start(wg[:], w_gate.rearrange("(k p) e -> p k e", p=P)).then_inc(loaded, 16)
            sp.dma_start(bg[:], b_gate.rearrange("(a e) -> a e", a=1).broadcast_to([B, E0])).then_inc(loaded, 16)
            sp.dma_start(al[:], alpha.broadcast_to([B, 1])).then_inc(loaded, 16)
            sp.wait_ge(chain, 12)
            sp.dma_start(rows_dram, row_sb[:]).then_inc(spilled, 16)
            sp.dma_start(coef_dram, coef_sb[:]).then_inc(spilled, 16)
            sp.wait_ge(spilled, 32)
            sp.dma_start(rows[:], rows_dram.rearrange("(a b) f -> a (b f)", a=1)).then_inc(back, 16)
            sp.dma_start(coef[:], coef_dram.rearrange("(a b) f -> a (b f)", a=1).broadcast_to([P, B * NF]))\
                .then_inc(back, 16)
            sp.wait_ge(back, 32)

        @block.gpsimd
        def _(pool):
            pool.memset(acc[:], 0.0).then_inc(cleared, 1)
            pool.wait_ge(cleared, 1)

        @block.tensor
        def _(pe):
            pe.wait_ge(loaded, 48)
            for k in range(KT):
                ins = pe.matmul(l_ps[0:B, 0:E0], xsum[:, k, :], wg[:, k, :], start=(k == 0), stop=(k == KT - 1))
            ins.then_inc(ready, 1)

        @block.scalar
        def _(act):
            act.wait_ge(chain, 2)
            act.activation(logits[:], logits[:], ACT.Exp, bias=tiny[:, 0:1], accum_out=tiny[:, 1:2])\
                .then_inc(exped, 1)

        @block.vector
        def _(dve):
            count = [0]

            def link(ins):
                count[0] += 1
                ins.then_inc(chain, 1)
                dve.wait_ge(chain, count[0])

            dve.wait_ge(ready, 1)
            link(dve.scalar_tensor_tensor(out=logits[:], in0=l_ps[0:B, 0:E0], scalar=1.0 / S, in1=bg[:],
                                          op0=ALU.mult, op1=ALU.add))
            link(dve.tensor_reduce(tiny[:, 0:1], logits[:], AX.X, ALU.max, negate=True))
            dve.wait_ge(exped, 1)
            link(dve.reciprocal(tiny[:, 2:3], tiny[:, 1:2]))
            link(dve.tensor_scalar(logits[:], logits[:], tiny[:, 2:3], None, ALU.mult))
            link(dve.max(top[:], logits[:]))
            link(dve.max_index(at[:], top[:], logits[:]))
            link(dve.tensor_tensor(tiny[:, 3:4], top[:, 0:1], top[:, 1:2], ALU.add))
            link(dve.reciprocal(tiny[:, 4:5], tiny[:, 3:4]))
            link(dve.tensor_scalar(coef_sb[:, 0:1], al[:], 0.1, 1.0, ALU.max, ALU.min))
            link(dve.tensor_scalar(tiny[:, 5:6], coef_sb[:, 0:1], -1.0, 1.0, ALU.mult, ALU.add))
            link(dve.tensor_scalar(coef_sb[:, 1:NF], top[:, 0:TOP], tiny[:, 4:5], tiny[:, 5:6], ALU.mult, ALU.mult))
            dve.memset(row_sb[:, 0:1], 0)
            link(dve.tensor_scalar(row_sb[:, 1:NF], at[:, 0:TOP], 1.0, None, ALU.add))


def network_phase(nc, x_dram, w1_all, w2_all, b1_all, b2_all, ident, rows, coef, xh_dram, xl_dram, acc, x1_dram):
    R = B * NF
    with ExitStack() as ctx:
        sb, ps, sem = hold(ctx, nc)
        w1_raw = [sb(f"nw_w1_raw{i}", [P, KT, HID]) for i in range(2)]
        w2_raw = [sb(f"nw_w2_raw{i}", [P, MT, D]) for i in range(2)]
        b1 = [sb(f"nw_b1_{i}", [P, MT]) for i in range(2)]
        b2 = [sb(f"nw_b2_{i}", [P, KT]) for i in range(2)]
        w1h, w1l = ([sb(f"nw_w1{x}{i}", [P, KT, HID], F32R) for i in range(2)] for x in "hl")
        w2h, w2l = ([sb(f"nw_w2{x}{i}", [P, MT, D], F32R) for i in range(2)] for x in "hl")
        xh, xl = ([sb(f"nw_x{x}{i}", [P, KT, S], F32R) for i in range(2)] for x in "hl")
        x_raw = sb("nw_x_raw", [P, 2, KT, S])
        hidden = sb("nw_h", [P, SLOTS, S])
        hh, hl = (sb(f"nw_h{x}", [P, SLOTS, S], F32R) for x in "hl")
        coef_now = sb("nw_coef_now", [P, 2])
        bsum = sb("nw_bsum", [P, 2, KT])
        zT = sb("nw_zT", [P, KT, S])
        x_nat = sb("nw_x", [P, TT, D])
        h_ps = [ps(f"nw_h_ps{i}") for i in range(SLOTS)]
        o_ps = [[ps(f"nw_o_ps{i}{k}") for k in range(KT)] for i in range(2)]
        z_ps = ps("nw_z_ps")

        raw_loaded = [sem("nw_raw_loaded0"), sem("nw_raw_loaded1")]
        x_loaded = sem("nw_x_loaded")
        x_placed = sem("nw_x_placed")
        nat_loaded = sem("nw_nat_loaded")
        stored = sem("nw_stored")
        hid_ready = sem("nw_hid_ready")
        unit_done = sem("nw_unit_done")
        z_turned = sem("nw_z_turned")
        gelued = sem("nw_gelued")
        gated = sem("nw_gated")
        h_high = sem("nw_h_high")
        w_high = sem("nw_w_high")
        h_low = sem("nw_h_low")
        w_low = sem("nw_w_low")
        b_sum = sem("nw_b_sum")
        mixed = sem("nw_mixed")
        added = sem("nw_added")
        coef_set = sem("nw_coef_set")
        pool_ticks, sp_ticks = sem("nw_pool_ticks"), sem("nw_sp_ticks")
        x_view = x_dram.rearrange("b (i p) d -> b p i d", p=P)
        x1_view = x1_dram.rearrange("b (i p) d -> b p i d", p=P)
        block = ctx.enter_context(nc.Block())

        @block.sync
        def _(sp):
            def load_round(r, par):
                row = sp.value_load(rows[0:1, ds(r, 1)], min_val=0, max_val=E0)
                sp.dma_start(w1_raw[par][:], w1_all[ds(row, 1)].rearrange("e (k p) h -> p (e k) h", p=P))\
                    .then_inc(raw_loaded[par], 16)
                sp.dma_start(w2_raw[par][:], w2_all[ds(row, 1)].rearrange("e (m p) d -> p (e m) d", p=P))\
                    .then_inc(raw_loaded[par], 16)
                sp.dma_start(b1[par][:], b1_all[ds(row, 1)].rearrange("e p m -> p (e m)")).then_inc(raw_loaded[par], 16)
                sp.dma_start(b2[par][:], b2_all[ds(row, 1)].rearrange("e p k -> p (e k)")).then_inc(raw_loaded[par], 16)

            def load_x(b, par):
                at = b * S
                for c, src in enumerate((xh_dram, xl_dram)):
                    sp.dma_start(x_raw[:, c], src[:, :, ds(at, S)]).then_inc(x_loaded, 16)

            def load_nat(b):
                sp.dma_start(x_nat[:], x_view[ds(b, 1)].rearrange("b p i d -> p (b i) d")).then_inc(nat_loaded, 16)

            load_x(0, 0)
            load_round(0, 0)
            load_round(1, 1)
            sp.wait_ge(x_placed, 1)
            load_x(1, 1)
            load_nat(B - 1)
            with sp.Fori(0, B // 2) as pair:
                for bp in range(2):
                    b = pair * 2 + bp
                    for f in range(NF):
                        r = pair * (2 * NF) + (bp * NF + f)
                        wait_alone(sp, w_low, r * MT + MT, sp_ticks)
                        wait_alone(sp, gelued, r * MT + MT, sp_ticks)
                        wait_alone(sp, b_sum, r + 1, sp_ticks)
                        load_round((r + 2) % R, (NF * bp + f) % 2)
                        if f == 0:
                            wait_alone(sp, added, b * 2 + 2, sp_ticks)
                            sp.dma_start(x1_view[ds((b + (B - 1)) % B, 1)].rearrange("b p i d -> p (b i) d"), x_nat[:])\
                                .then_inc(stored, 16)
                        if f == 1:
                            wait_alone(sp, stored, b * 16 + 16, sp_ticks)
                            load_nat(b)
                    wait_alone(sp, x_placed, b + 2, sp_ticks)
                    load_x((b + 2) % B, bp)
            sp.wait_ge(added, B * 2 + 2)
            sp.dma_start(x1_view[B - 1], x_nat[:]).then_inc(stored, 16)
            sp.wait_ge(stored, (B + 1) * 16)
            sp.wait_ge(x_loaded, 32 * (B + 2))
            for i in range(2):
                sp.wait_ge(raw_loaded[i], 64 * (R // 2 + 1))

        def pieces(par, m):
            c = slice(m * P, m * P + P)
            return ((w1_raw[par][:, :, c], w1h[par][:, :, c], w1l[par][:, :, c]),
                    (w2_raw[par][:, m, :], w2h[par][:, m, :], w2l[par][:, m, :]))

        @block.gpsimd
        def _(pool):
            def split_high(count, par, m):
                for raw, high, _ in pieces(par, m):
                    ins = pool.tensor_scalar(high, raw, 1.0, 1.0, ALU.mult, ALU.mult)
                ins.then_inc(w_high, 1)

            def place_x(n, par):
                wait_alone(pool, x_loaded, n * 32 + 32, pool_ticks)
                for c, part in enumerate((xh[par], xl[par])):
                    ins = pool.tensor_scalar(part[:], x_raw[:, c], 1.0, 1.0, ALU.mult, ALU.mult)
                ins.then_inc(x_placed, 1)

            place_x(0, 0)
            pool.wait_ge(raw_loaded[0], 64)
            for m in range(MT):
                split_high(m + 1, 0, m)
            with pool.Fori(0, B // 2) as pair:
                for bp in range(2):
                    b = pair * 2 + bp
                    for f in range(NF):
                        r = pair * (2 * NF) + (bp * NF + f)
                        par = (bp * NF + f) % 2
                        for m in range(MT):
                            U = r * MT + m
                            slot = (f * MT + m) % SLOTS
                            if m == 0:
                                pool.wait_ge(coef_set, r + 1)
                            pool.wait_ge(gelued, U + 1)
                            wait_alone(pool, unit_done, U + 1, pool_ticks)
                            pool.tensor_scalar(hh[:, slot, :], hidden[:, slot, :], coef_now[:, par:par + 1], 1.0,
                                               ALU.mult, ALU.mult).then_inc(h_high, 1)
                            if m == 0:
                                pool.wait_ge(raw_loaded[1 - par], (pair * NF + (bp * NF + f + 1) // 2) * 64 + 64)
                                wait_alone(pool, unit_done, r * MT + SLOTS, pool_ticks)
                            split_high(U + (MT + 1), 1 - par, m)
                            if f == 1 and m == 4:
                                place_x(b + 1, 1 - bp)

        @block.scalar
        def _(act):
            def gate(b, bp):
                act.wait_ge(unit_done, b * (NF * MT) + SLOTS)
                for k in range(KT):
                    ins = act.activation(zT[:, k, :], o_ps[1 - bp][k][:], ACT.Silu, bias=bsum[:, 1 - bp, k:k + 1])
                ins.then_inc(gated, 1)

            with act.Fori(0, B // 2) as pair:
                for bp in range(2):
                    b = pair * 2 + bp
                    for f in range(NF):
                        par = (bp * NF + f) % 2
                        for m in range(MT):
                            U = pair * (2 * NF * MT) + ((bp * NF + f) * MT + m)
                            slot = (f * MT + m) % SLOTS
                            act.wait_ge(hid_ready, U + 1)
                            act.wait_ge(h_low, U + 1)
                            act.activation(hidden[:, slot, :], h_ps[slot][:], ACT.Gelu_apprx_tanh,
                                           bias=b1[par][:, m:m + 1]).then_inc(gelued, 1)
                            if f == 0 and m == 2:
                                gate(b, bp)
            gate(B, 0)

        @block.vector
        def _(dve):
            dve.memset(bsum[:], 0.0)
            for k in range(KT):
                dve.memset(o_ps[1][k][:], 0.0)
            dve.drain()
            dve.sem_inc(h_low, SLOTS)

            def split_low(count, par, m):
                dve.wait_ge(w_high, count)
                for raw, high, low in pieces(par, m):
                    ins = dve.tensor_tensor(low, raw, high.bitcast(F32), ALU.subtract)
                ins.then_inc(w_low, 1)

            def mix(b, b_before):
                dve.wait_ge(gated, b + 1)
                for k in range(KT):
                    ins = dve.tensor_tensor(zT[:, k, :], zT[:, k, :], acc[:, k, ds(b_before * S, S)], ALU.mult)
                ins.then_inc(mixed, 1)

            def add(b, half):
                dve.wait_ge(z_turned, b * 2 + (half + 1))
                if half == 0:
                    dve.wait_ge(nat_loaded, b * 16 + 16)
                at = x_nat[:, 2 * half:2 * half + 2, :]
                dve.tensor_tensor(at, z_ps[:].rearrange("p (i d) -> p i d", d=D), at, ALU.add).then_inc(added, 1)

            dve.tensor_copy(coef_now[:, 0:1], coef[:, 0:1]).then_inc(coef_set, 1)
            for m in range(MT):
                split_low(m + 1, 0, m)
            with dve.Fori(0, B // 2) as pair:
                for bp in range(2):
                    b = pair * 2 + bp
                    for f in range(NF):
                        r = pair * (2 * NF) + (bp * NF + f)
                        par = (bp * NF + f) % 2
                        if f == 0:
                            dve.tensor_scalar(bsum[:, bp, :], b2[par][:], coef[:, ds(r, 1)], None, ALU.mult)\
                                .then_inc(b_sum, 1)
                        else:
                            dve.wait_ge(b_sum, r)
                            dve.scalar_tensor_tensor(out=bsum[:, bp, :], in0=b2[par][:], scalar=coef[:, ds(r, 1)],
                                                     in1=bsum[:, bp, :], op0=ALU.mult, op1=ALU.add).then_inc(b_sum, 1)
                        for m in range(MT):
                            U = pair * (2 * NF * MT) + ((bp * NF + f) * MT + m)
                            slot = (f * MT + m) % SLOTS
                            dve.wait_ge(h_high, U + 1)
                            if m == 0:
                                dve.wait_ge(coef_set, r + 1)
                            if m == 2:
                                dve.wait_ge(h_low, U + SLOTS)
                                dve.tensor_copy(coef_now[:, 1 - par:2 - par], coef[:, ds((r + 1) % R, 1)])\
                                    .then_inc(coef_set, 1)
                            dve.scalar_tensor_tensor(out=hl[:, slot, :], in0=hidden[:, slot, :],
                                                     scalar=coef_now[:, par:par + 1], in1=hh[:, slot, :].bitcast(F32),
                                                     op0=ALU.mult, op1=ALU.subtract).then_inc(h_low, 1)
                            split_low(U + (MT + 1), 1 - par, m)
                            if f == 0 and m == 3:
                                mix(b, (b + (B - 1)) % B)
                            if f == 0 and m in (5, 7):
                                add(b, (m - 5) // 2)
            mix(B, B - 1)
            add(B, 0)
            add(B, 1)

        @block.tensor
        def _(pe):
            pe.sem_inc(unit_done, SLOTS)

            def hidden_sums(U, pair, c):
                c_round, m = c // MT % (2 * NF), c % MT
                par, bp = c_round % 2, c_round // NF
                if c % (NF * MT) == 0:
                    pe.wait_ge(x_placed, pair * 2 + (c // (NF * MT) + 1))
                pe.wait_ge(w_low, U + 1)
                w = slice(m * P, m * P + P)
                for i, (weight, x) in enumerate([(w1h, xh), (w1l, xh), (w1h, xl)]):
                    for k in range(KT):
                        ins = pe.matmul(h_ps[c % SLOTS][:], weight[par][:, k, w], x[bp][:, k, :],
                                        start=(i == 0 and k == 0), stop=(i == 2 and k == KT - 1))
                ins.then_inc(hid_ready, 1)

            def output_sums(U, c):
                c_round, m = c // MT, c % MT
                par, bp, f = c_round % 2, c_round // NF, c_round % NF
                pe.wait_ge(h_low, U + (SLOTS + 1))
                for k in range(KT):
                    w = slice(k * P, k * P + P)
                    for i, (weight, h) in enumerate([(w2h, hh), (w2l, hh), (w2h, hl)]):
                        ins = pe.matmul(o_ps[bp][k][:], weight[par][:, m, w], h[:, c % SLOTS, :],
                                        start=(f == 0 and m == 0 and i == 0),
                                        stop=(f == NF - 1 and m == MT - 1 and i == 2))
                ins.then_inc(unit_done, 1)

            def turn(b, half):
                if half == 0:
                    pe.wait_ge(mixed, b + 1)
                else:
                    pe.wait_ge(added, b * 2 + 1)
                for i in range(2):
                    for k in range(KT):
                        at = (2 * half + i) * P
                        ins = pe.transpose(z_ps[:, i * D + k * P:i * D + k * P + P], zT[:, k, at:at + P], ident[:])
                ins.then_inc(z_turned, 1)

            hidden_sums(0, 0, 0)
            hidden_sums(1, 0, 1)
            with pe.Fori(0, B // 2) as pair:
                for c in range(2 * NF * MT):
                    U = pair * (2 * NF * MT) + c
                    hidden_sums(pair * (2 * NF * MT) + (c + 2), pair, c + 2)
                    output_sums(U, c)
                    if c % (NF * MT) in (4, 6):
                        turn(pair * 2 + c // (NF * MT), (c % (NF * MT) - 4) // 2)
            turn(B, 0)
            turn(B, 1)


def head_attention_phase(nc, w_heads, wo_heads, slopes, ident, xh, xl, acc):
    with ExitStack() as ctx:
        sb, ps, sem = hold(ctx, nc)
        rel = sb("at_rel", [P, S])
        slope_sb = sb("at_slope", [P, 2 * KVH])
        bias = sb("at_bias", [P, 2, S])
        w_raw = [sb(f"at_w_raw{i}", [P, KT, 256]) for i in range(2)]
        wo_raw = [sb(f"at_wo_raw{i}", [P, D]) for i in range(2)]
        wh, wl = (sb(f"at_w{x}", [P, KT, 256], F32R) for x in "hl")
        woh, wol = (sb(f"at_wo{x}", [P, D], F32R) for x in "hl")
        qst = [sb(f"at_q{i}", [P, 2, S], F32R) for i in range(2)]
        kh = [sb(f"at_kh{i}", [P, S], F32R) for i in range(2)]
        kl = [sb(f"at_kl{i}", [P, S], F32R) for i in range(2)]
        k_parts = sb("at_k_parts", [P, 2, S], F32R)
        k_twice = [sb(f"at_k_twice{i}", [P, 2, S]) for i in range(2)]
        vT = sb("at_vT", [P, S])
        v = [sb(f"at_v{i}", [P, TT, HD]) for i in range(2)]
        p_sb = sb("at_p", [P, 2 * TT, S])
        pT = sb("at_pT", [P, 4, S])
        nmax = sb("at_nmax", [P, 2 * TT])
        total = sb("at_total", [P, 2 * TT])
        recip = sb("at_recip", [P, 2 * TT])
        oh = [sb(f"at_oh{i}", [P, S], F32R) for i in range(2)]
        ol = [sb(f"at_ol{i}", [P, S], F32R) for i in range(2)]

        s_ps = [ps(f"at_s_ps{i}") for i in range(2)]
        t_ps = [ps(f"at_t_ps{i}") for i in range(2)]
        o_ps = [ps(f"at_o_ps{i}") for i in range(2)]
        m_ps = [ps(f"at_m_ps{i}") for i in range(2)]

        w_loaded = [sem("at_w_loaded0"), sem("at_w_loaded1")]
        slope_loaded = sem("at_slope_loaded")
        k_copied = [sem("at_k_copied0"), sem("at_k_copied1")]
        consts = sem("at_consts")
        w_split = sem("at_w_split")
        wo_split = sem("at_wo_split")
        w_chain = sem("at_w_chain")
        k_placed = sem("at_k_placed")
        scaled = sem("at_scaled")
        proj = sem("at_proj")
        scored = sem("at_scored")
        turned = sem("at_turned")
        summed = sem("at_summed")
        q_high = sem("at_q_high")
        vT_out = sem("at_vT_out")
        exped = sem("at_exped")
        o_high = sem("at_o_high")
        odd_out = sem("at_odd_out")
        even_out = sem("at_even_out")
        biased = sem("at_biased")
        masked = sem("at_masked")
        recips = sem("at_recips")
        proj_out = sem("at_proj_out")
        o_low = sem("at_o_low")
        zeroed = sem("at_zeroed")
        pool_ticks, dve_ticks, pe_ticks = sem("at_pool_ticks"), sem("at_dve_ticks"), sem("at_pe_ticks")
        block = ctx.enter_context(nc.Block())

        def kv_count(n):
            return n * 5 + (-3)

        def q_count(n):
            return n * 5

        def v_count(n):
            return n * 5 + 1

        def out_count(n, m):
            return n * 5 + (13 + m)

        PAIRS = B // 2

        @block.sync
        def _(sp):
            sp.dma_start(slope_sb[:], slopes).then_inc(slope_loaded, 16)
            for i in range(2):
                sp.dma_start(w_raw[i][:], w_heads[i]).then_inc(w_loaded[i], 16)
                sp.dma_start(wo_raw[i][:], wo_heads[i]).then_inc(w_loaded[i], 16)

            def copy_k(count, par):
                sp.wait_ge(proj_out, count)
                for half in range(2):
                    sp.dma_start(k_twice[par][HD * half:HD * half + HD, :, :], k_parts[0:HD, :, :].bitcast(F32))\
                        .then_inc(k_copied[par], 16)

            copy_k(1, 0)
            copy_k(4, 1)
            with sp.Fori(0, KVH // 2) as jj:
                for jp in range(2):
                    j = jj * 2 + jp
                    with sp.Fori(0, PAIRS) as pair:
                        for par in range(2):
                            copy_k(kv_count(j * B + pair * 2 + (par + 2)), par)
                    sp.wait_ge(w_split, j + 1)
                    sp.wait_ge(wo_split, j + 1)
                    sp.dma_start(w_raw[jp][:], w_heads[ds((j + 2) % KVH, 1)].rearrange("a p k n -> p (a k) n"))\
                        .then_inc(w_loaded[jp], 16)
                    sp.dma_start(wo_raw[jp][:], wo_heads[ds((j + 2) % KVH, 1)].rearrange("a p n -> p (a n)"))\
                        .then_inc(w_loaded[jp], 16)
            for i in range(2):
                sp.wait_ge(w_loaded[i], 32 * (KVH // 2 + 1))
                sp.wait_ge(k_copied[i], 32 * (KVH * B // 2 + 1))

        @block.gpsimd
        def _(pool):
            pool.iota(rel[:], [[-1, S]], base=S - P, channel_multiplier=1,
                      allow_small_or_imprecise_dtypes=True).then_inc(consts, 1)
            pool.wait_ge(consts, 1)
            pool.affine_select(out=rel[:], in_=rel[:], compare_op=ALU.is_ge, fill=BIG, base=S - P,
                               pattern=[[-1, S]], channel_multiplier=1).then_inc(consts, 1)

            def split(hi, lo, raw, n):
                pool.tensor_scalar(hi, raw, 1.0, 1.0, ALU.mult, ALU.mult).then_inc(w_chain, 1)
                pool.wait_ge(w_chain, n + 1)
                return pool.tensor_tensor(lo, raw, hi.bitcast(F32), ALU.subtract)

            def place_k(half, par):
                wait_alone(pool, k_copied[par], half * 32 + 32, pool_ticks)
                for c, part in enumerate((kh[par], kl[par])):
                    ins = pool.tensor_scalar(part[:], k_twice[par][:, c, :], 1.0, 1.0, ALU.mult, ALU.mult)
                ins.then_inc(k_placed, 1)

            def scale(t, qt):
                wait_alone(pool, recips, t * TT + (qt + 1), pool_ticks)
                for u in (2 * qt, 2 * qt + 1):
                    p = p_sb[:, u, 0:(qt + 1) * P]
                    pool.tensor_scalar(p, p, recip[:, u:u + 1], 1.0, ALU.mult, ALU.mult).then_inc(scaled, 1)

            def body(t, half, par):
                for qt in range(TT):
                    scale(t + 1 if qt == TT - 1 else t, (qt + 1) % TT)
                    if qt == 0:
                        place_k(half + par, 1 - par)

            pool.wait_ge(w_loaded[0], 32)
            split(wh[:], wl[:], w_raw[0][:], 0).then_inc(w_split, 1)
            place_k(0, 0)
            scale(0, 0)
            with pool.Fori(0, KVH // 2) as jj:
                for jp in range(2):
                    j = jj * 2 + jp
                    body(j * B, j * PAIRS, 0)
                    pool.wait_ge(proj, j * (5 * B) + out_count(-1, 1))
                    wait_alone(pool, w_loaded[jp], jj * 32 + 32, pool_ticks)
                    split(woh[:], wol[:], wo_raw[jp][:], j * 2 + 1).then_inc(wo_split, 1)
                    body(j * B + 1, j * PAIRS, 1)
                    with pool.Fori(1, PAIRS - 1) as pair:
                        for par in range(2):
                            body(j * B + pair * 2 + par, j * PAIRS + pair, par)
                    pool.wait_ge(proj, j * (5 * B) + q_count(B - 1))
                    wait_alone(pool, w_loaded[1 - jp], (jj + jp) * 32 + 32, pool_ticks)
                    split(wh[:], wl[:], w_raw[1 - jp][:], j * 2 + 2).then_inc(w_split, 1)
                    body(j * B + (B - 2), j * PAIRS + (PAIRS - 1), 0)
                    body(j * B + (B - 1), j * PAIRS + (PAIRS - 1), 1)

        @block.scalar
        def _(act):
            def take_q(count, par):
                act.wait_ge(proj, count)
                act.activation(qst[par][0:HD, 0, :], m_ps[1 - par][0:HD, :], ACT.Copy, scale=-HD ** -0.5)
                act.activation(qst[par][HD:P, 1, :], m_ps[1 - par][HD:P, :], ACT.Copy, scale=-HD ** -0.5)\
                    .then_inc(q_high, 1)

            def take_kv(count, par, n=None):
                act.wait_ge(proj, count)
                if n is not None:
                    act.wait_ge(k_placed, n)
                act.activation(k_parts[0:HD, 0, :], m_ps[par][0:HD, :], ACT.Copy)
                act.activation(vT[HD:P, :], m_ps[par][HD:P, :], ACT.Copy).then_inc(vT_out, 1)

            def exps(n, u):
                N = (u // 2 + 1) * P
                act.wait_ge(masked, n * 8 + (u + 3))
                act.activation(p_sb[:, u, 0:N], p_sb[:, u, 0:N], ACT.Exp, bias=nmax[:, u:u + 1],
                               scale=-1.0, accum_out=total[:, u:u + 1]).then_inc(exped, 1)

            def turn_out(n, u):
                N = (u // 2 + 1) * P
                act.wait_ge(turned, n * 8 + (u + 1))
                act.activation(pT[:, u % 4, 0:N], t_ps[1][:, 0:N], ACT.Copy).then_inc(odd_out, 1)

            def take_o(n, par):
                act.wait_ge(summed, n * TT + 1)
                act.activation(oh[par][:], o_ps[par][:], ACT.Copy).then_inc(o_high, 1)

            act.sem_inc(odd_out, 1)
            take_kv(1, 0)
            take_q(2, 0)
            take_kv(4, 1, 1)
            for u in range(4):
                exps(0, u)
            with act.Fori(0, KVH * B // 2) as pair:
                for par in range(2):
                    t = pair * 2 + par
                    for qt in range(TT):
                        n, u = (t, 2 * qt + 4) if qt < 2 else (t + 1, 2 * qt - 4)
                        if qt == 0:
                            take_q(q_count(t + 1), 1 - par)
                        exps(n, u)
                        turn_out(t, 2 * qt + 1)
                        if qt == 1:
                            take_kv(kv_count(t + 2), par, t + 2)
                        exps(n, u + 1)
                        if qt == 0:
                            take_o(t, 1 - par)
            take_o(KVH * B, 1)
            take_q(q_count(KVH * B + 1), 1)

        @block.vector
        def _(dve):
            dve.sem_inc(even_out, 1)
            dve.sem_inc(masked, 2)
            for tile in (woh, wol):
                dve.tensor_copy(tile[:], acc[:, 0, 0:D])
            dve.memset(o_ps[1][:], 0.0).then_inc(zeroed, 1)
            dve.wait_ge(slope_loaded, 16)
            dve.wait_ge(consts, 2)

            def set_bias(j, first, count):
                for h in range(2):
                    at = h if first else ds((j * 2 + h) % (2 * KVH), 1)
                    slope = slope_sb[:, h:h + 1] if first else slope_sb[:, at]
                    dve.tensor_scalar(bias[:, h, :], rel[:], slope, None, ALU.mult).then_inc(biased, 1)
                dve.wait_ge(biased, count)

            def q_rest(n, par):
                dve.wait_ge(q_high, n + 1)
                dve.scalar_tensor_tensor(out=qst[par][HD:P, 0, :], in0=m_ps[1 - par][0:HD, :], scalar=-HD ** -0.5,
                                         in1=qst[par][0:HD, 0, :].bitcast(F32), op0=ALU.mult, op1=ALU.subtract)
                dve.scalar_tensor_tensor(out=qst[par][0:HD, 1, :], in0=m_ps[1 - par][HD:P, :], scalar=-HD ** -0.5,
                                         in1=qst[par][HD:P, 1, :].bitcast(F32), op0=ALU.mult, op1=ALU.subtract)\
                    .then_inc(proj_out, 1)

            def k_rest(n, par):
                dve.wait_ge(vT_out, n + 1)
                dve.tensor_tensor(k_parts[0:HD, 1, :], m_ps[par][0:HD, :], k_parts[0:HD, 0, :].bitcast(F32),
                                  ALU.subtract).then_inc(proj_out, 1)

            def values(count, par):
                dve.wait_ge(proj, count)
                dve.tensor_copy(v[par][:].rearrange("p i d -> p (i d)"), m_ps[par][:, 0:TT * HD])\
                    .then_inc(proj_out, 1)

            def mask(n, u):
                N = (u // 2 + 1) * P
                wait_alone(dve, scored, n * 8 + (u + 1), dve_ticks)
                dve.tensor_tensor_reduce(out=p_sb[:, u, 0:N], in0=s_ps[u % 2][:, 0:N],
                                         in1=bias[:, u % 2, S - N:S], scale=1.0, scalar=BIG, op0=ALU.add,
                                         op1=ALU.min, accum_out=nmax[:, u:u + 1]).then_inc(masked, 1)

            def invert(n, qt):
                dve.wait_ge(exped, n * 8 + (2 * qt + 2))
                dve.reciprocal(recip[:, 2 * qt:2 * qt + 2], total[:, 2 * qt:2 * qt + 2]).then_inc(recips, 1)

            def turn_out(n, u):
                N = (u // 2 + 1) * P
                dve.wait_ge(turned, n * 8 + (u + 1))
                dve.tensor_copy(pT[:, u % 4, 0:N], t_ps[0][:, 0:N]).then_inc(even_out, 1)

            def add_out(n, par, b, m, skipped=0):
                dve.wait_ge(proj, out_count(n, m) + (-skipped))
                at = acc[:, m, ds(b * S, S)]
                dve.tensor_tensor(at, m_ps[(par + m) % 2][:], at, ALU.add).then_inc(proj_out, 1)

            def rest_o(n, par):
                dve.wait_ge(o_high, n + 1)
                dve.tensor_tensor(ol[par][:], o_ps[par][:], oh[par][:].bitcast(F32), ALU.subtract).then_inc(o_low, 1)

            def body(t, par, b_before, new_head=None):
                for qt in range(TT):
                    n, u = (t, 2 * qt + 4) if qt < 2 else (t + 1, 2 * qt - 4)
                    if qt == 2 and new_head is not None:
                        dve.wait_ge(masked, t * 8 + 10)
                        set_bias(new_head, False, new_head * 2 + 2)
                    if qt == 3:
                        add_out(t + (-1), 1 - par, b_before, 0)
                    mask(n, u)
                    invert(t + 1 if qt == TT - 1 else t, (qt + 1) % TT)
                    turn_out(t, 2 * qt)
                    mask(n, u + 1)
                    if qt == 0:
                        q_rest(t + 1, 1 - par)
                    if qt == 1:
                        values(v_count(t + 1), 1 - par)
                        rest_o(t, 1 - par)
                        k_rest(t + 2, par)
                    if qt == 3:
                        add_out(t + (-1), 1 - par, b_before, 1)

            set_bias(0, True, 2)
            k_rest(0, 0)
            q_rest(0, 0)
            values(3, 0)
            k_rest(1, 1)
            for u in range(4):
                mask(0, u)
            invert(0, 0)
            with dve.Fori(0, KVH) as j:
                with dve.Fori(0, PAIRS - 1) as pair:
                    for par in range(2):
                        body(j * B + pair * 2 + par, par, (pair * 2 + (par + B - 1)) % B)
                body(j * B + (B - 2), 0, B - 3)
                body(j * B + (B - 1), 1, B - 2, new_head=j + 1)
            q_rest(KVH * B + 1, 1)
            rest_o(KVH * B, 1)
            for m in range(KT):
                add_out(KVH * B - 1, 1, B - 1, m, skipped=2)

        @block.tensor
        def _(pe):
            def project(bank, w, b):
                terms = [(wh, xh), (wl, xh), (wh, xl)]
                for i, (weight, x) in enumerate(terms):
                    for k in range(KT):
                        ins = pe.matmul(bank[:], weight[:, k, w:w + P], x[:, k, ds(b * S, S)],
                                        start=(i == 0 and k == 0), stop=(i == 2 and k == KT - 1))
                ins.then_inc(proj, 1)

            def project_q(n, par, b):
                pe.wait_ge(proj_out, q_count(n) + (-2))
                project(m_ps[1 - par], 0, b)

            def project_kv(n, par, b):
                pe.wait_ge(proj_out, kv_count(n) + (-2))
                project(m_ps[par], P, b)

            def turn_v(n, par, out):
                pe.wait_ge(vT_out, n + 1)
                wait_alone(pe, proj_out, out, pe_ticks)
                for i in range(TT):
                    ins = pe.transpose(m_ps[par][:, HD * i:HD * i + HD], vT[HD:P, P * i:P * i + P], ident[HD:P, HD:P])
                ins.then_inc(proj, 1)

            def project_out(n, par, skipped=0):
                pe.wait_ge(o_low, n + 2)
                for m in range(KT):
                    bank = m_ps[(par + m) % 2]
                    pe.wait_ge(proj_out, out_count(n, m) + (-2 - skipped))
                    for i, (w, o) in enumerate([(woh, oh), (wol, oh), (woh, ol)]):
                        ins = pe.matmul(bank[:], w[:, m * P:m * P + P], o[par][:], start=(i == 0), stop=(i == 2))
                    ins.then_inc(proj, 1)

            def score(n, par, u):
                N = (u // 2 + 1) * P
                pe.wait_ge(masked, n * 8 + (u + 1))
                q = qst[par][:, u % 2, u // 2 * P:(u // 2 + 1) * P]
                pe.matmul(s_ps[u % 2][:, 0:N], q, kh[par][:, 0:N], start=True, stop=False)
                pe.matmul(s_ps[u % 2][:, 0:N], q, kl[par][:, 0:N], start=False, stop=True).then_inc(scored, 1)

            def turn(n, u):
                pe.wait_ge(even_out if u % 2 == 0 else odd_out, n * TT + (u // 2 + 1))
                pe.wait_ge(scaled, n * 8 + (u + 1))
                for k in range(u // 2 + 1):
                    ins = pe.transpose(t_ps[u % 2][:, k * P:k * P + P], p_sb[:, u, k * P:k * P + P], ident[:])
                ins.then_inc(turned, 1)

            def weigh(n, par, qt):
                pe.wait_ge(even_out, n * TT + (qt + 2))
                pe.wait_ge(odd_out, n * TT + (qt + 2))
                for k in range(qt + 1):
                    for h in range(2):
                        ins = pe.matmul(o_ps[par][HD * h:HD * h + HD, qt * P:qt * P + P], v[par][:, k, :],
                                        pT[:, (2 * qt + h) % 4, k * P:k * P + P], start=(k == 0), stop=(k == qt))
                ins.then_inc(summed, 1)

            def body(t, par, b_next, new_head=None, new_out=None):
                for qt in range(TT):
                    n, n_par, u = (t, par, 2 * qt + 4) if qt < 2 else (t + 1, 1 - par, 2 * qt - 4)
                    if qt == 2:
                        pe.wait_ge(proj_out, q_count(t + 1))
                        pe.wait_ge(k_placed, t + 2)
                    for h in range(2):
                        score(n, n_par, u + h)
                        turn(t, 2 * qt + h)
                    if qt > 0:
                        weigh(t, par, qt - 1)
                    if qt == 0:
                        turn_v(t + 1, 1 - par, v_count(t + 1) + (-2))
                    if qt == 1:
                        if new_head is not None:
                            pe.wait_ge(w_split, new_head + 1)
                        project_kv(t + 2, par, b_next)
                    if qt == 2:
                        if new_out is not None:
                            pe.wait_ge(wo_split, new_out + 1)
                        project_out(t + (-1), 1 - par)
                    if qt == 3:
                        project_q(t + 2, par, b_next)
                        weigh(t, par, 3)

            pe.wait_ge(zeroed, 1)
            pe.sem_inc(summed, 1)
            pe.wait_ge(w_split, 1)
            project(m_ps[0], P, 0)
            project(m_ps[1], 0, 0)
            turn_v(0, 0, 1)
            pe.wait_ge(proj_out, 2)
            project(m_ps[1], P, 1)
            pe.wait_ge(proj_out, 3)
            project(m_ps[0], 0, 1)
            pe.wait_ge(k_placed, 1)
            for u in range(4):
                score(0, 0, u)
            with pe.Fori(0, KVH) as j:
                body(j * B, 0, 2)
                body(j * B + 1, 1, 3, new_out=j)
                with pe.Fori(1, PAIRS - 1) as pair:
                    for par in range(2):
                        body(j * B + pair * 2 + par, par, pair * 2 + (par + 2))
                body(j * B + (B - 2), 0, 0, new_head=j + 1)
                body(j * B + (B - 1), 1, 1)
            project_out(KVH * B - 1, 1, skipped=2)


RH = D // HD
WIDTHS = [S - P * i for i in range(TT)]
STARTS = [sum(WIDTHS[:i]) for i in range(TT)]
EPS_RMS = 1.1920928955078125e-07


def recurrence_phase(nc, x1_dram, w_write, w_read, decay, log_alpha, ident, y, r1, s_dram):
    with ExitStack() as ctx:
        sb, ps, sem = hold(ctx, nc)
        x_in = [sb(f"rc_x{i}", [P, TT, D]) for i in range(2)]
        stats = sb("rc_stats", [P, TT, 6])
        mv = sb("rc_mv", [P, TT, 2])
        std = sb("rc_std", [P, 2, TT])
        rstd = sb("rc_rstd", [P, TT])
        squares = sb("rc_squares", [P, TT, D])
        sq_sum = sb("rc_sq_sum", [P, TT])
        eps = sb("rc_eps", [P, 2])
        carry = sb("rc_carry", [P, 1])
        ww = sb("rc_ww", [P, KT, D])
        wr = sb("rc_wr", [P, KT, D])
        gam = sb("rc_gam", [P, RH])
        la = sb("rc_la", [P, RH])
        ahead = sb("rc_ahead", [P, S])
        factor = sb("rc_factor", [P, RH, S])
        yT = [sb(f"rc_yT{i}", [P, KT, S + 1]) for i in range(2)]
        v = [sb(f"rc_v{i}", [P, TT, D]) for i in range(2)]
        prod = sb("rc_prod", [P, RH, sum(WIDTHS)])
        readT = sb("rc_readT", [P, KT, S])
        s_sb = [sb(f"rc_s{i}", [P, TT, D]) for i in range(2)]
        xT_ps = [ps(f"rc_xT_ps{k}") for k in range(KT)]
        n_ps = [ps(f"rc_n_ps{k}") for k in range(2)]
        d_ps = [ps(f"rc_d_ps{k}") for k in range(2)]
        r_ps = [ps(f"rc_r_ps{k}") for k in range(2)]

        x_loaded = [sem("rc_x_loaded0"), sem("rc_x_loaded1")]
        w_loaded = sem("rc_w_loaded")
        s_stored = [sem("rc_s_stored0"), sem("rc_s_stored1")]
        s_free = sem("rc_s_free")
        pool_chain = sem("rc_pool_chain")
        act_chain = sem("rc_act_chain")
        dve_chain = sem("rc_dve_chain")
        stats_done = sem("rc_stats_done")
        var_done = sem("rc_var_done")
        std_done = sem("rc_std_done")
        rstd_done = sem("rc_rstd_done")
        normed = sem("rc_normed")
        copied = sem("rc_copied")
        sp_ticks = sem("rc_sp_ticks")
        squared = sem("rc_squared")
        rms_done = sem("rc_rms_done")
        r1_done = sem("rc_r1_done")
        turned = sem("rc_turned")
        turn_out = sem("rc_turn_out")
        valued = sem("rc_valued")
        value_out = sem("rc_value_out")
        dotted = sem("rc_dotted")
        decayed = sem("rc_decayed")
        read = sem("rc_read")
        read_out = sem("rc_read_out")
        mixed = sem("rc_mixed")
        s_done = sem("rc_s_done")
        dve_ticks = sem("rc_dve_ticks")
        x_view = x1_dram.rearrange("b (i p) d -> b p i d", p=P)
        s_view = s_dram.rearrange("b (i p) d -> b p i d", p=P)
        block = ctx.enter_context(nc.Block())

        def row(vector):
            return vector.rearrange("(a h) -> a h", a=1).broadcast_to([P, RH])

        @block.sync
        def _(sp):
            sp.sem_inc(s_free, 2)
            for i in range(2):
                sp.dma_start(x_in[i][:], x_view[i]).then_inc(x_loaded[i], 16)
            sp.dma_start(gam[:], row(decay)).then_inc(w_loaded, 16)
            sp.dma_start(la[:], row(log_alpha)).then_inc(w_loaded, 16)
            sp.dma_start(ww[:], w_write.rearrange("(k p) n -> p k n", p=P)).then_inc(w_loaded, 16)
            sp.dma_start(wr[:], w_read.rearrange("(k p) n -> p k n", p=P)).then_inc(w_loaded, 16)
            with sp.Fori(0, B // 2) as pair:
                for par in range(2):
                    b = pair * 2 + par
                    sp.wait_ge(turned, b + 1)
                    sp.wait_ge(rms_done, b + 1)
                    wait_alone(sp, copied, b + 1, sp_ticks)
                    sp.dma_start(x_in[par][:], x_view[ds((b + 2) % B, 1)].rearrange("b p i d -> p (b i) d"))\
                        .then_inc(x_loaded[par], 16)
                    sp.wait_ge(s_done, b * 2 + 2)
                    sp.dma_start(s_view[ds(b, 1)].rearrange("b p i d -> p (b i) d"), s_sb[par][:])\
                        .then_inc(s_stored[par], 16)
                    sp.wait_ge(s_stored[par], pair * 16 + 16)
                    sp.sem_inc(s_free, 1)
            for i in range(2):
                sp.wait_ge(x_loaded[i], 16 * (B // 2 + 1))
                sp.wait_ge(s_stored[i], 16 * (B // 2))

        @block.gpsimd
        def _(pool):
            pool.iota(ahead[:], [[1, S]], base=-1, channel_multiplier=-1,
                      allow_small_or_imprecise_dtypes=True).then_inc(pool_chain, 1)
            pool.wait_ge(act_chain, 2 + RH)
            for h in range(RH):
                pool.affine_select(out=factor[:, h, :], in_=factor[:, h, :], compare_op=ALU.is_ge, fill=0.0,
                                   base=-1, pattern=[[1, S]], channel_multiplier=-1).then_inc(pool_chain, 1)

        @block.scalar
        def _(act):
            act.wait_ge(w_loaded, 64)
            act.activation(gam[:], gam[:], ACT.Exp, scale=-1.0).then_inc(act_chain, 1)
            act.wait_ge(dve_chain, 2)
            act.activation(gam[:], gam[:], ACT.Ln).then_inc(act_chain, 1)
            act.wait_ge(dve_chain, 3)
            for h in range(RH):
                act.activation(factor[:, h, :], ahead[:], ACT.Exp, scale=gam[:, h:h + 1], bias=la[:, h:h + 1])\
                    .then_inc(act_chain, 1)

            def roots(n, par):
                act.wait_ge(var_done, n * TT + TT)
                act.activation(std[:, 0, :], mv[:, :, 1], ACT.Sqrt, bias=eps[:, 0:1]).then_inc(std_done, 1)

            def rms(n, par):
                act.wait_ge(normed, n * TT + TT)
                for i in range(TT):
                    act.activation(squares[:, i, :], x_in[par][:, i, :], ACT.Square,
                                   accum_out=sq_sum[:, i:i + 1]).then_inc(squared, 1)
                act.wait_ge(squared, n * TT + TT)
                act.activation(std[:, 1, :], sq_sum[:], ACT.Sqrt, scale=1.0 / D, bias=eps[:, 1:2]).then_inc(rms_done, 1)

            def take_turn(n, par):
                act.wait_ge(turned, n + 1)
                for k in range(KT):
                    ins = act.activation(yT[par][:, k, 1:S + 1], xT_ps[k][:], ACT.Copy)
                ins.then_inc(turn_out, 1)

            def take_values(n, par):
                for half in range(2):
                    act.wait_ge(valued, n * 2 + (half + 1))
                    act.activation(v[par][:, 2 * half:2 * half + 2, :].rearrange("p i d -> p (i d)"), n_ps[half][:],
                                   ACT.Copy).then_inc(value_out, 1)

            def take_read(n, g):
                act.wait_ge(read, n * 2 + (g + 1))
                act.activation(readT[:, g, :], r_ps[g][:], ACT.Copy).then_inc(read_out, 1)

            roots(0, 0)
            rms(0, 0)
            take_turn(0, 0)
            take_values(0, 0)
            with act.Fori(0, B // 2) as pair:
                for par in range(2):
                    b, nxt = pair * 2 + par, 1 - par
                    roots(b + 1, nxt)
                    rms(b + 1, nxt)
                    take_turn(b + 1, nxt)
                    take_read(b, 0)
                    take_values(b + 1, nxt)
                    take_read(b, 1)

        @block.vector
        def _(dve):
            dve.sem_inc(decayed, 2)
            dve.memset(eps[:, 0:1], EPS_LN)
            dve.memset(eps[:, 1:2], EPS_RMS)
            for i in range(2):
                dve.memset(yT[i][:, :, 0:1], 0.0)
            dve.wait_ge(pool_chain, 1)
            dve.tensor_scalar(ahead[:], ahead[:], 0.0, None, ALU.max).then_inc(dve_chain, 1)
            dve.wait_ge(act_chain, 1)
            dve.tensor_scalar(gam[:], gam[:], 1.0, None, ALU.add).then_inc(dve_chain, 1)
            dve.wait_ge(act_chain, 2)
            dve.tensor_scalar(gam[:], gam[:], -1.0, None, ALU.mult).then_inc(dve_chain, 1)

            def norm(n, pair_n, par):
                wait_alone(dve, x_loaded[par], pair_n * 16 + 16, dve_ticks)
                for i in range(TT):
                    dve.bn_stats(stats[:, i, :], x_in[par][:, i, :]).then_inc(stats_done, 1)
                wait_alone(dve, stats_done, n * TT + TT, dve_ticks)
                for i in range(TT):
                    dve.bn_aggr(mv[:, i, :], stats[:, i, :]).then_inc(var_done, 1)
                dve.wait_ge(std_done, n + 1)
                dve.reciprocal(rstd[:], std[:, 0, :]).then_inc(rstd_done, 1)
                dve.wait_ge(rstd_done, n + 1)
                for i in range(TT):
                    dve.tensor_scalar(x_in[par][:, i, :], x_in[par][:, i, :], mv[:, i, 0:1], rstd[:, i:i + 1], ALU.subtract, ALU.mult).then_inc(normed, 1)
                wait_alone(dve, normed, n * TT + TT, dve_ticks)
                dve.tensor_copy(y[:, ds((n % B) * TT, TT), :], x_in[par][:]).then_inc(copied, 1)

            def invert_rms(n):
                dve.wait_ge(rms_done, n + 1)
                dve.reciprocal(r1[:, ds((n % B) * TT, TT)], std[:, 1, :]).then_inc(r1_done, 1)

            def decay_unit(n, h, i):
                dve.wait_ge(dotted, n * (RH * TT) + (h * TT + i + 1))
                dve.tensor_tensor(prod[:, h, STARTS[i]:STARTS[i] + WIDTHS[i]], d_ps[i % 2][:, 0:WIDTHS[i]],
                                  factor[:, h, 0:WIDTHS[i]], ALU.mult).then_inc(decayed, 1)

            def finish(n, par):
                wait_alone(dve, copied, n + 1, dve_ticks)
                dve.wait_ge(s_free, n + 1)
                for half in range(2):
                    dve.wait_ge(mixed, n * 2 + (half + 1))
                    dve.tensor_tensor(s_sb[par][:, 2 * half:2 * half + 2, :].rearrange("p i d -> p (i d)"), n_ps[half][:],
                                      y[:, ds(n * TT + 2 * half, 2), :].rearrange("p i d -> p (i d)"), ALU.add)\
                        .then_inc(s_done, 1)

            norm(0, 0, 0)
            invert_rms(0)
            dve.wait_ge(pool_chain, 1 + RH)
            with dve.Fori(0, B // 2) as pair:
                for par in range(2):
                    b, nxt = pair * 2 + par, 1 - par
                    for h in range(RH):
                        for i in range(TT):
                            decay_unit(b, h, i)
                        if h == 0:
                            norm(b + 1, pair + par, nxt)
                        if h == 2:
                            invert_rms(b + 1)
                    finish(b, par)

        @block.tensor
        def _(pe):
            def turn(n, par):
                pe.wait_ge(normed, n * TT + TT)
                for k in range(KT):
                    for i in range(TT):
                        ins = pe.transpose(xT_ps[k][:, P * i:P * i + P], x_in[par][:, i, P * k:P * k + P], ident[:])
                ins.then_inc(turned, 1)

            def values(n, par):
                pe.wait_ge(turn_out, n + 1)
                for half in range(2):
                    for i in range(2):
                        for k in range(KT):
                            at = 1 + (2 * half + i) * P
                            ins = pe.matmul(n_ps[half][:, i * D:i * D + D], yT[par][:, k, at:at + P], ww[:, k, :],
                                            start=(k == 0), stop=(k == KT - 1))
                    ins.then_inc(valued, 1)

            def dots(n, par, h):
                row = slice(HD * (h % 2), HD * (h % 2) + HD)
                for i in range(TT):
                    pe.wait_ge(decayed, n * (RH * TT) + (h * TT + i + 1))
                    pe.matmul(d_ps[i % 2][:, 0:WIDTHS[i]], yT[par][row, h // 2, P * i:P * i + P],
                              yT[par][row, h // 2, 1 + P * i:1 + S], start=True, stop=True).then_inc(dotted, 1)

            def reads(n, par, g):
                pe.wait_ge(decayed, n * (RH * TT) + ((2 * g + 2) * TT + 2))
                for i in range(TT):
                    for h in range(2):
                        head = 2 * g + h
                        ins = pe.matmul(r_ps[g][HD * h:HD * h + HD, P * i:S], v[par][:, i, HD * head:HD * head + HD],
                                        prod[:, head, STARTS[i]:STARTS[i] + WIDTHS[i]],
                                        start=(i == 0), stop=(i == TT - 1))
                ins.then_inc(read, 1)

            def mix(n):
                pe.wait_ge(read_out, n * 2 + 2)
                for half in range(2):
                    for i in range(2):
                        for g in range(KT):
                            at = (2 * half + i) * P
                            ins = pe.matmul(n_ps[half][:, i * D:i * D + D], readT[:, g, at:at + P], wr[:, g, :],
                                            start=(g == 0), stop=(g == KT - 1))
                    ins.then_inc(mixed, 1)

            pe.wait_ge(w_loaded, 64)
            turn(0, 0)
            values(0, 0)
            with pe.Fori(0, B // 2) as pair:
                for par in range(2):
                    b, nxt = pair * 2 + par, 1 - par
                    dots(b, par, 0)
                    dots(b, par, 1)
                    turn(b + 1, nxt)
                    dots(b, par, 2)
                    pe.wait_ge(value_out, b * 2 + 2)
                    reads(b, par, 0)
                    values(b + 1, nxt)
                    dots(b, par, 3)
                    reads(b, par, 1)
                    pe.wait_ge(value_out, b * 2 + 4)
                    mix(b)


QH = 16
QD = D // QH
KV1 = 4
REP = QH // KV1
VP = 32
AHEAD = 3
RING = 4
QUADS = KV1 * TT
PROJ = {"q0": 0, "s0": 2 * P, "q1": P, "s1": 3 * P, "kk": 4 * P, "v": 5 * P}
PROJ_COLS = 5 * P + KV1 * QD
JOBS = 22


def rope_tables():
    inv = (1.0 / 10000.0 ** (np.arange(0, QD, 2, dtype=np.float32) / np.float32(QD))).astype(np.float32)
    angle = (np.arange(S, dtype=np.float32)[:, None] * inv[None, :]).astype(np.float32)
    angle = np.concatenate([angle, angle], -1).T
    cos, sin = np.cos(angle).astype(np.float32), np.sin(angle).astype(np.float32)
    sin[:QD // 2] *= -1.0
    cos, sin = np.tile(cos, (P // QD, 1)), np.tile(sin, (P // QD, 1))
    k_table = np.concatenate([cos[:P // 2], sin[:P // 2]])
    return np.ascontiguousarray(np.stack([-0.25 * cos, -0.25 * sin, k_table], 1).astype(np.float32))


def spread_tables():
    table = np.zeros((P, 3, 4, P), np.float32)
    for n in range(4):
        for r in range(P):
            e, c, d = r // 64, r % 64 // QD, r % QD
            table[(2 * n + e) * QD + d, c // 2, n, r] = 1.0
            table[(c % 2) * 64 + n * QD + d, 2, n, r] = 1.0
    return table


def attention_phase(nc, w_proj, w_out, g1, ropes, spreads, ident, y, r1):
    with ExitStack() as ctx:
        sb, ps, sem = hold(ctx, nc)
        wp = sb("aa_wp", [P, KT, PROJ_COLS])
        wo = sb("aa_wo", [P, KV1, D])
        g1_sb = sb("aa_g1", [P, KT])
        rope = sb("aa_rope", [P, 3, S])
        spread = sb("aa_spread", [P, 3, 4, P], F32R)
        hidden = sb("aa_hidden", [P, S])
        xr = sb("aa_xr", [P, TT, D])
        xrT = sb("aa_xrT", [P, KT, S])
        turn1 = sb("aa_turn1", [P, 3, S])
        turn2 = sb("aa_turn2", [P, 3, S])
        qh = sb("aa_qh", [P, 2, S], F32R)
        ql = sb("aa_ql", [P, 2, S], F32R)
        kk = sb("aa_kk", [P, S], F32R)
        v = [sb(f"aa_v{i}", [P, TT, KV1, VP]) for i in range(2)]
        q_all = [sb(f"aa_q{i}", [P, QH // 2, S], F32R) for i in range(2)]
        k_all = [sb(f"aa_k{i}", [P, KV1, S], F32R) for i in range(2)]
        p_sb = sb("aa_p", [P, RING * REP, S])
        pT = sb("aa_pT", [P, 2 * REP, S])
        oT = sb("aa_oT", [P, KV1, S])
        nmax = sb("aa_nmax", [P, RING * REP])
        total = sb("aa_total", [P, RING * REP])
        recip = sb("aa_recip", [P, RING * REP])

        s_ps = [ps(f"aa_s_ps{i}") for i in range(2)]
        t_ps = [ps(f"aa_t_ps{i}") for i in range(2)]
        o_ps = [ps(f"aa_o_ps{i}") for i in range(2)]
        m_ps = [ps(f"aa_m_ps{i}") for i in range(2)]

        loaded = sem("aa_loaded")
        tables_loaded = sem("aa_tables_loaded")
        consts = sem("aa_consts")
        xr_made = sem("aa_xr_made")
        made = sem("aa_made")
        dve_out = sem("aa_dve_out")
        act_out = sem("aa_act_out")
        roped = sem("aa_roped")
        k_low = sem("aa_k_low")
        scored = sem("aa_scored")
        masked = sem("aa_masked")
        exped = sem("aa_exped")
        recips = sem("aa_recips")
        scaled = sem("aa_scaled")
        turned = sem("aa_turned")
        out_a = sem("aa_out_a")
        out_d = sem("aa_out_d")
        weighed = sem("aa_weighed")
        o_out = sem("aa_o_out")
        zeroed = sem("aa_zeroed")
        dve_ticks, pool_ticks = sem("aa_dve_ticks"), sem("aa_pool_ticks")

        block = ctx.enter_context(nc.Block())

        BY_DVE, BY_ACT = 10, JOBS - 10

        def s_place(q, h):
            return h % 2, 0

        def t_place(q, h):
            i = q % TT
            return [(0, h * P), (h // 2, (h % 2) * 2 * P), (h % 2, 0), (h % 2, 0)][i]

        ACT_TAKES = [[(0, (0, 4))], [(0, (0, 2))], [(0, (0, 1))], [(0, (0, 1))]]
        DVE_TAKES = [[], [(1, (2, 4))], [(1, (1, 2)), (0, (2, 3)), (1, (3, 4))], [(1, (1, 2)), (0, (2, 3)), (1, (3, 4))]]
        TAKEN = [0, 0, 1, 4, 7]

        def taken(b, q, more=0):
            return b * (KV1 * TAKEN[TT]) + (q // TT * TAKEN[TT] + TAKEN[q % TT] + 1 + more)

        def made_count(n, j):
            return n * JOBS + (JOBS - 2 + j + 1)

        def dve_count(n, j):
            return n * BY_DVE + (BY_DVE - 2 + j + 1)

        def act_count(n, j):
            return n * BY_ACT + (BY_ACT + j - BY_DVE + 1)

        @block.sync
        def _(sp):
            for to, src in ((g1_sb, g1), (wp, w_proj.rearrange("(k p) n -> p k n", p=P))):
                sp.dma_start(to[:], src).then_inc(loaded, 16)
            sp.dma_start(rope[:], ropes).then_inc(tables_loaded, 16)
            sp.dma_start(p_sb[:, 0:3, :], spreads).then_inc(tables_loaded, 16)
            sp.dma_start(wo[:], w_out).then_inc(tables_loaded, 16)
            sp.wait_ge(loaded, 32)
            sp.wait_ge(tables_loaded, 48)

        @block.gpsimd
        def _(pool):
            pool.memset(hidden[:], 0.0).then_inc(consts, 1)
            pool.wait_ge(consts, 1)
            pool.affine_select(out=hidden[:], in_=hidden[:], compare_op=ALU.is_ge, fill=BIG, base=S - P,
                               pattern=[[-1, S]], channel_multiplier=1).then_inc(consts, 1)

            def rope_q(n, m):
                wait_alone(pool, dve_out, dve_count(n, 5 + 2 * m), pool_ticks)
                base = (n + 1) * 8 + 3 * m
                pool.tensor_tensor(turn1[:, m, :], turn1[:, m, :], turn2[:, m, :], ALU.add).then_inc(roped, 1)
                wait_alone(pool, roped, base + 1, pool_ticks)
                pool.tensor_scalar(qh[:, m, :], turn1[:, m, :], 1.0, 1.0, ALU.mult, ALU.mult).then_inc(roped, 1)
                wait_alone(pool, roped, base + 2, pool_ticks)
                pool.tensor_tensor(ql[:, m, :], turn1[:, m, :], qh[:, m, :].bitcast(F32), ALU.subtract)\
                    .then_inc(roped, 1)

            def rope_k(n):
                wait_alone(pool, dve_out, dve_count(n, 8), pool_ticks)
                base = (n + 1) * 8 + 6
                low = slice(0, P // 2)
                pool.tensor_tensor(turn1[low, 2, :], turn1[low, 2, :], turn2[low, 2, :], ALU.add).then_inc(roped, 1)
                wait_alone(pool, roped, base + 1, pool_ticks)
                pool.tensor_scalar(kk[low, :], turn1[low, 2, :], 1.0, 1.0, ALU.mult, ALU.mult).then_inc(roped, 1)

            def scale(Q, q):
                wait_alone(pool, recips, Q + 1, pool_ticks)
                N = (q % TT + 1) * P
                for h in range(REP):
                    slot = q % RING * REP + h
                    pool.tensor_scalar(p_sb[:, slot, 0:N], p_sb[:, slot, 0:N], recip[:, slot:slot + 1], 1.0,
                                       ALU.mult, ALU.mult).then_inc(scaled, 1)

            rope_q(-1, 0)
            rope_q(-1, 1)
            rope_k(-1)
            scale(0, 0)
            scale(1, 1)
            with pool.Fori(0, B // 2) as pair:
                for par in range(2):
                    b = pair * 2 + par
                    for q in range(QUADS):
                        scale(b * QUADS + (q + AHEAD - 1), q + AHEAD - 1)
                        if q == 3:
                            rope_q(b, 0)
                        if q == 4:
                            rope_q(b, 1)
                        if q == 5:
                            rope_k(b)

        @block.scalar
        def _(act):
            def exps(Q, q, heads=range(REP)):
                N = (q % TT + 1) * P
                for h in heads:
                    slot = q % RING * REP + h
                    act.wait_ge(masked, Q * REP + (h + 3))
                    act.activation(p_sb[:, slot, 0:N], p_sb[:, slot, 0:N], ACT.Exp, bias=nmax[:, slot:slot + 1],
                                   scale=-1.0, accum_out=total[:, slot:slot + 1]).then_inc(exped, 1)

            def turn_out(Q, q):
                act.wait_ge(turned, Q * REP + (ACT_TAKES[q % TT][0][1][1]))
                for bank, (lo, hi) in ACT_TAKES[q % TT]:
                    N = (q % TT + 1) * P
                    act.activation(pT[:, q % 2 * REP + lo:q % 2 * REP + hi, 0:N],
                                   t_ps[bank][:, 0:(hi - lo) * N].rearrange("p (h n) -> p h n", n=N), ACT.Copy)\
                        .then_inc(out_a, 1)

            def take_spread(n, nxt, j):
                act.wait_ge(made, made_count(n, j))
                to = q_all[nxt][:, j - 10, :] if j < 18 else k_all[nxt][:, j - 18, :]
                act.activation(to, m_ps[j % 2][:], ACT.Copy).then_inc(act_out, 1)

            def take_o(n, g):
                act.wait_ge(weighed, n * QUADS + (g * TT + TT))
                act.activation(oT[:, g, :], o_ps[g % 2][:], ACT.Copy).then_inc(o_out, 1)

            act.sem_inc(o_out, 2)
            act.sem_inc(out_a, 1)
            for j in range(10, JOBS):
                take_spread(-1, 0, j)
            exps(0, 0)
            exps(1, 1)
            exps(2, 2)
            with act.Fori(0, B // 2) as pair:
                for par in range(2):
                    b, nxt = pair * 2 + par, 1 - par
                    for q in range(QUADS):
                        Q = b * QUADS + q
                        early = 1 if q % TT == 1 else 2 if q % TT == 0 else 0
                        exps(b * QUADS + (q + AHEAD), q + AHEAD, range(early))
                        turn_out(Q, q)
                        exps(b * QUADS + (q + AHEAD), q + AHEAD, range(early, REP))
                        if 6 <= q < 12:
                            take_spread(b, nxt, 2 * q - 2)
                            take_spread(b, nxt, 2 * q - 1)
                        if q % TT == 0 and q > 0:
                            take_o(b, q // TT - 1)
                        if q == QUADS - 1:
                            take_o(b, KV1 - 1)

        @block.vector
        def _(dve):
            def make_xr(n):
                at = (n % B) * TT
                for i in range(TT):
                    dve.tensor_scalar(xr[:, i, :], y[:, ds(at + i, 1), :].rearrange("p a d -> p (a d)"),
                                      r1[:, ds(at + i, 1)], None, ALU.mult).then_inc(xr_made, 1)

            make_xr(0)
            for i in range(2):
                dve.memset(v[i][:], 0.0)
            dve.memset(oT[:], 0.0).then_inc(zeroed, 1)
            dve.sem_inc(masked, 2)
            dve.sem_inc(out_d, 1)
            dve.wait_ge(consts, 2)

            def take_x(n):
                for k in range(KT):
                    dve.wait_ge(made, made_count(n, 2 + k))
                    dve.tensor_scalar(xrT[:, k, :], m_ps[k][:], g1_sb[:, k:k + 1], None, ALU.mult).then_inc(dve_out, 1)

            def take_q(n, m):
                for c, to in enumerate((turn1, turn2)):
                    dve.wait_ge(made, made_count(n, 4 + 2 * m + c))
                    dve.tensor_tensor(to[:, m, :], m_ps[c][:], rope[:, c, :], ALU.mult).then_inc(dve_out, 1)

            def take_k(n):
                dve.wait_ge(made, made_count(n, 8))
                low, high = slice(0, P // 2), slice(P // 2, P)
                dve.tensor_tensor(turn1[low, 2, :], m_ps[0][low, :], rope[low, 2, :], ALU.mult)
                dve.tensor_tensor(turn2[low, 2, :], m_ps[0][high, :], rope[high, 2, :], ALU.mult).then_inc(dve_out, 1)

            def low_k(n):
                dve.wait_ge(roped, (n + 1) * 8 + 8)
                low, high = slice(0, P // 2), slice(P // 2, P)
                dve.tensor_tensor(kk[high, :], turn1[low, 2, :], kk[low, :].bitcast(F32), ALU.subtract)\
                    .then_inc(k_low, 1)

            def take_v(n, nxt):
                dve.wait_ge(made, made_count(n, 9))
                dve.tensor_copy(v[nxt][:, :, :, 0:QD], m_ps[1][:, 0:TT * KV1 * QD]
                                .rearrange("p (i g d) -> p i g d", g=KV1, d=QD)).then_inc(dve_out, 1)

            def take_out(count, rows):
                for half in range(2):
                    dve.wait_ge(made, count + half)
                    at = y[:, ds(rows + 2 * half, 2), :].rearrange("p i d -> p (i d)")
                    dve.tensor_tensor(at, m_ps[half][:], at, ALU.add).then_inc(dve_out, 1)

            def mask(Q, q, h):
                N = (q % TT + 1) * P
                slot = q % RING * REP + h
                bank, at = s_place(q, h)
                wait_alone(dve, scored, Q * REP + (h + 1), dve_ticks)
                dve.tensor_tensor_reduce(out=p_sb[:, slot, 0:N], in0=s_ps[bank][:, at:at + N], in1=hidden[:, S - N:S],
                                         scale=1.0, scalar=BIG, op0=ALU.add, op1=ALU.min,
                                         accum_out=nmax[:, slot:slot + 1]).then_inc(masked, 1)

            def invert(Q, q):
                dve.wait_ge(exped, Q * REP + REP)
                at = slice(q % RING * REP, q % RING * REP + REP)
                dve.reciprocal(recip[:, at], total[:, at]).then_inc(recips, 1)

            def turn_out(Q, q, n):
                bank, (lo, hi) = DVE_TAKES[q % TT][n]
                N = (q % TT + 1) * P
                dve.wait_ge(turned, Q * REP + hi)
                dve.tensor_copy(pT[:, q % 2 * REP + lo:q % 2 * REP + hi, 0:N],
                                t_ps[bank][:, 0:(hi - lo) * N].rearrange("p (h n) -> p h n", n=N)).then_inc(out_d, 1)

            dve.wait_ge(loaded, 32)
            take_x(-1)
            dve.wait_ge(tables_loaded, 48)
            dve.tensor_copy(spread[:].rearrange("p a b c -> p a (b c)"), p_sb[:, 0:3, :]).then_inc(zeroed, 1)
            take_q(-1, 0)
            take_q(-1, 1)
            take_k(-1)
            low_k(-1)
            take_v(-1, 0)
            for q in range(AHEAD):
                for h in range(REP):
                    mask(q, q, h)
            invert(0, 0)
            invert(1, 1)
            with dve.Fori(0, B // 2) as pair:
                for par in range(2):
                    b, nxt = pair * 2 + par, 1 - par
                    for q in range(QUADS):
                        Q = b * QUADS + q
                        shares = len(DVE_TAKES[q % TT])
                        for h in range(REP):
                            mask(b * QUADS + (q + AHEAD), q + AHEAD, h)
                            if h == 1:
                                invert(b * QUADS + (q + AHEAD - 1), q + AHEAD - 1)
                            if shares == 3 and h < 3:
                                turn_out(Q, q, h)
                            if shares == 1 and h == 2:
                                turn_out(Q, q, 0)
                        if q == 0:
                            make_xr(b + 1)
                        if q == 1:
                            take_out(made_count(b, 0), ((b + (B - 1)) % B) * TT)
                        if q == 2:
                            take_x(b)
                        if q == 3:
                            take_q(b, 0)
                        if q == 4:
                            take_q(b, 1)
                        if q == 5:
                            take_k(b)
                            take_v(b, nxt)
                        if q == 6:
                            low_k(b)
            take_out(made_count(B, 0), (B - 1) * TT)

        @block.tensor
        def _(pe):
            def bank_free(n, j):
                last = j - 2 if j >= 2 else JOBS - 2 + j
                before = n if j >= 2 else n + (-1)
                if last < 10:
                    pe.wait_ge(dve_out, dve_count(before, last))
                else:
                    pe.wait_ge(act_out, act_count(before, last))

            def turn_x(n, first=False):
                pe.wait_ge(xr_made, (n + 1) * TT + TT)
                for k in range(KT):
                    if not first:
                        bank_free(n, 2 + k)
                    for i in range(TT):
                        ins = pe.transpose(m_ps[k][:, P * i:P * i + P], xr[:, i, P * k:P * k + P], ident[:])
                    ins.then_inc(made, 1)

            def project(n, j, name):
                bank_free(n, j)
                for k in range(KT):
                    ins = pe.matmul(m_ps[j % 2][:], wp[:, k, PROJ[name]:PROJ[name] + P], xrT[:, k, :],
                                    start=(k == 0), stop=(k == KT - 1))
                ins.then_inc(made, 1)

            def project_q(n, m):
                if m == 0:
                    pe.wait_ge(dve_out, dve_count(n, 3))
                project(n, 4 + 2 * m, f"q{m}")
                project(n, 5 + 2 * m, f"s{m}")

            def project_kv(n):
                project(n, 8, "kk")
                bank_free(n, 9)
                W = KV1 * QD
                for i in range(TT):
                    for k in range(KT):
                        ins = pe.matmul(m_ps[1][:, i * W:i * W + W], xrT[:, k, i * P:i * P + P],
                                        wp[:, k, PROJ["v"]:PROJ["v"] + W], start=(k == 0), stop=(k == KT - 1))
                ins.then_inc(made, 1)

            def spread_parts(n, j):
                bank_free(n, j)
                bank = m_ps[j % 2]
                if j == 10:
                    pe.wait_ge(roped, (n + 1) * 8 + 6)
                if j == 18:
                    pe.wait_ge(k_low, n + 2)
                if j < 18:
                    m, pair_of = divmod(j - 10, 4)
                    pe.matmul(bank[:], spread[:, 0, pair_of, :], qh[:, m, :], start=True, stop=False)
                    pe.matmul(bank[:], spread[:, 1, pair_of, :], ql[:, m, :], start=False, stop=True).then_inc(made, 1)
                else:
                    pe.matmul(bank[:], spread[:, 2, j - 18, :], kk[:], start=True, stop=True).then_inc(made, 1)

            def score(Q, q, par, h):
                g, N = q // TT, (q % TT + 1) * P
                head = g * REP + h
                row = slice(64 * (head % 2), 64 * (head % 2) + 64)
                bank, at = s_place(q, h)
                if h == 0:
                    pe.wait_ge(masked, Q * REP + 2)
                elif h >= 2:
                    pe.wait_ge(masked, Q * REP + (h + 1))
                pe.matmul(s_ps[bank][:, at:at + N], q_all[par][row, head // 2, N - P:N], k_all[par][row, g, 0:N],
                          start=True, stop=True).then_inc(scored, 1)

            def turn(b, Q, q, h):
                if h == 0:
                    pe.wait_ge(out_a, Q + 1)
                    pe.wait_ge(out_d, taken(b, q))
                if h == 2 and q % TT >= 2:
                    pe.wait_ge(out_a, Q + 2)
                if h == 3 and q % TT >= 2:
                    pe.wait_ge(out_d, taken(b, q, 1))
                pe.wait_ge(scaled, Q * REP + (h + 1))
                bank, at = t_place(q, h)
                slot = q % RING * REP + h
                for k in range(q % TT + 1):
                    ins = pe.transpose(t_ps[bank][:, at + k * P:at + k * P + P], p_sb[:, slot, k * P:k * P + P], ident[:])
                ins.then_inc(turned, 1)

            def weigh(b, Q, q, par):
                g, i = divmod(q, TT)
                if i == 0:
                    pe.wait_ge(o_out, b * KV1 + (g + 1))
                pe.wait_ge(out_a, Q + 2)
                pe.wait_ge(out_d, taken(b, q + 1))
                for k in range(i + 1):
                    for h in range(REP):
                        ins = pe.matmul(o_ps[g % 2][VP * h:VP * h + VP, i * P:i * P + P], v[par][:, k, g, :],
                                        pT[:, q % 2 * REP + h, k * P:k * P + P], start=(k == 0), stop=(k == i))
                ins.then_inc(weighed, 1)

            def project_out(n):
                for half in range(2):
                    bank_free(n, half)
                    for i in range(2):
                        for g in range(KV1):
                            at = (2 * half + i) * P
                            ins = pe.matmul(m_ps[half][:, i * D:i * D + D], oT[:, g, at:at + P], wo[:, g, :],
                                            start=(g == 0), stop=(g == KV1 - 1))
                    ins.then_inc(made, 1)

            turn_x(-1, first=True)
            pe.wait_ge(loaded, 32)
            project_q(-1, 0)
            project_q(-1, 1)
            project_kv(-1)
            pe.wait_ge(zeroed, 2)
            for j in range(10, JOBS):
                spread_parts(-1, j)
            pe.wait_ge(act_out, BY_ACT)
            for q in range(AHEAD):
                for h in range(REP):
                    score(q, q, 0, h)
            with pe.Fori(0, B // 2) as pair:
                for par in range(2):
                    b, nxt = pair * 2 + par, 1 - par
                    for q in range(QUADS):
                        Q = b * QUADS + q
                        ahead = q + AHEAD
                        if ahead == QUADS:
                            pe.wait_ge(act_out, act_count(b, JOBS - 1))
                        for h in range(REP):
                            turn(b, Q, q, h)
                            score(b * QUADS + ahead, ahead % QUADS, nxt if ahead >= QUADS else par, h)
                        if q > 0:
                            weigh(b, b * QUADS + (q - 1), q - 1, par)
                        if q == 1:
                            pe.wait_ge(o_out, b * KV1 + 2)
                            project_out(b)
                        if q == 2:
                            turn_x(b)
                        if q == 3:
                            project_q(b, 0)
                        if q == 4:
                            project_q(b, 1)
                        if q == 5:
                            project_kv(b)
                        if 6 <= q < 12:
                            spread_parts(b, 2 * q - 2)
                            spread_parts(b, 2 * q - 1)
                        if q == QUADS - 1:
                            weigh(b, Q, q, par)
            pe.wait_ge(o_out, B * KV1 + 2)
            project_out(B)


E1 = 4
H1 = 3 * D
M1 = H1 // P
RING1 = 3


def load_experts(sp, w1, w3, w2, e, w13_raw, w2_raw, w_loaded):
    for c, w in ((0, w1), (1, w3)):
        for k in range(KT):
            sp.dma_start(w13_raw[:, k, c, :], w[ds(e, 1), k * P:k * P + P, :].rearrange("e p h -> p (e h)"))\
                .then_inc(w_loaded, 16)
    sp.dma_start(w2_raw[:], w2[ds(e, 1)].rearrange("e (m p) d -> p (e m) d", p=P)).then_inc(w_loaded, 16)


def routing_phase(nc, g2, gate, ident, y, yh, yl, comb, w1, w3, w2, w13_raw, w2_raw, w_loaded):
    with ExitStack() as ctx:
        sb, ps, sem = hold(ctx, nc)
        squares = sb("rt_squares", [P, TT, D])
        sq_sum = sb("rt_sq_sum", [P, TT])
        rms = sb("rt_rms", [P, TT])
        r2 = sb("rt_r2", [P, 2, TT])
        eps = sb("rt_eps", [P, 1])
        yr = [sb(f"rt_yr{i}", [P, TT, D]) for i in range(2)]
        yg = [sb(f"rt_yg{i}", [P, KT, S]) for i in range(2)]
        g2_sb = sb("rt_g2", [P, KT])
        gate_sb = sb("rt_gate", [P, KT, E1])
        prob = sb("rt_prob", [P, E1, B * TT])
        rank = sb("rt_rank", [P, E1, B * TT])
        beats = sb("rt_beats", [P, E1 - 1, B * TT])
        top = sb("rt_top", [P, B * TT])
        y_ps = [[ps(f"rt_y_ps{i}{k}") for k in range(KT)] for i in range(2)]
        l_ps = [ps(f"rt_l_ps{i}") for i in range(2)]

        loaded = sem("rt_loaded")
        squared = sem("rt_squared")
        rooted = sem("rt_rooted")
        inverted = sem("rt_inverted")
        normed = sem("rt_normed")
        turned = sem("rt_turned")
        gained = sem("rt_gained")
        high = sem("rt_high")
        low = sem("rt_low")
        voted = sem("rt_voted")
        vote_out = sem("rt_vote_out")
        chain = sem("rt_chain")
        exped = sem("rt_exped")
        dve_ticks = sem("rt_dve_ticks")
        block = ctx.enter_context(nc.Block())

        @block.sync
        def _(sp):
            sp.dma_start(g2_sb[:], g2).then_inc(loaded, 16)
            sp.dma_start(gate_sb[:], gate.rearrange("(k p) e -> p k e", p=P)).then_inc(loaded, 16)
            load_experts(sp, w1, w3, w2, 0, w13_raw, w2_raw, w_loaded)
            sp.wait_ge(loaded, 32)

        @block.scalar
        def _(act):
            def root(n):
                for i in range(TT):
                    act.activation(squares[:, i, :], y[:, ds((n % B) * TT + i, 1), :].rearrange("p a d -> p (a d)"),
                                   ACT.Square, accum_out=sq_sum[:, i:i + 1]).then_inc(squared, 1)
                act.wait_ge(squared, n * TT + TT)
                act.activation(rms[:], sq_sum[:], ACT.Sqrt, scale=1.0 / D, bias=eps[:, 0:1]).then_inc(rooted, 1)

            act.wait_ge(chain, 1)
            act.wait_ge(loaded, 32)
            root(0)
            with act.Fori(0, B // 2) as pair:
                for par in range(2):
                    b = pair * 2 + par
                    act.wait_ge(inverted, b + 1)
                    root(b + 1)
                    act.wait_ge(gained, b * KT + KT)
                    act.activation(yh[:, :, ds(b * S, S)], yg[par][:], ACT.Copy).then_inc(high, 1)
            act.wait_ge(chain, 3)
            act.activation(prob[:], prob[:], ACT.Exp).then_inc(exped, 1)

        @block.vector
        def _(dve):
            dve.memset(eps[:], EPS_RMS).then_inc(chain, 1)
            dve.wait_ge(loaded, 32)

            def norm(n, par):
                dve.wait_ge(rooted, n + 1)
                dve.reciprocal(r2[:, par, :], rms[:]).then_inc(inverted, 1)
                wait_alone(dve, inverted, n + 1, dve_ticks)
                for i in range(TT):
                    dve.tensor_scalar(yr[par][:, i, :], y[:, ds((n % B) * TT + i, 1), :].rearrange("p a d -> p (a d)"),
                                      r2[:, par, i:i + 1], None, ALU.mult).then_inc(normed, 1)

            norm(0, 0)
            with dve.Fori(0, B // 2) as pair:
                for par in range(2):
                    b = pair * 2 + par
                    norm(b + 1, 1 - par)
                    dve.wait_ge(turned, b + 1)
                    for k in range(KT):
                        dve.tensor_scalar(yg[par][:, k, :], y_ps[par][k][:], g2_sb[:, k:k + 1], None, ALU.mult)\
                            .then_inc(gained, 1)
                    dve.wait_ge(high, b + 1)
                    at = ds(b * S, S)
                    dve.tensor_tensor(yl[:, :, at], yg[par][:], yh[:, :, at].bitcast(F32), ALU.subtract).then_inc(low, 1)
                    dve.wait_ge(voted, b + 1)
                    dve.tensor_copy(prob[:, :, ds(b * TT, TT)].rearrange("p e i -> p i e"),
                                    l_ps[par][:, 0:TT * E1].rearrange("p (i e) -> p i e", e=E1)).then_inc(vote_out, 1)

            count = [1]

            def link(ins):
                count[0] += 1
                ins.then_inc(chain, 1)
                dve.wait_ge(chain, count[0])

            def over_experts(tile):
                return tile[:].rearrange("p e t -> p t e")

            def each_expert(tile):
                return tile[:].rearrange("p (a t) -> p a t", a=1).broadcast_to([P, E1, B * TT])

            dve.wait_ge(vote_out, B)
            link(dve.tensor_reduce(top[:], over_experts(prob), AX.X, ALU.max))
            link(dve.tensor_tensor(prob[:], prob[:], each_expert(top), ALU.subtract))
            dve.wait_ge(exped, 1)
            link(dve.tensor_reduce(top[:], over_experts(prob), AX.X, ALU.add))
            link(dve.reciprocal(top[:], top[:]))
            link(dve.tensor_tensor(prob[:], prob[:], each_expert(top), ALU.mult))
            link(dve.memset(rank[:], 0.0))
            for d in range(1, E1):
                n = E1 - d
                link(dve.tensor_tensor(beats[:, 0:n, :], prob[:, 0:n, :], prob[:, d:E1, :], ALU.is_ge))
                link(dve.tensor_tensor(rank[:, d:E1, :], rank[:, d:E1, :], beats[:, 0:n, :], ALU.add))
                link(dve.tensor_scalar(beats[:, 0:n, :], beats[:, 0:n, :], -1.0, 1.0, ALU.mult, ALU.add))
                link(dve.tensor_tensor(rank[:, 0:n, :], rank[:, 0:n, :], beats[:, 0:n, :], ALU.add))
            link(dve.tensor_scalar(rank[:], rank[:], 1.5, None, ALU.is_lt))
            link(dve.tensor_tensor(prob[:], prob[:], rank[:], ALU.mult))
            link(dve.tensor_reduce(top[:], over_experts(prob), AX.X, ALU.add))
            link(dve.reciprocal(top[:], top[:]))
            link(dve.tensor_tensor(comb[:], prob[:], each_expert(top), ALU.mult))

        @block.tensor
        def _(pe):
            def turn(n, par):
                pe.wait_ge(normed, n * TT + TT)
                for k in range(KT):
                    for i in range(TT):
                        ins = pe.transpose(y_ps[par][k][:, P * i:P * i + P], yr[par][:, i, P * k:P * k + P], ident[:])
                ins.then_inc(turned, 1)

            turn(0, 0)
            with pe.Fori(0, B // 2) as pair:
                for par in range(2):
                    b = pair * 2 + par
                    turn(b + 1, 1 - par)
                    pe.wait_ge(gained, b * KT + KT)
                    for i in range(TT):
                        for k in range(KT):
                            ins = pe.matmul(l_ps[par][:, i * E1:i * E1 + E1], yg[par][:, k, i * P:i * P + P],
                                            gate_sb[:, k, :], start=(k == 0), stop=(k == KT - 1))
                    ins.then_inc(voted, 1)


def expert_phase(nc, w1, w3, w2, w13_raw, w2_raw, w_loaded, y, yh, yl, comb, x1_dram, s_dram, out_dram):
    with ExitStack() as ctx:
        sb, ps, sem = hold(ctx, nc)
        w13h, w13l = (sb(f"ex_w13{x}", [P, KT, 2, H1], F32R) for x in "hl")
        w2h, w2l = (sb(f"ex_w2{x}", [P, M1, D], F32R) for x in "hl")
        act1 = sb("ex_act1", [P, 2, S])
        hid = sb("ex_hid", [P, RING1, S])
        hh, hl = (sb(f"ex_h{x}", [P, RING1, S], F32R) for x in "hl")
        s_in = [sb(f"ex_s{i}", [P, TT, D]) for i in range(2)]
        x_in = [sb(f"ex_x{i}", [P, TT, D]) for i in range(2)]
        z = sb("ex_z", [P, TT, D])
        a_ps = [ps(f"ex_a_ps{i}") for i in range(2)]
        b_ps = [ps(f"ex_b_ps{i}") for i in range(2)]
        o_ps = [[ps(f"ex_o_ps{i}{k}") for k in range(2)] for i in range(2)]

        f_loaded = [sem("ex_f_loaded0"), sem("ex_f_loaded1")]
        stored = sem("ex_stored")
        ready = sem("ex_ready")
        unit_done = sem("ex_unit_done")
        silued = sem("ex_silued")
        gated = sem("ex_gated")
        h_high = sem("ex_h_high")
        h_low = sem("ex_h_low")
        w_high = sem("ex_w_high")
        w_low = sem("ex_w_low")
        added = sem("ex_added")
        f_silued = sem("ex_f_silued")
        f_mixed = sem("ex_f_mixed")
        f_added = sem("ex_f_added")
        pool_ticks = sem("ex_pool_ticks")
        dve_ticks = sem("ex_dve_ticks")
        x_view = x1_dram.rearrange("b (i p) d -> b p i d", p=P)
        s_view = s_dram.rearrange("b (i p) d -> b p i d", p=P)
        out_view = out_dram.rearrange("b (i p) d -> b p i d", p=P)
        block = ctx.enter_context(nc.Block())
        LAST = E1 - 1

        def pieces(m):
            c = slice(m * P, m * P + P)
            return ((w13_raw[:, :, :, c], w13h[:, :, :, c], w13l[:, :, :, c]),
                    (w2_raw[:, m, :], w2h[:, m, :], w2l[:, m, :]))

        @block.sync
        def _(sp):
            def load_final(b, par):
                sp.dma_start(s_in[par][:], s_view[b]).then_inc(f_loaded[par], 16)
                sp.dma_start(x_in[par][:], x_view[b]).then_inc(f_loaded[par], 16)

            with sp.Fori(0, E1) as e:
                sp.wait_ge(w_low, e * M1 + M1)
                load_experts(sp, w1, w3, w2, (e + 1) % E1, w13_raw, w2_raw, w_loaded)
            load_final(0, 0)
            load_final(1, 1)
            for b in range(B):
                sp.wait_ge(f_added, b + 1)
                sp.dma_start(out_view[b], x_in[b % 2][:]).then_inc(stored, 16)
                sp.wait_ge(stored, b * 16 + 16)
                if b + 2 < B:
                    load_final(b + 2, b % 2)
            sp.wait_ge(w_loaded, (2 * KT + 1) * 16 * (E1 + 1))
            sp.wait_ge(stored, 16 * B)

        @block.gpsimd
        def _(pool):
            def split_high(m):
                for raw, high, _ in pieces(m):
                    ins = pool.tensor_scalar(high, raw, 1.0, 1.0, ALU.mult, ALU.mult)
                ins.then_inc(w_high, 1)

            def unit(U, m):
                pool.wait_ge(gated, U + 3)
                wait_alone(pool, unit_done, U + 1, pool_ticks)
                pool.tensor_scalar(hh[:, m % RING1, :], hid[:, m % RING1, :], 1.0, 1.0, ALU.mult, ALU.mult)\
                    .then_inc(h_high, 1)

            pool.wait_ge(w_loaded, (2 * KT + 1) * 16)
            for m in range(M1):
                split_high(m)
            with pool.Fori(0, E1) as e:
                with pool.Fori(0, B - 1) as b:
                    for m in range(M1):
                        unit(e * (B * M1) + b * M1 + m, m)
                for m in range(M1):
                    U = e * (B * M1) + ((B - 1) * M1 + m)
                    unit(U, m)
                    if m == 0:
                        wait_alone(pool, w_loaded, e * ((2 * KT + 1) * 16) + (2 * KT + 1) * 32, pool_ticks)
                    wait_alone(pool, unit_done, U + (RING1 + 1), pool_ticks)
                    split_high(m)

        @block.scalar
        def _(act):
            def unit(U, m):
                act.wait_ge(ready, U + 1)
                act.activation(act1[:, m % 2, :], a_ps[m % 2][:], ACT.Silu).then_inc(silued, 1)

            def final(b):
                act.wait_ge(added, (LAST * B + b + 3) * TT)
                if b > 0:
                    act.wait_ge(f_added, b)
                act.activation(z[:], y[:, b * TT:b * TT + TT, :], ACT.Silu).then_inc(f_silued, 1)

            with act.Fori(0, LAST * B) as eb:
                for m in range(M1):
                    unit(eb * M1 + m, m)
            for b in range(B):
                for m in range(M1):
                    unit((LAST * B + b) * M1 + m, m)
                    if m == 3 and b > 0:
                        final(b - 1)
            final(B - 1)

        @block.vector
        def _(dve):
            dve.sem_inc(gated, 2)
            dve.sem_inc(added, 2 * TT)

            def split_low(count, m):
                dve.wait_ge(w_high, count)
                for raw, high, low in pieces(m):
                    ins = dve.tensor_tensor(low, raw, high.bitcast(F32), ALU.subtract)
                ins.then_inc(w_low, 1)

            def product(U, m):
                dve.wait_ge(silued, U + 1)
                dve.tensor_tensor(hid[:, m % RING1, :], act1[:, m % 2, :], b_ps[m % 2][:], ALU.mult).then_inc(gated, 1)

            def rest(U, m):
                dve.wait_ge(h_high, U + 1)
                dve.tensor_tensor(hl[:, m % RING1, :], hid[:, m % RING1, :], hh[:, m % RING1, :].bitcast(F32),
                                  ALU.subtract).then_inc(h_low, 1)

            def take(U_end, e, b, par):
                dve.wait_ge(unit_done, U_end + RING1)
                for i in range(TT):
                    at = y[:, ds(b * TT + i, 1), :].rearrange("p a d -> p (a d)")
                    dve.scalar_tensor_tensor(out=at, in0=o_ps[par][i // 2][:, i % 2 * D:i % 2 * D + D],
                                             scalar=comb[:, ds(e, 1), ds(b * TT + i, 1)].rearrange("p a c -> p (a c)"),
                                             in1=at, op0=ALU.mult, op1=ALU.add).then_inc(added, 1)

            def final(b):
                dve.wait_ge(f_silued, b + 1)
                dve.wait_ge(f_loaded[b % 2], (b // 2 + 1) * 32)
                dve.tensor_tensor(z[:], z[:], s_in[b % 2][:], ALU.mult).then_inc(f_mixed, 1)
                dve.wait_ge(f_mixed, b + 1)
                dve.tensor_tensor(x_in[b % 2][:], x_in[b % 2][:], z[:], ALU.add).then_inc(f_added, 1)

            def batch(e, b, par, split=False, finals=None):
                U = e * (B * M1) + b * M1
                for m in range(M1):
                    product(U + m, m)
                    if m > 0:
                        rest(U + (m - 1), m - 1)
                    if split and m > 1:
                        split_low(e * M1 + (M1 + m - 1), m - 2)
                    if finals is not None and finals > 0 and m == 4:
                        final(finals - 1)
                rest(U + (M1 - 1), M1 - 1)
                take(U + M1, e, b, par)
                if split:
                    for m in (M1 - 2, M1 - 1):
                        split_low(e * M1 + (M1 + m + 1), m)

            for m in range(M1):
                split_low(m + 1, m)
            with dve.Fori(0, LAST) as e:
                with dve.Fori(0, B // 2 - 1) as pair:
                    for par in range(2):
                        batch(e, pair * 2 + par, par)
                batch(e, B - 2, 0)
                batch(e, B - 1, 1, split=True)
            for b in range(B):
                batch(LAST, b, b % 2, finals=b, split=(b == B - 1))
            final(B - 1)

        @block.tensor
        def _(pe):
            pe.sem_inc(unit_done, RING1)

            def hidden_sums(U, e, b, m):
                pe.wait_ge(w_low, e * M1 + (m + 1))
                pe.wait_ge(gated, U + 1)
                for c, bank in ((0, a_ps[m % 2]), (1, b_ps[m % 2])):
                    for i, (w, x) in enumerate([(w13h, yh), (w13l, yh), (w13h, yl)]):
                        for k in range(KT):
                            ins = pe.matmul(bank[:], w[:, k, c, m * P:m * P + P], x[:, k, ds(b * S, S)],
                                            start=(i == 0 and k == 0), stop=(i == 2 and k == KT - 1))
                ins.then_inc(ready, 1)

            def output_sums(U, m, par):
                pe.wait_ge(h_low, U + 1)
                for t in range(TT):
                    bank = o_ps[par][t // 2][:, t % 2 * D:t % 2 * D + D]
                    for i, (h, w) in enumerate([(hh, w2h), (hl, w2h), (hh, w2l)]):
                        ins = pe.matmul(bank, h[:, m % RING1, t * P:t * P + P], w[:, m, :],
                                        start=(m == 0 and i == 0 and t % 2 == 0),
                                        stop=(m == M1 - 1 and i == 2 and t % 2 == 1))
                ins.then_inc(unit_done, 1)

            def batch(e, b, par, e_next, b_next):
                U = e * (B * M1) + b * M1
                for m in range(M1):
                    if m + 2 < M1:
                        hidden_sums(U + (m + 2), e, b, m + 2)
                    else:
                        hidden_sums(U + (m + 2), e_next, b_next, m + 2 - M1)
                    if m == 0:
                        pe.wait_ge(added, e * (B * TT) + (b * TT + TT))
                    output_sums(U + m, m, par)

            hidden_sums(0, 0, 0, 0)
            hidden_sums(1, 0, 0, 1)
            with pe.Fori(0, E1) as e:
                with pe.Fori(0, B // 2 - 1) as pair:
                    for par in range(2):
                        batch(e, pair * 2 + par, par, e, pair * 2 + (par + 1))
                batch(e, B - 2, 0, e, B - 1)
                batch(e, B - 1, 1, e + 1, 0)


def recurrent_kernel(nc, x, w_heads, wo_heads, slopes, w_gate, b_gate, alpha, w1_all, w2_all, b1_all, b2_all, w_write,
                     w_read, decay, log_alpha, w_proj, w_out, g1, ropes, spreads, g2, gate1, w1, w3, w2, out):
    xh_dram = nc.dram_tensor("xh_dram", [P, KT, T], F32).ap()
    xl_dram = nc.dram_tensor("xl_dram", [P, KT, T], F32).ap()
    rows_dram = nc.dram_tensor("rows_dram", [B, NF], U32).ap()
    coef_dram = nc.dram_tensor("coef_dram", [B, NF], F32).ap()
    x1_dram = nc.dram_tensor("x1_dram", [B, S, D], F32).ap()
    s_dram = nc.dram_tensor("s_dram", [B, S, D], F32).ap()
    with ExitStack() as whole:
        sb, _, _ = hold(whole, nc)
        ident = sb("ident", [P, P])
        with ExitStack() as layer0:
            sb, _, _ = hold(layer0, nc)
            xsum = sb("xsum", [P, KT, B])
            rows = sb("rows", [1, B * NF], U32)
            coef = sb("coef", [P, B * NF])
            acc = sb("acc", [P, KT, T])
            with ExitStack() as mixer:
                sb, _, _ = hold(mixer, nc)
                xh = sb("xh", [P, KT, T], F32R)
                xl = sb("xl", [P, KT, T], F32R)
                layernorm_phase(nc, x, ident, xh, xl, xsum, xh_dram, xl_dram)
                gate_phase(nc, xsum, w_gate, b_gate, alpha, rows_dram, coef_dram, rows, coef, acc)
                head_attention_phase(nc, w_heads, wo_heads, slopes, ident, xh, xl, acc)
            network_phase(nc, x, w1_all, w2_all, b1_all, b2_all, ident, rows, coef, xh_dram, xl_dram, acc, x1_dram)
        with ExitStack() as layer1:
            sb, _, _ = hold(layer1, nc)
            y = sb("y", [P, B * TT, D])
            r1 = sb("r1", [P, B * TT])
            comb = sb("comb", [P, E1, B * TT])
            recurrence_phase(nc, x1_dram, w_write, w_read, decay, log_alpha, ident, y, r1, s_dram)
            attention_phase(nc, w_proj, w_out, g1, ropes, spreads, ident, y, r1)
            yh = sb("yh", [P, KT, T], F32R)
            yl = sb("yl", [P, KT, T], F32R)
            w13_raw = sb("w13_raw", [P, KT, 2, H1])
            w2_raw = sb("w2_raw", [P, M1, D])
            w_loaded = layer1.enter_context(nc.semaphore("experts_loaded"))
            routing_phase(nc, g2, gate1, ident, y, yh, yl, comb, w1, w3, w2, w13_raw, w2_raw, w_loaded)
            expert_phase(nc, w1, w3, w2, w13_raw, w2_raw, w_loaded, y, yh, yl, comb, x1_dram, s_dram, out)


def lay_out(inputs):
    a = {name: np.ascontiguousarray(value) for name, value in inputs.items()}

    def join(parts, axis=0):
        return np.ascontiguousarray(np.concatenate(parts, axis))

    def by_partition(vector):
        return np.ascontiguousarray(np.moveaxis(vector.reshape(*vector.shape[:-1], -1, P), -2, -1))

    def halves_exchanged(w):
        return w.reshape(D, -1, 2, QD // 2)[:, :, ::-1].reshape(D, -1)

    w_qkv, n_q, n_kv = a["L0_attn_W_qkv"], 2 * KVH * HD, KVH * HD
    heads = [w_qkv[:, lo:hi].reshape(KT, P, KVH, -1) for lo, hi in
             ((0, n_q), (n_q, n_q + n_kv), (n_q + n_kv, n_q + 2 * n_kv))]
    slopes = (2.0 ** (-2.0 ** (-(np.log2(2 * KVH) - 3)))) ** np.arange(1, 2 * KVH + 1, dtype=np.float32)
    wq, wk, wv = a["L1_ffn_wq"], a["L1_ffn_wk"], a["L1_ffn_wv"]
    wo = np.zeros((REP, VP, KV1, D), np.float32)
    wo[:, :QD] = a["L1_ffn_wo"].reshape(KV1, REP, QD, D).transpose(1, 2, 0, 3)
    return {
        "x": a["L0_attn_inputs"],
        "w_heads": np.ascontiguousarray(join(heads, 3).transpose(2, 1, 0, 3)),
        "wo_heads": a["L0_attn_W_out"].reshape(KVH, P, D),
        "slopes": np.tile(slopes.astype(np.float32), (P, 1)),
        "w_gate": a["L0_ffn_w_gate"],
        "b_gate": a["L0_ffn_b_gate"],
        "alpha": a["L0_ffn_alpha"].reshape(1, 1),
        "w1_all": join([a["L0_ffn_W1m"][None], a["L0_ffn_W1e"]]),
        "w2_all": join([a["L0_ffn_W2m"][None], a["L0_ffn_W2e"]]),
        "b1_all": by_partition(join([a["L0_ffn_b1m"][None], a["L0_ffn_b1e"]])),
        "b2_all": by_partition(join([a["L0_ffn_b2m"][None], a["L0_ffn_b2e"]])),
        "w_write": np.ascontiguousarray(a["L1_attn_W_write"].T),
        "w_read": np.ascontiguousarray(a["L1_attn_W_read"].T),
        "decay": a["L1_attn_decay"],
        "log_alpha": a["L1_attn_log_alpha"],
        "w_proj": join([wq, halves_exchanged(wq), wk, halves_exchanged(wk), wv], 1),
        "w_out": wo.reshape(P, KV1, D),
        "g1": by_partition(a["L1_ffn_g1"]),
        "ropes": rope_tables(),
        "spreads": spread_tables(),
        "g2": by_partition(a["L1_ffn_g2"]),
        "gate1": a["L1_ffn_gate"],
        "w1": a["L1_ffn_w1"],
        "w3": a["L1_ffn_w3"],
        "w2": a["L1_ffn_w2"],
    }


def kernel(**inputs):
    import concourse.bacc as _bacc
    from concourse.bass_utils import run_bass_kernel_spmd as _run

    nc = _bacc.Bacc("TRN2", target_bir_lowering=False, num_devices=1)
    arrays, args = {}, []
    for name, a in lay_out(inputs).items():
        arrays[f"in_{name}_dram"] = a
        args.append(nc.dram_tensor(f"in_{name}_dram", a.shape, mybir.dt.from_np(a.dtype), kind="ExternalInput").ap())
    args.append(nc.dram_tensor("out_0_dram", (B, S, D), F32, kind="ExternalOutput").ap())
    recurrent_kernel(nc, *args)
    r = _run(nc, [arrays], core_ids=[0])
    return r.results[0]["out_0_dram"]
```
